# Optimizing a Trainium2 kernel written in Bass

```python
import numpy as np
import jax
import jax.numpy as jnp

def _softmax(x, axis=-1):
    return jax.nn.softmax(x, axis=axis)

def _gelu(x):
    return jax.nn.gelu(x, approximate=True)

def _silu(x):
    return jax.nn.silu(x)

def _sigmoid(x):
    return jax.nn.sigmoid(x)

def _layernorm(x, axis=-1, eps=1e-05):
    m = jnp.mean(x, axis=axis, keepdims=True)
    v = jnp.var(x, axis=axis, keepdims=True)
    return (x - m) / jnp.sqrt(v + eps)

def _scatter_add(tgt, idx, src, axis=0):
    return tgt.at[idx].add(src)

def _segment_sum(src, seg, n):
    return jax.ops.segment_sum(src, seg, n)
kernel_name = 'mk_gnn_resnorm_d4_gnn_r8_13d2c7'

def setup_inputs(seed: int=0):
    np.random.seed(seed)
    _w = jnp.asarray

    def _rec_inputs():
        import jax
        import jax.numpy as jnp
        _gk = jax.random.key(seed)
        x = -0.0007083 + 1.001 * jax.random.normal(jax.random.fold_in(_gk, 1), (6250, 48), jnp.float32)
        _s = jax.random.randint(jax.random.fold_in(_gk, 2), (100000,), 0, 6250, jnp.int32)
        _d = jax.random.randint(jax.random.fold_in(_gk, 3), (100000,), 0, 6250, jnp.int32)
        _loop = jnp.arange(6250, dtype=jnp.int32)
        src = jnp.concatenate([_s, _d, _loop])
        dst = jnp.concatenate([_d, _s, _loop])
        _o = jnp.argsort(dst, stable=True)
        src = src[_o]
        dst = dst[_o]
        edge_attr_40 = jax.random.uniform(jax.random.fold_in(_gk, 13), (206250, 40), jnp.float32, 0.0, 1)
        edge_type_8 = jax.random.randint(jax.random.fold_in(_gk, 15), (206250,), 0, 8, jnp.int32)
        edge_weight = jax.random.uniform(jax.random.fold_in(_gk, 16), (206250,), jnp.float32, 0.0, 6.99999)
        edge_weight1 = jax.random.uniform(jax.random.fold_in(_gk, 17), (206250, 1), jnp.float32, 0.0, 1)
        node_type_119 = jax.random.randint(jax.random.fold_in(_gk, 18), (6250,), 0, 119, jnp.int32)
        node_vec = jax.random.uniform(jax.random.fold_in(_gk, 19), (6250,), jnp.float32, 0.0, 1.49999)
        return (x, src, dst, edge_attr_40, edge_type_8, edge_weight, edge_weight1, node_type_119, node_vec)
    x, src, dst, edge_attr_40, edge_type_8, edge_weight, edge_weight1, node_type_119, node_vec = _rec_inputs()

    def _L0_gnn_setup():
        import jax, jax.numpy as jnp
        import numpy as np
        N = 6250
        E = 200000
        C_IN = 48
        C_OUT = 48
        K = 16
        LAMBDA_MAX = 2.0
        key = jax.random.key(seed)
        k0, k1, k2, k3 = jax.random.split(key, 4)
        node_emb = jax.random.normal(k0, (N, C_IN), dtype=jnp.float32)
        edge_index = jax.random.randint(k1, (2, E), 0, N, dtype=jnp.int32)
        weights = jax.random.normal(k2, (K, C_IN, C_OUT), dtype=jnp.float32) * 0.05
        bias = jax.random.normal(k3, (C_OUT,), dtype=jnp.float32) * 0.05
        return {'node_emb': node_emb, 'edge_index': edge_index, 'weights': weights, 'bias': bias}
    _L0_gnn_all = _L0_gnn_setup()
    _L0_gnn_in = {k: v for k, v in _L0_gnn_all.items() if k in ('weights', 'bias')}
    del _L0_gnn_all

    def _L1_gnn_setup():
        import jax, jax.numpy as jnp
        import numpy as np
        CUTOFF = 6.0
        LN_EPS = 1e-05
        key = jax.random.key(seed)
        ks = jax.random.split(key, 16)
        N, E, H, R, NEL, G = (6250, 100000, 48, 40, 119, 32)
        inp = {'h': jax.random.normal(ks[0], (N, H), jnp.float32), 'edge_index': jax.random.randint(ks[1], (2, E), 0, N, jnp.int64), 'edge_attr': jax.random.uniform(ks[2], (E, R), jnp.float32), 'distances': jax.random.uniform(ks[3], (E,), jnp.float32) * 7.0, 'atom_z': jax.random.randint(ks[4], (N,), 0, NEL, jnp.int64), 'node_mult': jax.random.uniform(ks[5], (N,), jnp.float32) + 0.5, 'batch': jnp.zeros((N,), jnp.int64), 'W1': jax.random.normal(ks[6], (H, R), jnp.float32) / np.sqrt(R), 'b1': jax.random.normal(ks[7], (H,), jnp.float32) * 0.01, 'W2': jax.random.normal(ks[8], (H, H), jnp.float32) / np.sqrt(H), 'b2': jax.random.normal(ks[9], (H,), jnp.float32) * 0.01, 'emb': jax.random.normal(ks[10], (NEL, G), jnp.float32) * 0.01, 'adaptW': jax.random.normal(ks[11], (G, G), jnp.float32) * 0.01, 'gamma': jnp.ones((H,), jnp.float32), 'beta': jnp.zeros((H,), jnp.float32)}
        return inp
    _L1_gnn_all = _L1_gnn_setup()
    _L1_gnn_in = {k: v for k, v in _L1_gnn_all.items() if k in ('W1', 'b1', 'W2', 'b2', 'emb', 'adaptW', 'gamma', 'beta')}
    del _L1_gnn_all

    def _L2_gnn_setup():
        import jax, jax.numpy as jnp
        import numpy as np
        N_NODES = 6250
        N_EDGES = 200000
        IN_FEAT = 48
        OUT_FEAT = 48
        NUM_RELS = 8
        key = jax.random.key(seed)
        ks = jax.random.split(key, 9)
        s1 = float(np.sqrt(2.0) * np.sqrt(6.0 / (IN_FEAT + IN_FEAT)))
        s2 = float(np.sqrt(2.0) * np.sqrt(6.0 / (IN_FEAT + OUT_FEAT)))
        return {'inputs': jax.random.normal(ks[0], (N_NODES, IN_FEAT), dtype=jnp.float32), 'norm': jax.random.uniform(ks[1], (N_EDGES, 1), dtype=jnp.float32), 'weight1': jax.random.uniform(ks[2], (NUM_RELS, IN_FEAT, IN_FEAT), jnp.float32, -s1, s1), 'weight2': jax.random.uniform(ks[3], (NUM_RELS, IN_FEAT, OUT_FEAT), jnp.float32, -s2, s2), 'bias1': jax.random.normal(ks[4], (IN_FEAT,), dtype=jnp.float32) * 0.1, 'bias2': jax.random.normal(ks[5], (OUT_FEAT,), dtype=jnp.float32) * 0.1, 'src': jax.random.randint(ks[6], (N_EDGES,), 0, N_NODES, dtype=jnp.int64) if jax.config.jax_enable_x64 else jax.random.randint(ks[6], (N_EDGES,), 0, N_NODES).astype(jnp.int32), 'dst': jax.random.randint(ks[7], (N_EDGES,), 0, N_NODES).astype(jnp.int32), 'rel_type': jax.random.randint(ks[8], (N_EDGES,), 0, NUM_RELS).astype(jnp.int32)}
    _L2_gnn_all = _L2_gnn_setup()
    _L2_gnn_in = {k: v for k, v in _L2_gnn_all.items() if k in ('weight1', 'weight2', 'bias1', 'bias2')}
    del _L2_gnn_all

    def _L3_gnn_setup():
        import jax, jax.numpy as jnp
        import numpy as np
        N_NODES = 6250
        N_EDGES = 200000
        D_IN = 48
        D_OUT = 48
        key = jax.random.key(seed)
        k1, k2, k3, k4 = jax.random.split(key, 4)
        features = jax.random.normal(k1, (N_NODES, D_IN), dtype=jnp.float32)
        src = jax.random.randint(k2, (N_EDGES,), 0, N_NODES, dtype=jnp.int64)
        dst = jax.random.randint(k3, (N_EDGES,), 0, N_NODES, dtype=jnp.int64)
        std = np.sqrt(2.0 / (D_IN + D_OUT))
        W = jax.random.normal(k4, (D_OUT, D_IN), dtype=jnp.float32) * std
        b = jnp.zeros((D_OUT,), dtype=jnp.float32)
        return {'features': features, 'src': src, 'dst': dst, 'W': W, 'b': b}
    _L3_gnn_all = _L3_gnn_setup()
    _L3_gnn_in = {k: v for k, v in _L3_gnn_all.items() if k in ('W', 'b')}
    del _L3_gnn_all
    return {'x': x, 'src': src, 'dst': dst, 'edge_attr_40': edge_attr_40, 'edge_type_8': edge_type_8, 'edge_weight': edge_weight, 'edge_weight1': edge_weight1, 'node_type_119': node_type_119, 'node_vec': node_vec, 'L0_gnn_weights': _L0_gnn_in['weights'], 'L0_gnn_bias': _L0_gnn_in['bias'], 'L1_gnn_W1': _L1_gnn_in['W1'], 'L1_gnn_b1': _L1_gnn_in['b1'], 'L1_gnn_W2': _L1_gnn_in['W2'], 'L1_gnn_b2': _L1_gnn_in['b2'], 'L1_gnn_emb': _L1_gnn_in['emb'], 'L1_gnn_adaptW': _L1_gnn_in['adaptW'], 'L1_gnn_gamma': _L1_gnn_in['gamma'], 'L1_gnn_beta': _L1_gnn_in['beta'], 'L2_gnn_weight1': _L2_gnn_in['weight1'], 'L2_gnn_weight2': _L2_gnn_in['weight2'], 'L2_gnn_bias1': _L2_gnn_in['bias1'], 'L2_gnn_bias2': _L2_gnn_in['bias2'], 'L3_gnn_W': _L3_gnn_in['W'], 'L3_gnn_b': _L3_gnn_in['b']}

def reference(x, src, dst, edge_attr_40, edge_type_8, edge_weight, edge_weight1, node_type_119, node_vec, L0_gnn_weights, L0_gnn_bias, L1_gnn_W1, L1_gnn_b1, L1_gnn_W2, L1_gnn_b2, L1_gnn_emb, L1_gnn_adaptW, L1_gnn_gamma, L1_gnn_beta, L2_gnn_weight1, L2_gnn_weight2, L2_gnn_bias1, L2_gnn_bias2, L3_gnn_W, L3_gnn_b):
    import jax
    import jax.numpy as jnp

    def _L0_gnn_ref(node_emb, edge_index, weights, bias):
        import jax, jax.numpy as jnp
        import numpy as np
        N = 6250
        E = 200000
        C_IN = 48
        C_OUT = 48
        K = 16
        LAMBDA_MAX = 2.0
        src, dst = (edge_index[0], edge_index[1])
        ones = jnp.ones((edge_index.shape[1],), node_emb.dtype)
        deg = jax.ops.segment_sum(ones, src, num_segments=N)
        dis = jnp.where(deg > 0, jax.lax.rsqrt(jnp.maximum(deg, 1e-12)), 0.0)
        w = 2.0 / LAMBDA_MAX * (-dis[src] * dis[dst])
        diag_w = 2.0 / LAMBDA_MAX - 1.0

        def lhat(v):
            return jax.ops.segment_sum(w[:, None] * v[src], dst, num_segments=N) + diag_w * v
        tx_prev = node_emb
        out = tx_prev @ weights[0]
        tx = lhat(node_emb)
        out = out + tx @ weights[1]
        for k in range(2, K):
            tx_new = 2.0 * lhat(tx) - tx_prev
            out = out + tx_new @ weights[k]
            tx_prev, tx = (tx, tx_new)
        out = out + bias
        return jax.nn.relu(out)

    def _L1_gnn_ref(h, edge_index, edge_attr, distances, atom_z, node_mult, batch, W1, b1, W2, b2, emb, adaptW, gamma, beta):
        import jax, jax.numpy as jnp
        import numpy as np
        CUTOFF = 6.0
        LN_EPS = 1e-05
        src, dst = (edge_index[0], edge_index[1])
        N = h.shape[0]
        gate = jax.nn.silu(edge_attr @ W1.T + b1) @ W2.T + b2
        ei = emb[atom_z[src]]
        ej = emb[atom_z[dst]]
        adapt_logit = jnp.sum(ei * (ej @ adaptW.T), axis=-1, keepdims=True)
        gate = gate + adapt_logit
        cw = jnp.where(distances < CUTOFF, 0.5 * (jnp.cos(jnp.pi * distances / CUTOFF) + 1.0), 0.0)
        mj = node_mult[dst]
        msg = gate * h[dst] * (cw * mj)[:, None]
        agg = jax.ops.segment_sum(msg, src, num_segments=N)
        tot = jax.ops.segment_sum(mj, src, num_segments=N)
        agg = agg / jnp.clip(tot, 1e-08, None)[:, None]
        x = h + agg
        mu = jnp.mean(x, axis=-1, keepdims=True)
        var = jnp.mean(jnp.square(x - mu), axis=-1, keepdims=True)
        return (x - mu) / jnp.sqrt(var + LN_EPS) * gamma + beta

    def _L2_gnn_ref(inputs, norm, weight1, weight2, bias1, bias2, src, dst, rel_type):
        import jax, jax.numpy as jnp
        import numpy as np
        N_NODES = 6250
        N_EDGES = 200000
        IN_FEAT = 48
        OUT_FEAT = 48
        NUM_RELS = 8
        h1 = jax.nn.relu(jnp.einsum('ni,rij->nrj', inputs, weight1) + bias1)
        h2 = jnp.einsum('nrj,rjo->nro', h1, weight2)
        msg = h2[src, rel_type] * norm
        agg = jax.ops.segment_sum(msg, dst, num_segments=inputs.shape[0])
        return jax.nn.relu(agg + bias2)

    def _L3_gnn_ref(features, src, dst, W, b):
        import jax, jax.numpy as jnp
        import numpy as np
        N_NODES = 6250
        N_EDGES = 200000
        D_IN = 48
        D_OUT = 48
        n = features.shape[0]
        ones = jnp.ones(src.shape[0], dtype=features.dtype)
        out_deg = jax.ops.segment_sum(ones, src, num_segments=n)
        in_deg = jax.ops.segment_sum(ones, dst, num_segments=n)
        ci = jax.lax.rsqrt(jnp.maximum(out_deg, 1.0))
        cj = jax.lax.rsqrt(jnp.maximum(in_deg, 1.0))
        msg = features[src] * ci[src][:, None]
        agg = jax.ops.segment_sum(msg, dst, num_segments=n) * cj[:, None]
        h = jnp.where(in_deg[:, None] > 0, agg, features)
        out = jax.nn.relu(h @ W.T + b)
        return out
    edge_index = jnp.stack([src, dst])
    batch0 = jnp.zeros((6250,), jnp.int32)
    x = _layernorm(x + _L0_gnn_ref(x, edge_index, L0_gnn_weights, L0_gnn_bias), axis=-1)
    x = _layernorm(x + _L1_gnn_ref(x, edge_index, edge_attr_40, edge_weight, node_type_119, node_vec, batch0, L1_gnn_W1, L1_gnn_b1, L1_gnn_W2, L1_gnn_b2, L1_gnn_emb, L1_gnn_adaptW, L1_gnn_gamma, L1_gnn_beta), axis=-1)
    x = _layernorm(x + _L2_gnn_ref(x, edge_weight1, L2_gnn_weight1, L2_gnn_weight2, L2_gnn_bias1, L2_gnn_bias2, src, dst, edge_type_8), axis=-1)
    x = _layernorm(x + _L3_gnn_ref(x, src, dst, L3_gnn_W, L3_gnn_b), axis=-1)
    return x

_drawn_inputs = setup_inputs


def setup_inputs(seed=0):
    import zlib

    import numpy as np

    out = dict(_drawn_inputs(seed))
    spreads = {'L1_gnn_gamma': (1.0, 0.2), 'L1_gnn_beta': (0.0, 0.1), 'L3_gnn_b': (0.0, 0.1)}
    factors = {'edge_attr_40': 6.581,
     'edge_weight': 5.435,
     'node_vec': 7.158,
     'L1_gnn_W1': 3.852,
     'L1_gnn_b1': 171.84,
     'L1_gnn_W2': 3.543,
     'L1_gnn_b2': 200.0,
     'L1_gnn_emb': 64.0,
     'L1_gnn_adaptW': 64.0,
     'L2_gnn_bias2': 2.769}
    for name, (base, spread) in spreads.items():
        noise = np.random.default_rng([zlib.crc32(name.encode()), seed]).standard_normal(out[name].shape)
        drawn = base * np.exp(spread * noise) if base else spread * noise
        out[name] = jnp.asarray(drawn.astype(out[name].dtype))
    for name, factor in factors.items():
        out[name] = (out[name] * factor).astype(out[name].dtype)
    return out
```

```python
import concourse.bass as bass
from concourse import mybir
from concourse.alu_op_type import AluOpType as ALU
from contextlib import ExitStack, contextmanager

F32 = mybir.dt.float32
BF16 = mybir.dt.bfloat16
FP8 = mybir.dt.float8e4
I32 = mybir.dt.int32
U8 = mybir.dt.uint8
U32 = mybir.dt.uint32
ACT = mybir.ActivationFunctionType
AX = mybir.AxisListType

P = 128
N = 6250
D = 48
NB = -(-N // P)
NP = NB * P
E = 206250
G = 4
NG = 404
T = G * NG
K = 16
R = 40
Z, EM = 119, 32
NR = 8
ROW = 64 * P
STRIP = P * ROW
COPIES = G
AGROWS = NP + P
UW = D + 1 + EM
MW = D + 1
BEFORE = 1024.0


@contextmanager
def stage(nc):
    held = []

    def sem(name):
        held.append(nc.alloc_semaphore(name=name))
        return held[-1]
    with ExitStack() as memory:
        yield sem, memory
    nc.clear_and_free_semaphores(held)
    nc.all_engine_barrier()


def wait_alone(eng, semaphore, value, passed):
    eng.wait_ge(semaphore, value)
    eng.sem_inc(passed, 1)


def gnn_kernel(nc, h, out):
    dram = lambda name, shape, dt: nc.dram_tensor(name, shape, dt).ap()
    counts = dram("counts", ((NB + 1) * STRIP, 1), F32)
    strips8 = dram("strips8", (NB, P, NB * P), U8)
    cheb = dram("cheb", (P, NB, K, D), F32)
    z_table = dram("z_table", (Z, 2 * EM), F32)
    e_table = dram("e_table", (NP, EM), F32)
    u_table = dram("u_table", (NP, UW), F32)
    r_table = dram("r_table", (NP * NR, D), F32)
    agg1 = [dram(f"agg1_{c}", (AGROWS, MW), F32) for c in range(COPIES)]
    agg2 = [dram(f"agg2_{c}", (AGROWS, D), F32) for c in range(COPIES)]

    def strip32(j):
        return counts[bass.ds(j * STRIP, STRIP), :].rearrange("(p c) o -> p (c o)", p=P)[:, 0:NP]

    ctx = ExitStack()
    with ctx:
        def keep_sem(name):
            return ctx.enter_context(nc.semaphore(name))

        def sb(name, shape, dt, c=ctx):
            return c.enter_context(nc.sbuf_tensor(name, shape, dt))

        passed_sp, passed_act, passed_dve, passed_pe, passed_pool = passed = [
            keep_sem(f"passed_{e}") for e in ("sp", "act", "dve", "pe", "pool")]

        keys = sb("keys", [P, 2, T + 2 * G], I32)
        x_sb = sb("x_sb", [P, NB, D], F32)
        outdeg = sb("outdeg", [P, NB], F32)
        before = sb("before", [P, G, G * P], F32)
        ones_w = sb("ones_w", [P, G * P], F32)
        eye = sb("eye", [P, P], F32)

        with stage(nc) as (sem, c1):
            zeros = sb("zeros", [P, NP], F32, c1)
            s_keys, s_xin = sem("s_keys"), sem("s_xin")
            s_zero, s_clear, s_ones, s_eye0 = sem("s_zero"), sem("s_clear"), sem("s_ones"), sem("s_eye0")
            s_masks = sem("s_masks")
            with nc.Block() as block:
                @block.sync
                def _(sp):
                    sp.dma_start(keys[:, :, :], h["key_cols"]).then_inc(s_keys, 16)
                    sp.dma_start(x_sb[:, :, :], h["x"]).then_inc(s_xin, 16)
                    sp.wait_ge(s_zero, 1)
                    with sp.Fori(0, NB) as j:
                        sp.dma_start(strip32(j), zeros[:, :]).then_inc(s_clear, 16)
                    sp.dma_start(counts[NB * STRIP:NB * STRIP + G * P, :].rearrange("(p c) o -> p (c o)", p=P),
                                 zeros[:, 0:G]).then_inc(s_clear, 16)
                    for c in range(COPIES):
                        sp.dma_start(agg1[c].rearrange("(p b) f -> p (b f)", p=P),
                                     zeros[:, 0:AGROWS // P * MW]).then_inc(s_clear, 16)
                        sp.dma_start(agg2[c].rearrange("(p b) f -> p (b f)", p=P),
                                     zeros[:, 0:AGROWS // P * D]).then_inc(s_clear, 16)
                    sp.wait_ge(s_keys, 16)
                    sp.wait_ge(s_xin, 16)
                    sp.wait_ge(s_clear, 16 * (NB + 1 + 2 * COPIES))

                @block.vector
                def _(dve):
                    nc.vector.memset(zeros[:, :], 0.0).then_inc(s_zero, 1)

                @block.gpsimd
                def _(pool):
                    pool.memset(ones_w[:, :], 1.0).then_inc(s_ones, 1)
                    pool.memset(eye[:, :], 0.0).then_inc(s_eye0, 1)
                    pool.wait_ge(s_ones, 1)
                    for j in range(G):
                        pool.affine_select(out=before[:, j, :], in_=ones_w[:, :], compare_op=ALU.is_ge,
                                           fill=BEFORE, base=-P * j, pattern=[[1, G * P]],
                                           channel_multiplier=-1).then_inc(s_masks, 1)
                    pool.wait_ge(s_eye0, 1)
                    pool.affine_select(out=eye[:, :], in_=eye[:, :], compare_op=ALU.not_equal, fill=1.0,
                                       base=0, pattern=[[-1, P]], channel_multiplier=1).then_inc(s_masks, 1)

        with stage(nc) as (sem, c2):
            keyf = sb("keyf", [P, 2, T], F32, c2)
            cell = sb("cell", [P, T], I32, c2)
            cell_t = sb("cell_t", [P, T], I32, c2)
            rows = sb("rows", [P, 2, 2, G * P], I32, c2)
            eq_dst = sb("eq_dst", [P, G, G * P], F32, c2)
            found = sb("found", [P, 2, G], F32, c2)
            late = sb("late", [P, 2, G], I32, c2)
            where = sb("where", [P, 2, G], I32, c2)
            spare = sb("spare", [P, G], I32, c2)
            s_prep, s_spare = sem("s_prep"), sem("s_spare")
            s_rows = [sem("s_rows0"), sem("s_rows1")]
            s_rowfree = sem("s_rowfree")
            s_eqd, s_eqs, s_late, s_cellcp, s_where, s_added = (
                sem("s_eqd"), sem("s_eqs"), sem("s_late"), sem("s_cellcp"), sem("s_where"), sem("s_added"))
            s_slot = sem("s_slot")
            with nc.Block() as block:
                @block.sync
                def _(sp):
                    def load(g, b):
                        wait_alone(sp, s_rowfree, g + 1, passed_sp)
                        src = h["key_rows"][bass.ds(g, 1), :].rearrange("o (k c) -> o k c", k=2)
                        sp.dma_start(rows[:, b, :, :], src.to_broadcast([P, 2, G * P])).then_inc(s_rows[b], 16)
                    with sp.Fori(0, NG // 2) as i:
                        for b in range(2):
                            load(i * 2 + b, b)

                @block.vector
                def _(dve):
                    dve.sem_inc(s_rowfree, 2)
                    n = 0
                    src, dst = keys[:, 0, 0:T], keys[:, 1, 0:T]
                    nc.vector.tensor_copy(keyf[:, :, :], keys[:, :, 0:T]).then_inc(s_prep, 1)
                    blocks = (P - 1) * P * 0 + 0x1F80
                    nc.vector.tensor_scalar(cell[:, :], dst, blocks, 13, ALU.bitwise_and,
                                            ALU.logical_shift_left).then_inc(s_prep, 1)
                    nc.vector.tensor_scalar(cell_t[:, :], src, P - 1, 13, ALU.bitwise_and,
                                            ALU.logical_shift_left).then_inc(s_prep, 1)
                    dve.wait_ge(s_prep, 3)
                    nc.vector.tensor_tensor(cell[:, :], cell[:, :], cell_t[:, :], ALU.bitwise_or).then_inc(s_prep, 1)
                    dve.wait_ge(s_prep, 4)
                    nc.vector.tensor_scalar(cell_t[:, :], src, blocks, None, ALU.bitwise_and).then_inc(s_prep, 1)
                    dve.wait_ge(s_prep, 5)
                    nc.vector.tensor_tensor(cell[:, :], cell[:, :], cell_t[:, :], ALU.bitwise_or).then_inc(s_prep, 1)
                    dve.wait_ge(s_prep, 6)
                    nc.vector.tensor_scalar(cell_t[:, :], dst, P - 1, None, ALU.bitwise_and).then_inc(s_prep, 1)
                    dve.wait_ge(s_prep, 7)
                    nc.vector.tensor_tensor(cell[:, :], cell[:, :], cell_t[:, :], ALU.bitwise_or).then_inc(s_prep, 1)
                    dve.wait_ge(s_prep, 8)
                    dve.wait_ge(s_spare, 1)
                    dve.sem_inc(s_slot, 2)

                    def group(i, g, b):
                        dve.wait_ge(s_rows[b], 16 * (i + 1))
                        for j in range(G):
                            nc.vector.scalar_tensor_tensor(
                                eq_dst[:, j, :], rows[:, b, 1, :], keyf[:, 1, bass.ds(g * G + j, 1)],
                                before[:, j, :], ALU.is_equal, ALU.mult).then_inc(s_eqd, 1)
                        dve.wait_ge(s_slot, g + 1)
                        nc.vector.tensor_copy(where[:, b, :], cell[:, bass.ds(g * G, G)]).then_inc(s_cellcp, 1)
                        for j in range(G):
                            dve.wait_ge(s_eqd, g * G + j + 1)
                            eq = nc.vector.scalar_tensor_tensor(
                                eq_dst[:, j, :], rows[:, b, 0, :], keyf[:, 0, bass.ds(g * G + j, 1)],
                                eq_dst[:, j, :], ALU.is_equal, ALU.mult, accum_out=found[:, b, j:j + 1])
                            eq.then_inc(s_eqs, 1)
                        dve.wait_ge(s_eqs, (g + 1) * G)
                        nc.vector.tensor_scalar(late[:, b, :], found[:, b, :], BEFORE, None,
                                                ALU.is_ge).then_inc(s_late, 1)
                        dve.wait_ge(s_cellcp, g + 1)
                        dve.wait_ge(s_late, g + 1)
                        dve.sem_inc(s_rowfree, 1)
                        nc.vector.copy_predicated(where[:, b, :], late[:, b, :], spare[:, :]).then_inc(s_where, 1)

                    with dve.Fori(0, NG // 2) as i:
                        for b in range(2):
                            group(i, i * 2 + b, b)

                @block.gpsimd
                def _(pool):
                    pool.iota(spare[:, :], pattern=[[P, G]], base=NB * STRIP, channel_multiplier=1).then_inc(s_spare, 1)

                    def group(g, b):
                        wait_alone(pool, s_where, g + 1, passed_pool)
                        for j in range(G):
                            pool.indirect_dma_start(
                                out=counts,
                                out_offset=bass.IndirectOffsetOnAxis(ap=where[:, b, j:j + 1].bitcast(U32), axis=0),
                                in_=found[:, b, j:j + 1], in_offset=None,
                                compute_op=ALU.add).then_inc(s_added, 16)
                        pool.wait_ge(s_added, 16 * G * (g + 1))
                        pool.sem_inc(s_slot, 1)

                    with pool.Fori(0, NG // 2) as i:
                        for b in range(2):
                            group(i * 2 + b, b)

        with stage(nc) as (sem, c3):
            U = 4
            wide = sb("wide", [P, U, NP], F32, c3)
            narrow = sb("narrow", [P, U, NP], FP8, c3)
            relu_out = sb("relu_out", [P, NP], BF16, c3)
            part = sb("part", [P, U, NB], F32, c3)
            s_in = [sem(f"s_in{u}") for u in range(U)]
            s_saved = [sem(f"s_saved{u}") for u in range(U)]
            s_cast, s_sum, s_deg = sem("s_cast"), sem("s_sum"), sem("s_deg")
            with nc.Block() as block:
                @block.sync
                def _(sp):
                    def load(j, u, first):
                        if not first:
                            wait_alone(sp, s_cast, j - U + 1, passed_sp)
                            wait_alone(sp, s_sum, j - U + 1, passed_sp)
                        sp.dma_start(wide[:, u, :], strip32(j)).then_inc(s_in[u], 16)
                    for u in range(U):
                        load(u, u, True)
                    with sp.Fori(1, NB // U) as i:
                        for u in range(U):
                            load(i * U + u, u, False)
                    load(NB - 1, 0, False)

                @block.scalar
                def _(act):
                    def cast(i, j, u, first):
                        act.wait_ge(s_in[u], 16 * (i + 1))
                        if not first:
                            wait_alone(act, s_saved[u], 16 * i, passed_act)
                        nc.scalar.activation(narrow[:, u, :], wide[:, u, :], ACT.Copy, saturate=False).then_inc(s_cast, 1)
                        wait_alone(act, s_cast, j + 1, passed_act)
                        act.dma_start(strips8[bass.ds(j, 1), :, :].rearrange("o p c -> p (o c)"),
                                      narrow[:, u, :].bitcast(U8)).then_inc(s_saved[u], 16)
                    for u in range(U):
                        cast(0, u, u, True)
                    with act.Fori(1, NB // U) as i:
                        for u in range(U):
                            cast(i, i * U + u, u, False)
                    cast(NB // U, NB - 1, 0, False)
                    act.wait_ge(s_saved[0], 16 * (NB // U + 1))
                    for u in range(1, U):
                        act.wait_ge(s_saved[u], 16 * (NB // U))

                @block.vector
                def _(dve):
                    nc.vector.memset(outdeg[:, :], 0.0).then_inc(s_deg, 1)

                    def degrees(i, j, u):
                        dve.wait_ge(s_in[u], 16 * (i + 1))
                        nc.vector.tensor_reduce(part[:, u, :], wide[:, u, :].rearrange("p (b c) -> p b c", c=P),
                                                AX.X, ALU.add).then_inc(s_sum, 1)
                        dve.wait_ge(s_sum, j + 1)
                        dve.wait_ge(s_deg, j + 1)
                        nc.vector.tensor_tensor(outdeg[:, :], outdeg[:, :], part[:, u, :], ALU.add).then_inc(s_deg, 1)
                    with dve.Fori(0, NB // U) as i:
                        for u in range(U):
                            degrees(i, i * U + u, u)
                    degrees(NB // U, NB - 1, 0)

        stage4(nc, h, sb, strips8, cheb, x_sb, outdeg, eye, passed)
        tables_of_layer1(nc, h, sb, z_table, e_table, u_table, x_sb)
        gather_and_sum(nc, h, sb, 1, keys, before, u_table, e_table, agg1)
        end_of_layer1(nc, h, sb, agg1, x_sb)
        table_of_layer2(nc, h, sb, r_table, x_sb, eye, passed_pe)
        gather_and_sum(nc, h, sb, 2, keys, before, r_table, None, agg2)
        end_of_layer2(nc, h, sb, agg2, x_sb)
        layer3(nc, h, sb, strips8, x_sb, outdeg, eye, passed)
        with stage(nc) as (sem, c9):
            s_o = sem("s_o")
            with nc.Block() as block:
                @block.sync
                def _(sp):
                    sp.dma_start(out, x_sb[:, :, :]).then_inc(s_o, 16)
                    sp.wait_ge(s_o, 16)


def in_order(eng, done):
    count = [0]

    def step(instruction):
        count[0] += 1
        instruction.then_inc(done, 1)
        eng.wait_ge(done, count[0])
    return step


def wide_ap(col):
    return col.unsqueeze(2).to_broadcast([P, NB, D])


def row_ap(row):
    return row.unsqueeze(1).to_broadcast([P, NB, D])


def normalize(nc, step, sqrt_of, x, sq, col, eps_col):
    mean, var = col[:, 0, :], col[:, 1, :]
    step(nc.vector.tensor_reduce(mean, x, AX.X, ALU.add))
    step(nc.vector.tensor_scalar(mean, mean, 1.0 / D, None, ALU.mult))
    step(nc.vector.tensor_tensor(x, x, wide_ap(mean), ALU.subtract))
    step(nc.vector.tensor_tensor(sq, x, x, ALU.mult))
    step(nc.vector.tensor_reduce(var, sq, AX.X, ALU.add))
    step(nc.vector.tensor_scalar(var, var, 1.0 / D, 1e-5, ALU.mult, ALU.add))
    sqrt_of(var)
    step(nc.vector.reciprocal(var, var))
    step(nc.vector.tensor_tensor(x, x, wide_ap(var), ALU.mult))


def stage4(nc, h, sb, strips8, cheb, x_sb, outdeg, eye, passed):
    passed_sp, passed_act, passed_dve, passed_pe, passed_pool = passed
    U = 7
    W3 = 3 * D
    with stage(nc) as (sem, c4):
        dis = sb("dis", [P, NB], F32, c4)
        dis_m1 = sb("dis_m1", [P, NB], F32, c4)
        dis_m2 = sb("dis_m2", [P, NB], F32, c4)
        has = sb("has", [P, NB], F32, c4)
        term = sb("term", [P, 2, NB, D], F32, c4)
        parts = sb("parts", [P, 2, NB, W3], BF16, c4)
        cbuf = sb("cbuf", [P, U, NP], FP8, c4)
        y = sb("y", [P, U, D], F32, c4)
        v = sb("v", [P, U, D], F32, c4)
        r = sb("r", [P, U, D], F32, c4)
        acc = [c4.enter_context(nc.psum_tensor(f"acc{u}", [P, 512], F32)) for u in range(U)]
        s_c = [sem(f"s_c{u}") for u in range(U)]
        s_strip, s_accfree, s_parts, s_term = sem("s_strip"), sem("s_accfree"), sem("s_parts"), sem("s_term")
        s_kept = [sem("s_kept0"), sem("s_kept1")]
        s_prep4, s_root, s_root_in = sem("s_prep4"), sem("s_root"), sem("s_root_in")
        s_y, s_v, s_hi, s_r, s_mid = sem("s_y"), sem("s_v"), sem("s_hi"), sem("s_r"), sem("s_mid")
        with nc.Block() as block:
            @block.sync
            def _(sp):
                def load(n0, rr, u, first):
                    if not first:
                        wait_alone(sp, s_strip, n0 + rr * U + u - U + 1, passed_sp)
                    sp.dma_start(cbuf[:, u, :].bitcast(U8), strips8[bass.ds(rr * U + u, 1), :, :].rearrange("o p c -> p (o c)")
                                 ).then_inc(s_c[u], 16)
                for u in range(U):
                    load(0, 0, u, True)
                with sp.Fori(1, NB // U) as rr:
                    for u in range(U):
                        load(0, rr, u, False)
                with sp.Fori(1, K - 1) as k:
                    with sp.Fori(0, NB // U) as rr:
                        for u in range(U):
                            load(k * NB, rr, u, False)

            @block.tensor
            def _(pe):
                def strip(slot, n_div, n, u):
                    pe.wait_ge(s_c[u], 16 * (n_div + 1))
                    wait_alone(pe, s_accfree, n + 1, passed_pe)
                    for s in range(NB):
                        mm = nc.tensor.matmul(acc[u][:, 0:W3], cbuf[:, u, s * P:(s + 1) * P],
                                              parts[:, slot, s, :], start=(s == 0), stop=(s == NB - 1))
                    mm.then_inc(s_strip, 1)

                def one_pass(k):
                    wait_alone(pe, s_parts, NB * k, passed_pe)

                def strips(k, slot):
                    with pe.Fori(0, NB // U) as rr:
                        for u in range(U):
                            strip(slot, (k - 1) * (NB // U) + rr, (k - 1) * NB + rr * U + u, u)
                one_pass(1)
                strips(1, 0)
                with pe.Fori(0, (K - 2) // 2) as m:
                    one_pass(m * 2 + 2)
                    strips(m * 2 + 2, 1)
                    one_pass(m * 2 + 3)
                    strips(m * 2 + 3, 0)

            @block.scalar
            def _(act):
                act.wait_ge(s_root_in, 1)
                nc.scalar.activation(dis[:, :], dis[:, :], ACT.Sqrt).then_inc(s_root, 1)
                def keep(k, slot):
                    wait_alone(act, s_term, NB * (k + 1), passed_act)
                    act.dma_start(cheb[:, :, bass.ds(k, 1), :].rearrange("p b k f -> p b (k f)"),
                                  term[:, slot, :, :]).then_inc(s_kept[slot], 16)
                keep(0, 0)
                with act.Fori(0, (K - 2) // 2) as m:
                    keep(m * 2 + 1, 1)
                    keep(m * 2 + 2, 0)
                keep(K - 1, 1)
                act.wait_ge(s_kept[0], 16 * (K // 2))
                act.wait_ge(s_kept[1], 16 * (K // 2))

            @block.vector
            def _(dve):
                step = in_order(dve, s_prep4)
                step(nc.vector.tensor_scalar(dis[:, :], outdeg[:, :], 1e-12, None, ALU.max))
                dve.sem_inc(s_root_in, 1)
                step(nc.vector.tensor_scalar(has[:, :], outdeg[:, :], 0.0, None, ALU.is_gt))
                dve.wait_ge(s_root, 1)
                step(nc.vector.reciprocal(dis[:, :], dis[:, :]))
                step(nc.vector.tensor_tensor(dis[:, :], dis[:, :], has[:, :], ALU.mult))
                step(nc.vector.tensor_scalar(dis_m1[:, :], dis[:, :], -1.0, None, ALU.mult))
                step(nc.vector.tensor_scalar(dis_m2[:, :], dis[:, :], -2.0, None, ALU.mult))
                step(nc.vector.tensor_copy(term[:, 0, :, :], x_sb[:, :, :]))
                step(nc.vector.memset(term[:, 1, :, :], 0.0))
                dve.sem_inc(s_accfree, U)

                def split(slot, b, u, n):
                    blk = lambda t: t[:, slot, bass.ds(b, 1), :].rearrange("p o f -> p (o f)")
                    hi, mid, lo = (parts[:, slot, bass.ds(b, 1), i * D:(i + 1) * D].rearrange("p o f -> p (o f)")
                                   for i in range(3))
                    dve.wait_ge(s_term, n + 1)
                    nc.vector.tensor_scalar(v[:, u, :], blk(term), dis[:, bass.ds(b, 1)], None, ALU.mult).then_inc(s_v, 1)
                    dve.wait_ge(s_v, n + 1)
                    nc.vector.tensor_copy(hi, v[:, u, :]).then_inc(s_hi, 1)
                    dve.wait_ge(s_hi, n + 1)
                    nc.vector.tensor_tensor(r[:, u, :], v[:, u, :], hi, ALU.subtract).then_inc(s_r, 1)
                    dve.wait_ge(s_r, n + 1)
                    nc.vector.tensor_copy(mid, r[:, u, :]).then_inc(s_mid, 1)
                    dve.wait_ge(s_mid, n + 1)
                    nc.vector.tensor_tensor(lo, r[:, u, :], mid, ALU.subtract).then_inc(s_parts, 1)

                def block_of_term(k, rr, u, slot, scale):
                    b = rr * U + u
                    n = (k - 1) * NB + b
                    dve.wait_ge(s_strip, n + 1)
                    nc.vector.tensor_reduce(y[:, u, :], acc[u][:, 0:W3].rearrange("p (s f) -> p f s", f=D),
                                            AX.X, ALU.add).then_inc(s_y, 1)
                    dve.wait_ge(s_y, n + 1)
                    dve.sem_inc(s_accfree, 1)
                    t = term[:, slot, bass.ds(b, 1), :].rearrange("p o f -> p (o f)")
                    nc.vector.scalar_tensor_tensor(t, y[:, u, :], scale[:, bass.ds(b, 1)], t,
                                                   ALU.mult, ALU.subtract).then_inc(s_term, 1)
                    split(slot, b, u, n + NB)

                dve.sem_inc(s_term, NB)
                with dve.Fori(0, NB // U) as rr:
                    for u in range(U):
                        split(0, rr * U + u, u, rr * U + u)
                with dve.Fori(0, NB // U) as rr:
                    for u in range(U):
                        block_of_term(1, rr, u, 1, dis_m1)
                with dve.Fori(0, (K - 2) // 2) as m:
                    for odd in range(2):
                        wait_alone(dve, s_kept[odd], (m + 1) * 16, passed_dve)
                        with dve.Fori(0, NB // U) as rr:
                            for u in range(U):
                                block_of_term(m * 2 + 2 + odd, rr, u, odd, dis_m2)

    U = 4
    Q = K // 2
    with stage(nc) as (sem, c5):
        tin = sb("tin", [P, U, K, D], F32, c5)
        tT = sb("tT", [2 * D, 2, Q, P], F32, c5)
        w0 = sb("w0", [2 * D, Q, D], F32, c5)
        b0 = sb("b0", [P, D], F32, c5)
        o_sb = sb("o_sb", [P, NB, D], F32, c5)
        sq = sb("sq", [P, NB, D], F32, c5)
        col = sb("col", [P, 2, NB], F32, c5)
        turned = [[c5.enter_context(nc.psum_tensor(f"turned{a}{b}", [P, 512], F32)) for b in range(2)] for a in range(2)]
        acc = [c5.enter_context(nc.psum_tensor(f"acc5_{u}", [P, 512], F32)) for u in range(2)]
        s_t = [sem(f"s_t{u}") for u in range(U)]
        s_w0 = sem("s_w0")
        s_turn, s_copyA, s_copyB, s_out0, s_ofree, s_tfree = (
            sem("s_turn"), sem("s_copyA"), sem("s_copyB"), sem("s_out0"), sem("s_ofree"), sem("s_tfree"))
        s_ln0, s_sq0, s_sqi0 = sem("s_ln0"), sem("s_sq0"), sem("s_sqi0")

        def over_blocks(eng, body):
            with eng.Fori(0, NB // U) as i:
                for u in range(U):
                    body(i, i * U + u, u)
            body(NB // U, NB - 1, 0)

        with nc.Block() as block:
            @block.sync
            def _(sp):
                sp.dma_start(w0[:, :, :], h["w0"]).then_inc(s_w0, 16)
                sp.dma_start(b0[:, :], h["b0"]).then_inc(s_w0, 16)
                sp.sem_inc(s_tfree, U)

                def load(i, b, u):
                    wait_alone(sp, s_tfree, b + 1, passed_sp)
                    sp.dma_start(tin[:, u, :, :], cheb[:, bass.ds(b, 1), :, :].rearrange("p o k f -> p (o k) f")
                                 ).then_inc(s_t[u], 16)
                over_blocks(sp, load)

            @block.tensor
            def _(pe):
                pe.wait_ge(s_w0, 32)

                def body(i, b, u):
                    o = u % 2
                    pe.wait_ge(s_t[u], 16 * (i + 1))
                    for a in range(2):
                        for q in range(Q // 2):
                            tr = nc.tensor.transpose(turned[o][a][0:2 * D, q * P:(q + 1) * P],
                                                     tin[:, u, 2 * (a * Q // 2 + q):2 * (a * Q // 2 + q) + 2, :]
                                                     .rearrange("p k f -> p (k f)"), eye[:, :])
                        tr.then_inc(s_turn, 1)
                    pe.wait_ge(s_copyA, b + 1)
                    pe.wait_ge(s_copyB, b + 1)
                    pe.sem_inc(s_tfree, 1)
                    pe.wait_ge(s_ofree, b + 1)
                    for q in range(Q):
                        mm = nc.tensor.matmul(acc[o][:, 0:D], tT[:, o, q, :], w0[:, q, :], start=(q == 0), stop=(q == Q - 1))
                    mm.then_inc(s_out0, 1)
                over_blocks(pe, body)

            @block.scalar
            def _(act):
                def body(i, b, u):
                    act.wait_ge(s_turn, b * 2 + 1)
                    act.wait_ge(s_out0, b + 1)
                    nc.scalar.activation(tT[:, u % 2, 0:Q // 2, :].rearrange("p q c -> p (q c)"),
                                         turned[u % 2][0][0:2 * D, :], ACT.Copy).then_inc(s_copyA, 1)
                act.sem_inc(s_out0, 2)
                over_blocks(act, body)
                act.wait_ge(s_sqi0, 1)
                nc.scalar.activation(col[:, 1, :], col[:, 1, :], ACT.Sqrt).then_inc(s_sq0, 1)

            @block.vector
            def _(dve):
                dve.sem_inc(s_ofree, 2)

                def body(i, b, u):
                    dve.wait_ge(s_turn, b * 2 + 2)
                    dve.wait_ge(s_out0, b + 1)
                    nc.vector.tensor_copy(tT[:, u % 2, Q // 2:Q, :].rearrange("p q c -> p (q c)"),
                                          turned[u % 2][1][0:2 * D, :]).then_inc(s_copyB, 1)
                    dve.wait_ge(s_out0, b + 3)
                    nc.vector.tensor_tensor(o_sb[:, bass.ds(b, 1), :].rearrange("p o f -> p (o f)"),
                                            acc[u % 2][:, 0:D], b0[:, :], ALU.add).then_inc(s_ofree, 1)
                dve.wait_ge(s_w0, 32)
                over_blocks(dve, body)
                step = in_order(dve, s_ln0)
                dve.wait_ge(s_ofree, NB + 2)
                step(nc.vector.scalar_tensor_tensor(x_sb[:, :, :], o_sb[:, :, :], 0.0, x_sb[:, :, :], ALU.max, ALU.add))

                def root(var):
                    dve.sem_inc(s_sqi0, 1)
                    dve.wait_ge(s_sq0, 1)
                normalize(nc, step, root, x_sb[:, :, :], sq[:, :, :], col, None)


def tables_of_layer1(nc, h, sb, z_table, e_table, u_table, x_sb):
    with stage(nc) as (sem, c6):
        emb = sb("emb", [Z, 2 * EM], F32, c6)
        embT = sb("embT", [EM, Z], F32, c6)
        adapt = sb("adapt", [EM, EM], F32, c6)
        kind = sb("kind", [P, NB], I32, c6)
        mult = sb("mult", [P, NB], F32, c6)
        of_node = sb("of_node", [P, NB, 2 * EM], F32, c6)
        u_rows = sb("u_rows", [P, NB, UW], F32, c6)
        adapted = c6.enter_context(nc.psum_tensor("adapted", [P, 512], F32))
        s_small, s_adapted, s_emb, s_ztab, s_node, s_rows6, s_tab6, s_kind = (
            sem("s_small"), sem("s_adapted"), sem("s_emb"), sem("s_ztab"), sem("s_node"), sem("s_rows6"),
            sem("s_tab6"), sem("s_kind"))
        with nc.Block() as block:
            @block.sync
            def _(sp):
                sp.dma_start(emb[:, 0:EM], h["emb"]).then_inc(s_small, 16)
                sp.dma_start(embT[:, :], h["embT"]).then_inc(s_small, 16)
                sp.dma_start(adapt[:, :], h["adaptT"]).then_inc(s_small, 16)
                sp.dma_start(kind[:, :], h["kind"]).then_inc(s_kind, 16)
                sp.dma_start(mult[:, :], h["mult"]).then_inc(s_kind, 16)
                sp.wait_ge(s_emb, 1)
                sp.wait_ge(s_small, 48)
                sp.dma_start(z_table, emb[:, :]).then_inc(s_ztab, 16)
                sp.wait_ge(s_node, 16 * NB)
                sp.dma_start(e_table.rearrange("(b p) f -> p b f", p=P), of_node[:, :, 0:EM]).then_inc(s_tab6, 16)
                sp.wait_ge(s_rows6, 3)
                sp.dma_start(u_table.rearrange("(b p) f -> p b f", p=P), u_rows[:, :, :]).then_inc(s_tab6, 16)
                sp.wait_ge(s_tab6, 32)

            @block.tensor
            def _(pe):
                pe.wait_ge(s_small, 48)
                nc.tensor.matmul(adapted[0:Z, 0:EM], embT[:, :], adapt[:, :], start=True, stop=True).then_inc(s_adapted, 1)

            @block.gpsimd
            def _(pool):
                pool.wait_ge(s_ztab, 16)
                pool.wait_ge(s_kind, 32)
                for b in range(NB):
                    pool.indirect_dma_start(out=of_node[:, b, :], out_offset=None, in_=z_table,
                                            in_offset=bass.IndirectOffsetOnAxis(ap=kind[:, b:b + 1].bitcast(U32), axis=0)
                                            ).then_inc(s_node, 16)

            @block.vector
            def _(dve):
                dve.wait_ge(s_adapted, 1)
                nc.vector.tensor_copy(emb[:, EM:2 * EM], adapted[0:Z, 0:EM]).then_inc(s_emb, 1)
                dve.wait_ge(s_kind, 32)
                nc.vector.tensor_tensor(u_rows[:, :, 0:D], x_sb[:, :, :], wide_ap(mult[:, :]), ALU.mult).then_inc(s_rows6, 1)
                nc.vector.tensor_copy(u_rows[:, :, D:D + 1].rearrange("p b o -> p (b o)"), mult[:, :]).then_inc(s_rows6, 1)
                dve.wait_ge(s_node, 16 * NB)
                nc.vector.tensor_copy(u_rows[:, :, D + 1:UW], of_node[:, :, EM:2 * EM]).then_inc(s_rows6, 1)


def gather_and_sum(nc, h, sb, layer, keys, before, table, e_table, agg):
    one = layer == 1
    W = MW if one else D
    GW = UW if one else D
    side = 0 if one else 1
    n_gather = 2 if one else 1
    L = f"L{layer}_"
    with stage(nc) as (sem, c7):
        def s_(name):
            return sem(L + name)

        def t_(name, shape, dt=F32):
            return sb(L + name, shape, dt, c7)

        keyf = t_("keyf", [P, T])
        weight = t_("weight", [P, T])
        rows = t_("rows", [P, 2, G * P], I32)
        equal = t_("equal", [P, 2, G, P])
        earlier = t_("earlier", [P, G, P])
        found = t_("found", [P, G])
        late = t_("late", [P, G], I32)
        where = t_("where", [P, 2, G], I32)
        spare = t_("spare", [P, G], I32)
        ring = t_("ring", [P, 2, 2, G], I32)
        got = t_("got", [P, 2, G, GW])
        total = t_("total", [P, 2, G, W])
        summed = [c7.enter_context(nc.psum_tensor(L + f"summed{b}", [P, 512], F32)) for b in range(2)]
        if one:
            got_e = t_("got_e", [P, 2, G, EM])
            prod = t_("prod", [P, G, EM])
            logit = t_("logit", [P, G])
            gate = t_("gate", [P, G, D])
            msg = t_("msg", [P, 2, G, MW])
            attr = t_("attr", [2 * R, 2, G // 2 * P])
            hid = t_("hid", [2 * D + 1, 2, G // 2 * P])
            w1 = t_("w1", [2 * R, 2 * D])
            w2 = t_("w2", [2 * D + 1, 2 * D])
            b1 = t_("b1", [2 * D, 1])
            half_pi = t_("half_pi", [P, 1])
            hidp = [c7.enter_context(nc.psum_tensor(L + f"hidp{b}", [P, 512], F32)) for b in range(2)]
            gatep = [c7.enter_context(nc.psum_tensor(L + f"gatep{b}", [P, 512], F32)) for b in range(2)]
            s_attr = [s_("attr0"), s_("attr1")]
            s_mm1, s_hid, s_gate, s_gadd, s_prod, s_logit, s_gcw, s_multcol = (
                s_("mm1"), s_("hid"), s_("gate"), s_("gadd"), s_("prod"), s_("logit"), s_("gcw"), s_("multcol"))
            s_cos_in, s_cos, s_ones = s_("cos_in"), s_("cos"), s_("ones")
        else:
            relation = t_("relation", [P, T + 2 * G], I32)
        s_rows = [s_("rows0"), s_("rows1")]
        s_got = [s_("got0"), s_("got1")]
        s_ring, s_used, s_rowsfree, s_equal, s_earlier, s_late, s_cp, s_where = (
            s_("ring"), s_("used"), s_("rowsfree"), s_("equal"), s_("earlier"), s_("late"), s_("cp"), s_("where"))
        s_summed, s_total, s_slot, s_const, s_w, s_prep, s_spare = (
            s_("summed"), s_("total"), s_("slot"), s_("const"), s_("w"), s_("prep"), s_("spare"))
        s_passed = s_("passed")
        s_sc = [s_(f"sc{j}") for j in range(COPIES)]

        with nc.Block() as block:
            @block.sync
            def _(sp):
                sp.dma_start(weight[:, :], h["distance" if one else "weight"]).then_inc(s_w, 16)
                if one:
                    sp.dma_start(w1[:, :], h["l1_w1"]).then_inc(s_const, 16)
                    sp.dma_start(w2[:, :], h["l1_w2"]).then_inc(s_const, 16)
                    sp.dma_start(b1[:, :], h["l1_b1"]).then_inc(s_const, 16)
                else:
                    sp.dma_start(relation[:, :], h["relation"]).then_inc(s_const, 16)
                sp.sem_inc(s_rowsfree, 2)

                def load_rows(g, b):
                    wait_alone(sp, s_rowsfree, g + 1, s_passed)
                    src = h["key_rows"][bass.ds(g, 1), side * G * P:(side + 1) * G * P]
                    sp.dma_start(rows[:, b, :], src.to_broadcast([P, G * P])).then_inc(s_rows[b], 16)

                def load_attr(g, b):
                    if one:
                        wait_alone(sp, s_hid, g + 1, s_passed)
                        sp.dma_start(attr[:, b, :], h["attr"][bass.ds(g, 1), :, :].rearrange("o p c -> p (o c)")
                                     ).then_inc(s_attr[b], 16)
                load_attr(0, 0)
                with sp.Fori(0, NG // 2) as i:
                    for b in range(2):
                        g = i * 2 + b
                        load_rows(g, b)
                        load_attr(g + 1, 1 - b)

            @block.tensor
            def _(pe):
                def hidden(i, g, b):
                    if one:
                        pe.wait_ge(s_attr[b], 16 * (i + 1))
                        pe.wait_ge(s_hid, g + 1)
                        nc.tensor.matmul(hidp[b][0:2 * D, 0:G // 2 * P], w1[:, :], attr[:, b, :],
                                         start=True, stop=True).then_inc(s_mm1, 1)
                if one:
                    pe.wait_ge(s_const, 48)
                hidden(0, 0, 0)
                with pe.Fori(0, NG // 2) as i:
                    for b in range(2):
                        g = i * 2 + b
                        hidden(i + b, g + 1, 1 - b)
                        if one:
                            pe.wait_ge(s_hid, g + 3)
                            pe.wait_ge(s_gadd, g + 1)
                            for q in range(G // 2):
                                mm = nc.tensor.matmul(gatep[b][:, q * 2 * D:(q + 1) * 2 * D],
                                                      hid[:, b, q * P:(q + 1) * P], w2[:, :], start=True, stop=True)
                            mm.then_inc(s_gate, 1)
                        if one:
                            pe.wait_ge(s_used, g + 3)
                        else:
                            pe.wait_ge(s_got[b], 16 * G * (i + 1))
                        pe.wait_ge(s_equal, (g + 1) * G)
                        pe.wait_ge(s_total, g + 1)
                        for j in range(G):
                            mm = nc.tensor.matmul(summed[b][:, j * W:(j + 1) * W], equal[:, b, j, :],
                                                  (msg if one else got)[:, b, j, :], start=True, stop=True)
                        mm.then_inc(s_summed, 1)

            @block.scalar
            def _(act):
                act.sem_inc(s_total, 2)
                if one:
                    act.wait_ge(s_const, 48)
                    act.wait_ge(s_cos_in, 1)
                    nc.scalar.activation(weight[:, :], weight[:, :], ACT.Sin, bias=half_pi[:, :],
                                         scale=-3.141592653589793 / 6.0).then_inc(s_cos, 1)
                    act.sem_inc(s_hid, 2)

                def silu(g, b):
                    if one:
                        act.wait_ge(s_mm1, g + 1)
                        act.wait_ge(s_gate, g + 1)
                        nc.scalar.activation(hid[0:2 * D, b, :], hidp[b][0:2 * D, 0:G // 2 * P], ACT.Silu,
                                             bias=b1[:, :]).then_inc(s_hid, 1)
                if one:
                    act.wait_ge(s_ones, 1)
                silu(0, 0)
                with act.Fori(0, NG // 2) as i:
                    for b in range(2):
                        g = i * 2 + b
                        silu(g + 1, 1 - b)
                        act.wait_ge(s_summed, g + 3)
                        act.wait_ge(s_slot, g + 1)
                        nc.scalar.activation(total[:, b, :, :].rearrange("p j f -> p (j f)"), summed[b][:, 0:G * W],
                                             ACT.Copy).then_inc(s_total, 1)

            @block.gpsimd
            def _(pool):
                pool.iota(spare[:, :], pattern=[[0, G]], base=NP, channel_multiplier=1).then_inc(s_spare, 1)
                pool.sem_inc(s_slot, 2)

                def gather(g, b):
                    wait_alone(pool, s_ring, g + 1, s_passed)
                    wait_alone(pool, s_used if one else s_summed, g + 1, s_passed)
                    for j in range(G):
                        pool.indirect_dma_start(
                            out=got[:, b, j, :], out_offset=None, in_=table,
                            in_offset=bass.IndirectOffsetOnAxis(ap=ring[:, b, 0, j:j + 1].bitcast(U32), axis=0)
                        ).then_inc(s_got[b], 16)
                        if one:
                            pool.indirect_dma_start(
                                out=got_e[:, b, j, :], out_offset=None, in_=e_table,
                                in_offset=bass.IndirectOffsetOnAxis(ap=ring[:, b, 1, j:j + 1].bitcast(U32), axis=0)
                            ).then_inc(s_got[b], 16)

                gather(0, 0)
                gather(1, 1)
                with pool.Fori(0, NG // 2) as i:
                    for b in range(2):
                        g = i * 2 + b
                        wait_alone(pool, s_where, g + 1, s_passed)
                        wait_alone(pool, s_total, g + 3, s_passed)
                        for j in range(G):
                            pool.indirect_dma_start(
                                out=agg[j],
                                out_offset=bass.IndirectOffsetOnAxis(ap=where[:, b, j:j + 1].bitcast(U32), axis=0),
                                in_=total[:, b, j, :], in_offset=None, compute_op=ALU.add).then_inc(s_sc[j], 16)
                        gather(g + 2, b)
                        for j in range(G):
                            pool.wait_ge(s_sc[j], 16 * (g + 1))
                        pool.sem_inc(s_slot, 1)
                for b in range(2):
                    pool.wait_ge(s_got[b], 16 * G * n_gather * (NG // 2 + 1))

            @block.vector
            def _(dve):
                step = in_order(dve, s_prep)
                dve.sem_inc(s_used, 2)
                dve.sem_inc(s_earlier, 1)
                dve.sem_inc(s_summed, 2)
                dve.wait_ge(s_w, 16)
                if one:
                    dve.sem_inc(s_gate, 2)
                    dve.sem_inc(s_gadd, 2)
                    nc.vector.memset(hid[2 * D:2 * D + 1, :, :], 1.0).then_inc(s_ones, 1)
                    step(nc.vector.memset(half_pi[:, :], 3.141592653589793 / 2.0))
                    step(nc.vector.tensor_scalar(keyf[:, :], weight[:, :], 6.0, None, ALU.is_lt))
                    step(nc.vector.tensor_scalar(weight[:, :], weight[:, :], 6.0, None, ALU.min))
                    dve.sem_inc(s_cos_in, 1)
                    dve.wait_ge(s_cos, 1)
                    step(nc.vector.tensor_scalar(weight[:, :], weight[:, :], 1.0, 0.5, ALU.add, ALU.mult))
                    step(nc.vector.tensor_tensor(weight[:, :], weight[:, :], keyf[:, :], ALU.mult))
                else:
                    dve.wait_ge(s_const, 16)
                    step(nc.vector.scalar_tensor_tensor(relation[:, :], keys[:, 0, :], float(NR), relation[:, :],
                                                        ALU.mult, ALU.add))
                step(nc.vector.tensor_copy(keyf[:, :], keys[:, side, 0:T]))

                def fill_ring(g, b):
                    cols = bass.ds(g * G, G)
                    if one:
                        nc.vector.tensor_copy(ring[:, b, 0, :], keys[:, 1, cols])
                        nc.vector.tensor_copy(ring[:, b, 1, :], keys[:, 0, cols]).then_inc(s_ring, 1)
                    else:
                        nc.vector.tensor_copy(ring[:, b, 0, :], relation[:, cols]).then_inc(s_ring, 1)
                fill_ring(0, 0)
                fill_ring(1, 1)
                dve.wait_ge(s_spare, 1)

                with dve.Fori(0, NG // 2) as i:
                    for b in range(2):
                        g = i * 2 + b
                        dve.wait_ge(s_rows[b], 16 * (i + 1))
                        dve.wait_ge(s_summed, g + 1)
                        dve.wait_ge(s_earlier, g * G + 1)
                        for j in range(G):
                            key = keyf[:, bass.ds(g * G + j, 1)]
                            row = rows[:, b, j * P:(j + 1) * P]
                            if one:
                                nc.vector.tensor_scalar(equal[:, b, j, :], row, key, None, ALU.is_equal).then_inc(s_equal, 1)
                            else:
                                nc.vector.tensor_scalar(equal[:, b, j, :], row, key, weight[:, bass.ds(g * G + j, 1)],
                                                        ALU.is_equal, ALU.mult).then_inc(s_equal, 1)
                            nc.vector.scalar_tensor_tensor(earlier[:, j, :], row, key, before[:, 0, 0:P], ALU.is_equal,
                                                           ALU.mult, accum_out=found[:, j:j + 1]).then_inc(s_earlier, 1)
                        dve.wait_ge(s_slot, g + 1)
                        nc.vector.tensor_copy(where[:, b, :], keys[:, side, bass.ds(g * G, G)]).then_inc(s_cp, 1)
                        dve.wait_ge(s_earlier, (g + 1) * G + 1)
                        nc.vector.tensor_scalar(late[:, :], found[:, :], BEFORE, None, ALU.is_ge).then_inc(s_late, 1)
                        dve.wait_ge(s_got[b], 16 * G * n_gather * (i + 1))
                        if one:
                            nc.vector.tensor_tensor(prod[:, :, :], got_e[:, b, :, :], got[:, b, :, D + 1:UW],
                                                    ALU.mult).then_inc(s_prod, 1)
                        dve.wait_ge(s_cp, g + 1)
                        dve.wait_ge(s_late, g + 1)
                        dve.sem_inc(s_rowsfree, 1)
                        nc.vector.copy_predicated(where[:, b, :], late[:, :], spare[:, :]).then_inc(s_where, 1)
                        fill_ring(g + 2, b)
                        if one:
                            dve.wait_ge(s_prod, g + 1)
                            nc.vector.tensor_reduce(logit[:, :], prod[:, :, :], AX.X, ALU.add).then_inc(s_logit, 1)
                            nc.vector.tensor_copy(msg[:, b, :, D:MW], got[:, b, :, D:MW]).then_inc(s_multcol, 1)
                            dve.wait_ge(s_logit, g + 1)
                            dve.wait_ge(s_gate, g + 3)
                            nc.vector.tensor_tensor(gate[:, :, :], gatep[b][:, 0:G * D].rearrange("p (j f) -> p j f", j=G),
                                                    logit[:, :].unsqueeze(2).to_broadcast([P, G, D]),
                                                    ALU.add).then_inc(s_gadd, 1)
                            dve.wait_ge(s_gadd, g + 3)
                            nc.vector.tensor_tensor(gate[:, :, :], gate[:, :, :],
                                                    weight[:, bass.ds(g * G, G)].unsqueeze(2).to_broadcast([P, G, D]),
                                                    ALU.mult).then_inc(s_gcw, 1)
                            dve.wait_ge(s_gcw, g + 1)
                            dve.wait_ge(s_multcol, g + 1)
                            nc.vector.tensor_tensor(msg[:, b, :, 0:D], gate[:, :, :], got[:, b, :, 0:D],
                                                    ALU.mult).then_inc(s_used, 1)
                            dve.wait_ge(s_used, g + 3)


def end_of_layer1(nc, h, sb, agg, x_sb):
    with stage(nc) as (sem, c8):
        cp = sb("cp1", [P, COPIES, NB, MW], F32, c8)
        gamma = sb("gamma", [P, D], F32, c8)
        beta = sb("beta", [P, D], F32, c8)
        y = sb("y8", [P, NB, D], F32, c8)
        sq = sb("sq8", [P, NB, D], F32, c8)
        tot = sb("tot8", [P, NB], F32, c8)
        col = sb("col8", [P, 2, NB], F32, c8)
        s_in8, s_chain8, s_rt8, s_rti8 = sem("s_in8"), sem("s_chain8"), sem("s_rt8"), sem("s_rti8")
        with nc.Block() as block:
            @block.sync
            def _(sp):
                for c in range(COPIES):
                    sp.dma_start(cp[:, c, :, :], agg[c][0:NP, :].rearrange("(b p) f -> p b f", p=P)).then_inc(s_in8, 16)
                sp.dma_start(gamma[:, :], h["gamma"]).then_inc(s_in8, 16)
                sp.dma_start(beta[:, :], h["beta"]).then_inc(s_in8, 16)

            @block.scalar
            def _(act):
                for n in range(2):
                    act.wait_ge(s_rti8, n + 1)
                    nc.scalar.activation(col[:, 1, :], col[:, 1, :], ACT.Sqrt).then_inc(s_rt8, 1)

            @block.vector
            def _(dve):
                step = in_order(dve, s_chain8)
                dve.wait_ge(s_in8, 16 * (COPIES + 2))
                roots = [0]

                def root(var):
                    roots[0] += 1
                    dve.sem_inc(s_rti8, 1)
                    dve.wait_ge(s_rt8, roots[0])
                a = cp[:, 0, :, :]
                step(nc.vector.tensor_tensor(a, a, cp[:, 1, :, :], ALU.add))
                step(nc.vector.tensor_tensor(cp[:, 2, :, :], cp[:, 2, :, :], cp[:, 3, :, :], ALU.add))
                step(nc.vector.tensor_tensor(a, a, cp[:, 2, :, :], ALU.add))
                step(nc.vector.tensor_scalar(tot[:, :], cp[:, 0, :, D:MW].rearrange("p b o -> p (b o)"), 1e-8, None, ALU.max))
                step(nc.vector.reciprocal(tot[:, :], tot[:, :]))
                step(nc.vector.tensor_tensor(y[:, :, :], cp[:, 0, :, 0:D], wide_ap(tot[:, :]), ALU.mult))
                step(nc.vector.tensor_tensor(y[:, :, :], y[:, :, :], x_sb[:, :, :], ALU.add))
                normalize(nc, step, root, y[:, :, :], sq[:, :, :], col, None)
                step(nc.vector.tensor_tensor(y[:, :, :], y[:, :, :], row_ap(gamma[:, :]), ALU.mult))
                step(nc.vector.tensor_tensor(y[:, :, :], y[:, :, :], row_ap(beta[:, :]), ALU.add))
                step(nc.vector.tensor_tensor(x_sb[:, :, :], y[:, :, :], x_sb[:, :, :], ALU.add))
                normalize(nc, step, root, x_sb[:, :, :], sq[:, :, :], col, None)


def table_of_layer2(nc, h, sb, r_table, x_sb, eye, passed_pe):
    Q = NR // 2
    C = 4
    with stage(nc) as (sem, c9):
        xc = sb("xc", [P, C, D], F32, c9)
        xT = sb("xT9", [D, C * P], F32, c9)
        hT = sb("hT9", [2 * D, Q, C * P], F32, c9)
        rows = sb("rows9", [P, C, NR * D], F32, c9)
        w1 = sb("w1_9", [D, Q, 2 * D], F32, c9)
        w2 = sb("w2_9", [2 * D, Q, 2 * D], F32, c9)
        b1 = sb("b1_9", [2 * D, 1], F32, c9)
        turned = c9.enter_context(nc.psum_tensor("turned9", [P, 512], F32))
        hp = [c9.enter_context(nc.psum_tensor(f"hp9_{q}", [P, 512], F32)) for q in range(2)]
        rp = [c9.enter_context(nc.psum_tensor(f"rp9_{c}", [P, 512], F32)) for c in range(C)]
        s_c9, s_xc, s_turn9, s_xT, s_hp, s_hT, s_rp, s_rows9, s_stored = (
            sem("s_c9"), sem("s_xc"), sem("s_turn9"), sem("s_xT"), sem("s_hp"), sem("s_hT"), sem("s_rp"),
            sem("s_rows9"), sem("s_stored9"))

        def chunks(eng, body):
            with eng.Fori(0, NB // C) as i:
                body(i, i * C, C)
            body(NB // C, NB - 1, 1)

        with nc.Block() as block:
            @block.sync
            def _(sp):
                sp.dma_start(w1[:, :, :], h["l2_w1"]).then_inc(s_c9, 16)
                sp.dma_start(w2[:, :, :], h["l2_w2"]).then_inc(s_c9, 16)
                sp.dma_start(b1[:, :], h["l2_b1"]).then_inc(s_c9, 16)

                def body(i, b0, n):
                    sp.wait_ge(s_rows9, i + 1)
                    sp.sem_inc(s_c9, 1)
                    dst = r_table.rearrange("(b p r) f -> p b (r f)", p=P, r=NR)[:, bass.ds(b0, n), :]
                    sp.dma_start(dst, rows[:, 0:n, :]).then_inc(s_stored, 16)
                chunks(sp, body)
                sp.wait_ge(s_stored, 16 * (NB // C + 2))

            @block.tensor
            def _(pe):
                pe.wait_ge(s_c9, 48)

                def body(i, b0, n):
                    wait_alone(pe, s_xc, i + 1, passed_pe)
                    for c in range(n):
                        tr = nc.tensor.transpose(turned[0:D, c * P:(c + 1) * P], xc[:, c, :], eye[:, :])
                    tr.then_inc(s_turn9, 1)
                    pe.wait_ge(s_xT, i + 1)
                    for q in range(Q):
                        pe.wait_ge(s_hT, i * Q + q + 1)
                        nc.tensor.matmul(hp[q % 2][0:2 * D, 0:n * P], w1[:, q, :], xT[:, 0:n * P],
                                         start=True, stop=True).then_inc(s_hp, 1)
                    pe.wait_ge(s_hT, (i + 1) * Q + 2)
                    for c in range(n):
                        for q in range(Q):
                            mm = nc.tensor.matmul(rp[c][:, q * 2 * D:(q + 1) * 2 * D], hT[:, q, c * P:(c + 1) * P],
                                                  w2[:, q, :], start=True, stop=True)
                    mm.then_inc(s_rp, 1)
                chunks(pe, body)

            @block.scalar
            def _(act):
                act.sem_inc(s_hT, 2)
                act.wait_ge(s_c9, 48)

                def body(i, b0, n):
                    for q in range(Q):
                        act.wait_ge(s_hp, i * Q + q + 1)
                        nc.scalar.activation(hT[:, q, 0:n * P], hp[q % 2][0:2 * D, 0:n * P], ACT.Relu,
                                             bias=b1[:, :]).then_inc(s_hT, 1)
                chunks(act, body)

            @block.vector
            def _(dve):
                dve.sem_inc(s_stored, 16)

                def body(i, b0, n):
                    nc.vector.tensor_copy(xc[:, 0:n, :], x_sb[:, bass.ds(b0, n), :]).then_inc(s_xc, 1)
                    dve.wait_ge(s_turn9, i + 1)
                    nc.vector.tensor_copy(xT[:, 0:n * P], turned[0:D, 0:n * P]).then_inc(s_xT, 1)
                    dve.wait_ge(s_rp, i + 1)
                    dve.wait_ge(s_stored, 16 * (i + 1))
                    for c in range(n):
                        cpy = nc.vector.tensor_copy(rows[:, c, :], rp[c][:, 0:NR * D])
                    cpy.then_inc(s_rows9, 1)
                chunks(dve, body)


def end_of_layer2(nc, h, sb, agg, x_sb):
    with stage(nc) as (sem, c8):
        cp = sb("cp2", [P, COPIES, NB, D], F32, c8)
        bias = sb("bias10", [P, D], F32, c8)
        sq = sb("sq10", [P, NB, D], F32, c8)
        col = sb("col10", [P, 2, NB], F32, c8)
        s_in10, s_chain10, s_rt10, s_rti10 = sem("s_in10"), sem("s_chain10"), sem("s_rt10"), sem("s_rti10")
        with nc.Block() as block:
            @block.sync
            def _(sp):
                for c in range(COPIES):
                    sp.dma_start(cp[:, c, :, :], agg[c][0:NP, :].rearrange("(b p) f -> p b f", p=P)).then_inc(s_in10, 16)
                sp.dma_start(bias[:, :], h["l2_b2"]).then_inc(s_in10, 16)

            @block.scalar
            def _(act):
                act.wait_ge(s_rti10, 1)
                nc.scalar.activation(col[:, 1, :], col[:, 1, :], ACT.Sqrt).then_inc(s_rt10, 1)

            @block.vector
            def _(dve):
                step = in_order(dve, s_chain10)
                dve.wait_ge(s_in10, 16 * (COPIES + 1))

                def root(var):
                    dve.sem_inc(s_rti10, 1)
                    dve.wait_ge(s_rt10, 1)
                a = cp[:, 0, :, :]
                step(nc.vector.tensor_tensor(a, a, cp[:, 1, :, :], ALU.add))
                step(nc.vector.tensor_tensor(cp[:, 2, :, :], cp[:, 2, :, :], cp[:, 3, :, :], ALU.add))
                step(nc.vector.tensor_tensor(a, a, cp[:, 2, :, :], ALU.add))
                step(nc.vector.tensor_tensor(a, a, row_ap(bias[:, :]), ALU.add))
                step(nc.vector.scalar_tensor_tensor(x_sb[:, :, :], a, 0.0, x_sb[:, :, :], ALU.max, ALU.add))
                normalize(nc, step, root, x_sb[:, :, :], sq[:, :, :], col, None)


def layer3(nc, h, sb, strips8, x_sb, outdeg, eye, passed):
    U = 7
    W3 = 3 * D
    passed_sp, passed_act, passed_dve, passed_pe, passed_pool = passed
    with stage(nc) as (sem, c11):
        ci = sb("ci", [P, NB], F32, c11)
        v = sb("v11", [P, NB, D], F32, c11)
        r = sb("r11", [P, NB, D], F32, c11)
        parts = sb("parts11", [P, NB, W3 + 1], BF16, c11)
        cbuf = sb("cbuf11", [P, U, NP], FP8, c11)
        agg = sb("agg11", [P, NB, D], F32, c11)
        deg = sb("deg11", [P, NB], F32, c11)
        cj = sb("cj11", [P, NB], F32, c11)
        acc = [c11.enter_context(nc.psum_tensor(f"acc11_{u}", [P, 512], F32)) for u in range(U)]
        s_c = [sem(f"s_c11_{u}") for u in range(U)]
        s_strip, s_accfree, s_chain, s_parts, s_sum, s_deg = (
            sem("s_strip11"), sem("s_accfree11"), sem("s_chain11"), sem("s_parts11"), sem("s_sum11"), sem("s_deg11"))
        s_rt, s_rti = sem("s_rt11"), sem("s_rti11")
        with nc.Block() as block:
            @block.sync
            def _(sp):
                def load(rr, u, first):
                    if not first:
                        wait_alone(sp, s_strip, rr * U + u - U + 1, passed_sp)
                    sp.dma_start(cbuf[:, u, :].bitcast(U8), strips8[bass.ds(rr * U + u, 1), :, :].rearrange("o p c -> p (o c)")
                                 ).then_inc(s_c[u], 16)
                for u in range(U):
                    load(0, u, True)
                with sp.Fori(1, NB // U) as rr:
                    for u in range(U):
                        load(rr, u, False)

            @block.tensor
            def _(pe):
                pe.wait_ge(s_parts, 1)
                with pe.Fori(0, NB // U) as rr:
                    for u in range(U):
                        n = rr * U + u
                        wait_alone(pe, s_c[u], 16 * (rr + 1), passed_pe)
                        wait_alone(pe, s_accfree, n + 1, passed_pe)
                        for s in range(NB):
                            mm = nc.tensor.matmul(acc[u][:, 0:W3 + 1], cbuf[:, u, s * P:(s + 1) * P], parts[:, s, :],
                                                  start=(s == 0), stop=(s == NB - 1))
                        mm.then_inc(s_strip, 1)

            @block.scalar
            def _(act):
                act.wait_ge(s_rti, 1)
                nc.scalar.activation(ci[:, :], ci[:, :], ACT.Sqrt).then_inc(s_rt, 1)
                act.wait_ge(s_rti, 2)
                nc.scalar.activation(cj[:, :], cj[:, :], ACT.Sqrt).then_inc(s_rt, 1)

            @block.vector
            def _(dve):
                step = in_order(dve, s_chain)
                step(nc.vector.tensor_scalar(ci[:, :], outdeg[:, :], 1.0, None, ALU.max))
                dve.sem_inc(s_rti, 1)
                dve.wait_ge(s_rt, 1)
                step(nc.vector.reciprocal(ci[:, :], ci[:, :]))
                step(nc.vector.tensor_tensor(v[:, :, :], x_sb[:, :, :], wide_ap(ci[:, :]), ALU.mult))
                step(nc.vector.tensor_copy(parts[:, :, 0:D], v[:, :, :]))
                step(nc.vector.tensor_tensor(r[:, :, :], v[:, :, :], parts[:, :, 0:D], ALU.subtract))
                step(nc.vector.tensor_copy(parts[:, :, D:2 * D], r[:, :, :]))
                step(nc.vector.tensor_tensor(parts[:, :, 2 * D:W3], r[:, :, :], parts[:, :, D:2 * D], ALU.subtract))
                step(nc.vector.memset(parts[:, :, W3:W3 + 1], 1.0))
                dve.sem_inc(s_parts, 1)
                dve.sem_inc(s_accfree, U)
                with dve.Fori(0, NB // U) as rr:
                    for u in range(U):
                        n = rr * U + u
                        dve.wait_ge(s_strip, n + 1)
                        nc.vector.tensor_reduce(agg[:, bass.ds(n, 1), :].rearrange("p o f -> p (o f)"),
                                                acc[u][:, 0:W3].rearrange("p (s f) -> p f s", f=D),
                                                AX.X, ALU.add).then_inc(s_sum, 1)
                        nc.vector.tensor_copy(deg[:, bass.ds(n, 1)], acc[u][:, W3:W3 + 1]).then_inc(s_deg, 1)
                        dve.wait_ge(s_sum, n + 1)
                        dve.wait_ge(s_deg, n + 1)
                        dve.sem_inc(s_accfree, 1)
                step(nc.vector.tensor_scalar(cj[:, :], deg[:, :], 1.0, None, ALU.max))
                dve.sem_inc(s_rti, 1)
                dve.wait_ge(s_rt, 2)
                step(nc.vector.reciprocal(cj[:, :], cj[:, :]))
                step(nc.vector.tensor_tensor(agg[:, :, :], agg[:, :, :], wide_ap(cj[:, :]), ALU.mult))
                step(nc.vector.tensor_scalar(deg[:, :], deg[:, :], 0.0, None, ALU.is_gt))
                step(nc.vector.tensor_scalar(cj[:, :], deg[:, :], -1.0, 1.0, ALU.mult, ALU.add))
                step(nc.vector.tensor_tensor(agg[:, :, :], agg[:, :, :], wide_ap(deg[:, :]), ALU.mult))
                step(nc.vector.tensor_tensor(v[:, :, :], x_sb[:, :, :], wide_ap(cj[:, :]), ALU.mult))
                step(nc.vector.tensor_tensor(agg[:, :, :], agg[:, :, :], v[:, :, :], ALU.add))

        hc = sb("hc", [P, 2, D], F32, c11)
        hT = sb("hT11", [D, 2, P], F32, c11)
        wt = sb("wt11", [D, D], F32, c11)
        b3 = sb("b3", [P, D], F32, c11)
        col = sb("col11", [P, 2, NB], F32, c11)
        s_w, s_hc, s_tn, s_hT, s_mm, s_o = (
            sem("s_w11"), sem("s_hc11"), sem("s_tn11"), sem("s_hT11"), sem("s_mm11"), sem("s_o11"))
        s_chainb, s_rtb, s_rtib = sem("s_chain11b"), sem("s_rt11b"), sem("s_rti11b")

        def blocks(eng, body):
            with eng.Fori(0, NB // 2) as i:
                for u in range(2):
                    body(i * 2 + u, u)
            body(NB - 1, 0)
        with nc.Block() as block:
            @block.sync
            def _(sp):
                sp.dma_start(wt[:, :], h["l3_w"]).then_inc(s_w, 16)
                sp.dma_start(b3[:, :], h["l3_b"]).then_inc(s_w, 16)

            @block.tensor
            def _(pe):
                pe.wait_ge(s_w, 32)

                def body(b, u):
                    wait_alone(pe, s_hc, b + 1, passed_pe)
                    nc.tensor.transpose(acc[u][0:D, 0:P], hc[:, u, :], eye[:, :]).then_inc(s_tn, 1)
                    pe.wait_ge(s_hT, b + 1)
                    nc.tensor.matmul(acc[2 + u][:, 0:D], hT[:, u, :], wt[:, :], start=True, stop=True).then_inc(s_mm, 1)
                blocks(pe, body)

            @block.scalar
            def _(act):
                def body(b, u):
                    act.wait_ge(s_tn, b + 1)
                    nc.scalar.activation(hT[:, u, :], acc[u][0:D, 0:P], ACT.Copy).then_inc(s_hT, 1)
                blocks(act, body)
                act.wait_ge(s_rtib, 1)
                nc.scalar.activation(col[:, 1, :], col[:, 1, :], ACT.Sqrt).then_inc(s_rtb, 1)

            @block.vector
            def _(dve):
                dve.wait_ge(s_w, 32)

                def body(b, u):
                    nc.vector.tensor_copy(hc[:, u, :], agg[:, bass.ds(b, 1), :].rearrange("p o f -> p (o f)")).then_inc(s_hc, 1)
                    dve.wait_ge(s_mm, b + 1)
                    nc.vector.tensor_tensor(v[:, bass.ds(b, 1), :].rearrange("p o f -> p (o f)"), acc[2 + u][:, 0:D],
                                            b3[:, :], ALU.add).then_inc(s_o, 1)
                blocks(dve, body)
                dve.wait_ge(s_o, NB)
                step = in_order(dve, s_chainb)
                step(nc.vector.scalar_tensor_tensor(x_sb[:, :, :], v[:, :, :], 0.0, x_sb[:, :, :], ALU.max, ALU.add))

                def root(var):
                    dve.sem_inc(s_rtib, 1)
                    dve.wait_ge(s_rtb, 1)
                normalize(nc, step, root, x_sb[:, :, :], r[:, :, :], col, None)


def kernel(**inputs):
    import numpy as np
    import concourse.bacc as bacc
    from concourse.bass_utils import run_bass_kernel_spmd

    a = {k: np.asarray(v) for k, v in inputs.items()}

    def pad(v, rows, fill=0):
        w = np.full((rows,) + v.shape[1:], fill, v.dtype)
        w[:len(v)] = v
        return w

    def by_node(v, w):
        return pad(v.reshape(N, w), NP).reshape(NB, P, w).transpose(1, 0, 2)

    def by_edge(v, fill=0):
        return pad(v.reshape(E), P * T, fill).reshape(P, T)

    def every(v):
        return np.broadcast_to(v.reshape(1, -1), (P, v.size))

    def two2(m, o):
        w = np.zeros((2, m.shape[0], 2, m.shape[1]), m.dtype)
        w[0, :, 0], w[1, :, 1] = m, o
        return w.reshape(2 * m.shape[0], 2 * m.shape[1])

    def two(m):
        return two2(m, m)

    i, w = np.arange(P * T - E, dtype=np.int32), NP - N
    src = np.concatenate([a["src"], N + i % w]).reshape(P, T)
    dst = np.concatenate([a["dst"], N + i // w % w]).reshape(P, T)
    keys = np.stack([src, dst], 1)
    more = np.zeros((P, 2 * G), np.int32)
    attr = pad(a["edge_attr_40"], P * T).reshape(P, NG, G // 2, 2, R).transpose(1, 3, 4, 2, 0)
    arrays = {
        "x": by_node(a["x"], D),
        "key_cols": np.concatenate([keys, np.zeros((P, 2, 2 * G), np.int32)], 2),
        "key_rows": keys.reshape(P, 2, NG, G).transpose(2, 1, 3, 0).reshape(NG, 2 * G * P),
        "w0": a["L0_gnn_weights"].reshape(K // 2, 2 * D, D).transpose(1, 0, 2),
        "b0": every(a["L0_gnn_bias"]),
        "emb": a["L1_gnn_emb"],
        "embT": a["L1_gnn_emb"].T,
        "adaptT": a["L1_gnn_adaptW"].T,
        "kind": by_node(a["node_type_119"], 1)[:, :, 0],
        "mult": by_node(a["node_vec"], 1)[:, :, 0],
        "distance": by_edge(a["edge_weight"]),
        "weight": by_edge(a["edge_weight1"]),
        "relation": np.concatenate([by_edge(a["edge_type_8"]), more], 1),
        "attr": pad(attr.reshape(NG, 2 * R, G // 2 * P), NG + 1),
        "l1_w1": two(a["L1_gnn_W1"].T),
        "l1_b1": np.tile(a["L1_gnn_b1"], 2).reshape(-1, 1),
        "l1_w2": np.concatenate([two(a["L1_gnn_W2"].T), np.tile(a["L1_gnn_b2"], 2).reshape(1, -1)]),
        "gamma": every(a["L1_gnn_gamma"]),
        "beta": every(a["L1_gnn_beta"]),
        "l2_w1": a["L2_gnn_weight1"].reshape(NR // 2, 2, D, D).transpose(2, 0, 1, 3).reshape(D, NR // 2, 2 * D),
        "l2_b1": np.tile(a["L2_gnn_bias1"], 2).reshape(-1, 1),
        "l2_w2": np.stack([two2(a["L2_gnn_weight2"][2 * q], a["L2_gnn_weight2"][2 * q + 1]) for q in range(NR // 2)], 1),
        "l2_b2": every(a["L2_gnn_bias2"]),
        "l3_w": a["L3_gnn_W"].T,
        "l3_b": every(a["L3_gnn_b"]),
    }
    nc = bacc.Bacc("TRN2", target_bir_lowering=False, num_devices=1)
    arrays = {f"in_{k}": np.ascontiguousarray(v) for k, v in arrays.items()}
    h = {k[3:]: nc.dram_tensor(k, v.shape, mybir.dt.from_np(v.dtype), kind="ExternalInput").ap()
         for k, v in arrays.items()}
    out = nc.dram_tensor("out", (P, NB, D), F32, kind="ExternalOutput").ap()
    gnn_kernel(nc, h, out)
    r = run_bass_kernel_spmd(nc, [arrays], core_ids=[0])
    return r.results[0]["out"].transpose(1, 0, 2).reshape(NP, D)[:N]
```

```python
import concourse.bass as bass
from concourse import mybir
from concourse.alu_op_type import AluOpType as ALU
from contextlib import ExitStack, contextmanager

F32 = mybir.dt.float32
BF16 = mybir.dt.bfloat16
FP8 = mybir.dt.float8e4
I32 = mybir.dt.int32
U8 = mybir.dt.uint8
U32 = mybir.dt.uint32
ACT = mybir.ActivationFunctionType
AX = mybir.AxisListType

P = 128
N = 6250
D = 48
NB = -(-N // P)
NP = NB * P
E = 206250
G = 4
NG = 404
T = G * NG
K = 16
R = 40
Z, EM = 119, 32
NR = 8
ROW = 64 * P
STRIP = P * ROW
SLOTS = G * P
NGS = 452
AHEAD = 4
R1 = R + 3
TWO = R1 + R
R2 = 3
BLANK = -1.0
UW = D + 1 + EM
MW = D + 1
BEFORE = 1024.0
MANY = 16.0
assert NGS >= (P * T + NB * (SLOTS - 1)) // SLOTS and NGS % 4 == 0
PI = 3.141592653589793


@contextmanager
def stage(nc, label):
    held = []

    def sem(name):
        held.append(nc.alloc_semaphore(name=f"{label}_{name}"))
        return held[-1]
    with ExitStack() as memory:
        yield sem, memory
    nc.clear_and_free_semaphores(held)
    nc.all_engine_barrier()


def wait_alone(eng, semaphore, value, passed):
    eng.wait_ge(semaphore, value)
    eng.sem_inc(passed, 1)


def sort_places(nc, dve, step, srt, key, block_no, group_no, sums, place, block_of, first_of,
                s_counted, s_count, s_hit, s_run, s_pos, s_end, passed):
    c = srt
    full = lambda t: t[:, :]
    step(nc.vector.tensor_scalar(full(c["shifted"]), key, 7, None, ALU.logical_shift_right))
    step(nc.vector.tensor_copy(full(c["block"]), full(c["shifted"])))
    dve.sem_inc(s_counted, 1)
    with dve.Fori(0, NB) as b:
        dve.wait_ge(s_counted, b + 1)
        nc.vector.tensor_scalar(full(c["hit"]), full(c["block"]), block_no[:, bass.ds(b, 1)], None, ALU.is_equal,
                                ALU.add, accum_out=c["count"][:, bass.ds(b, 1)]).then_inc(s_counted, 1)
    dve.wait_ge(s_count, 2)
    step(nc.vector.tensor_copy(full(c["total"]), sums[:, 64:64 + NB]))
    step(nc.vector.tensor_scalar(full(c["groups_i"]), full(c["total"]), float(SLOTS - 1), None, ALU.add))
    step(nc.vector.tensor_scalar(full(c["groups_i"]), full(c["groups_i"]), 9, None, ALU.logical_shift_right))
    step(nc.vector.tensor_copy(full(c["groups"]), full(c["groups_i"])))
    step(nc.vector.memset(full(c["total"]), 1.0))
    step(nc.vector.tensor_tensor_scan(full(c["end"]), full(c["total"]), full(c["groups"]), 0.0, ALU.mult, ALU.add))
    step(nc.vector.tensor_tensor(full(c["base"]), full(c["end"]), full(c["groups"]), ALU.subtract))
    step(nc.vector.tensor_scalar(full(c["base"]), full(c["base"]), float(SLOTS), -1.0, ALU.mult, ALU.add))
    step(nc.vector.tensor_tensor(full(c["base"]), full(c["base"]), sums[:, 0:NB], ALU.add))
    step(nc.vector.memset(full(c["blk"]), 0.0))
    dve.sem_inc(s_end, 1)
    with dve.Fori(0, NB) as b:
        dve.wait_ge(s_end, b + 1)
        nc.vector.scalar_tensor_tensor(full(c["blk"]), full(group_no), c["end"][:, bass.ds(b, 1)], full(c["blk"]),
                                       ALU.is_ge, ALU.add).then_inc(s_end, 1)
    dve.wait_ge(s_end, NB + 1)
    step(nc.vector.tensor_scalar(full(c["blk"]), full(c["blk"]), float(NB - 1), None, ALU.min))
    step(nc.vector.tensor_copy(full(block_of), full(c["blk"])))
    step(nc.vector.tensor_scalar(full(first_of), full(c["blk"]), float(P), None, ALU.mult))
    step(nc.vector.memset(full(c["run"]), 1.0))
    dve.sem_inc(s_pos, 1)
    with dve.Fori(0, NB) as b:
        dve.wait_ge(s_pos, b + 1)
        nc.vector.tensor_scalar(full(c["hit"]), full(c["block"]), block_no[:, bass.ds(b, 1)], None,
                                ALU.is_equal).then_inc(s_hit, 1)
        dve.wait_ge(s_hit, b + 1)
        nc.vector.tensor_tensor_scan(full(c["run"]), full(c["hit"]), full(c["hit"]), c["base"][:, bass.ds(b, 1)],
                                     ALU.add, ALU.bypass).then_inc(s_run, 1)
        wait_alone(dve, s_run, b + 1, passed)
        nc.vector.copy_predicated(full(c["pos"]), full(c["hit"]), full(c["run"])).then_inc(s_pos, 1)
    dve.wait_ge(s_pos, NB + 1)
    step(nc.vector.tensor_copy(full(place), full(c["pos"])))


def gnn_kernel(nc, h, out):
    dram = lambda name, shape, dt: nc.dram_tensor(name, shape, dt).ap()
    counts = dram("counts", ((NB + 1) * STRIP, 1), F32)
    strips8 = dram("strips8", (NB, P, NB * P), U8)
    cheb = dram("cheb", (P, NB, K, D), F32)
    z_table = dram("z_table", (Z, 2 * EM), F32)
    u_table = dram("u_table", (NP, UW), F32)
    r_table = dram("r_table", (NP * NR, D), F32)
    sorted1 = dram("sorted1", ((NGS + AHEAD) * SLOTS, R1), F32)
    sorted2 = dram("sorted2", ((NGS + AHEAD) * SLOTS, R2), F32)

    def strip32(j):
        return counts[bass.ds(j * STRIP, STRIP), :].rearrange("(p c) o -> p (c o)", p=P)[:, 0:NP]

    ctx = ExitStack()
    with ctx:
        def keep_sem(name):
            return ctx.enter_context(nc.semaphore(name))

        def sb(name, shape, dt, c=ctx):
            return c.enter_context(nc.sbuf_tensor(name, shape, dt))

        passed_sp, passed_act, passed_dve, passed_pe, passed_pool = passed = [
            keep_sem(f"passed_{e}") for e in ("sp", "act", "dve", "pe", "pool")]

        keys = sb("keys", [P, 2, T], I32)
        r_row = sb("r_row", [P, T], F32)
        weight = sb("weight", [P, T], F32)
        cutoff = sb("cutoff", [P, T], F32)
        place = [sb(f"place{n}", [P, T], I32) for n in (1, 2)]
        block_of = [sb(f"block_of{n}", [P, NGS + AHEAD], I32) for n in (1, 2)]
        first_of = [sb(f"first_of{n}", [P, NGS + AHEAD], F32) for n in (1, 2)]
        e_parts = sb("e_parts", [P, NB, 3 * EM], BF16)
        x_sb = sb("x_sb", [P, NB, D], F32)
        outdeg = sb("outdeg", [P, NB], F32)
        many = sb("many", [1, 1], I32)
        before = sb("before", [P, G, G * P], F32)
        ones_w = sb("ones_w", [P, G * P], F32)
        eye = sb("eye", [P, P], F32)

        with stage(nc, "clear") as (sem, c1):
            zeros = sb("zeros", [P, NP], F32, c1)
            fill1 = sb("fill1", [P, 96, R1], F32, c1)
            fill2 = sb("fill2", [P, (NGS + AHEAD) * G, R2], F32, c1)
            half_pi = sb("half_pi", [P, 1], F32, c1)
            below = sb("below", [P, T], F32, c1)
            s_keys, s_xin, s_edge = sem("s_keys"), sem("s_xin"), sem("s_edge")
            s_zero, s_fill, s_clear, s_ones, s_eye0 = (
                sem("s_zero"), sem("s_fill"), sem("s_clear"), sem("s_ones"), sem("s_eye0"))
            s_masks, s_cos_in, s_cos, s_chain1 = sem("s_masks"), sem("s_cos_in"), sem("s_cos"), sem("s_chain1")
            lower = sb("lower", [P, P], F32, c1)
            ones = sb("ones", [P, P], F32, c1)
            block_no = sb("block_no", [P, NB], F32, c1)
            group_no = sb("group_no", [P, NGS + AHEAD], F32, c1)
            sums = c1.enter_context(nc.psum_tensor("sums", [P, 512], F32))
            srt = dict(
                block=sb("srt_block", [P, T], BF16, c1), hit=sb("srt_hit", [P, T], mybir.dt.int16, c1),
                run=sb("srt_run", [P, T], F32, c1), pos=sb("srt_pos", [P, T], F32, c1),
                shifted=sb("srt_shifted", [P, T], I32, c1),
                count=sb("srt_count", [P, NB], F32, c1), total=sb("srt_total", [P, NB], F32, c1),
                groups_i=sb("srt_groups_i", [P, NB], I32, c1), groups=sb("srt_groups", [P, NB], F32, c1),
                end=sb("srt_end", [P, NB], F32, c1), base=sb("srt_base", [P, NB], F32, c1),
                blk=sb("srt_blk", [P, NGS + AHEAD], F32, c1))
            s_counted = [sem("s_counted1"), sem("s_counted2")]
            s_count = [sem("s_count1"), sem("s_count2")]
            s_hit = [sem("s_hit1"), sem("s_hit2")]
            s_run = [sem("s_run1"), sem("s_run2")]
            s_pos = [sem("s_pos1"), sem("s_pos2")]
            s_end = [sem("s_end1"), sem("s_end2")]
            s_iota = sem("s_iota")
            with nc.Block() as block:
                @block.sync
                def _(sp):
                    sp.dma_start(keys[:, :, :], h["key_cols"]).then_inc(s_keys, 16)
                    sp.dma_start(x_sb[:, :, :], h["x"]).then_inc(s_xin, 16)
                    sp.dma_start(cutoff[:, :], h["distance"]).then_inc(s_edge, 16)
                    sp.dma_start(weight[:, :], h["weight"]).then_inc(s_edge, 16)
                    sp.dma_start(place[0][:, :], h["relation"]).then_inc(s_edge, 16)
                    sp.wait_ge(s_zero, 1)
                    with sp.Fori(0, NB) as j:
                        sp.dma_start(strip32(j), zeros[:, :]).then_inc(s_clear, 16)
                    sp.dma_start(counts[NB * STRIP:NB * STRIP + G * P, :].rearrange("(p c) o -> p (c o)", p=P),
                                 zeros[:, 0:G]).then_inc(s_clear, 16)
                    sp.wait_ge(s_fill, 4)
                    n = (NGS + AHEAD) * G // 96
                    with sp.Fori(0, n) as j:
                        sp.dma_start(sorted1.rearrange("(p r) f -> p (r f)", p=P)[:, bass.ds(j * (96 * R1), 96 * R1)],
                                     fill1[:, :, :].rearrange("p r f -> p (r f)")).then_inc(s_clear, 16)
                    sp.dma_start(sorted2.rearrange("(p r) f -> p (r f)", p=P),
                                 fill2[:, :, :].rearrange("p r f -> p (r f)")).then_inc(s_clear, 16)
                    sp.wait_ge(s_keys, 16)
                    sp.wait_ge(s_xin, 16)
                    sp.wait_ge(s_clear, 16 * (NB + 1 + n + 1))

                @block.gpsimd
                def _(pool):
                    pool.memset(ones_w[:, :], 1.0).then_inc(s_ones, 1)
                    pool.memset(ones[:, :], 1.0).then_inc(s_ones, 1)
                    pool.memset(eye[:, :], 0.0).then_inc(s_eye0, 1)
                    pool.iota(block_no[:, :], pattern=[[1, NB]], base=0, channel_multiplier=0,
                              allow_small_or_imprecise_dtypes=True).then_inc(s_iota, 1)
                    pool.iota(group_no[:, :], pattern=[[1, NGS + AHEAD]], base=0, channel_multiplier=0,
                              allow_small_or_imprecise_dtypes=True).then_inc(s_iota, 1)
                    pool.wait_ge(s_ones, 2)
                    pool.affine_select(out=lower[:, :], in_=ones[:, :], compare_op=ALU.is_gt, fill=0.0, base=0,
                                       pattern=[[1, P]], channel_multiplier=-1).then_inc(s_iota, 1)
                    for j in range(G):
                        pool.affine_select(out=before[:, j, :], in_=ones_w[:, :], compare_op=ALU.is_ge,
                                           fill=BEFORE, base=-P * j, pattern=[[1, G * P]],
                                           channel_multiplier=-1).then_inc(s_masks, 1)
                    pool.wait_ge(s_eye0, 1)
                    pool.affine_select(out=eye[:, :], in_=eye[:, :], compare_op=ALU.not_equal, fill=1.0,
                                       base=0, pattern=[[-1, P]], channel_multiplier=1).then_inc(s_masks, 1)

                @block.scalar
                def _(act):
                    act.wait_ge(s_cos_in, 1)
                    nc.scalar.activation(cutoff[:, :], cutoff[:, :], ACT.Sin, bias=half_pi[:, :],
                                         scale=-PI / 6.0).then_inc(s_cos, 1)

                @block.tensor
                def _(pe):
                    pe.wait_ge(s_iota, 3)
                    for n in range(2):
                        pe.wait_ge(s_counted[n], NB + 1)
                        nc.tensor.matmul(sums[:, 0:NB], lower[:, :], srt["count"][:, :], start=True, stop=True
                                         ).then_inc(s_count[n], 1)
                        nc.tensor.matmul(sums[:, 64:64 + NB], ones[:, :], srt["count"][:, :], start=True, stop=True
                                         ).then_inc(s_count[n], 1)

                @block.vector
                def _(dve):
                    nc.vector.memset(zeros[:, :], 0.0).then_inc(s_zero, 1)
                    nc.vector.memset(fill1[:, :, :], 0.0).then_inc(s_fill, 1)
                    nc.vector.memset(fill2[:, :, :], 0.0).then_inc(s_fill, 1)
                    dve.wait_ge(s_fill, 2)
                    nc.vector.memset(fill1[:, :, R1 - 1:R1], BLANK).then_inc(s_fill, 1)
                    nc.vector.memset(fill2[:, :, R2 - 1:R2], BLANK).then_inc(s_fill, 1)
                    step = in_order(dve, s_chain1)
                    dve.wait_ge(s_edge, 48)
                    dve.wait_ge(s_keys, 16)
                    step(nc.vector.memset(half_pi[:, :], PI / 2.0))
                    step(nc.vector.tensor_scalar(below[:, :], cutoff[:, :], 6.0, None, ALU.is_lt))
                    step(nc.vector.tensor_scalar(cutoff[:, :], cutoff[:, :], 6.0, None, ALU.min))
                    dve.sem_inc(s_cos_in, 1)
                    step(nc.vector.scalar_tensor_tensor(r_row[:, :], keys[:, 0, :], float(NR), place[0][:, :],
                                                        ALU.mult, ALU.add))
                    dve.wait_ge(s_cos, 1)
                    step(nc.vector.tensor_scalar(cutoff[:, :], cutoff[:, :], 1.0, 0.5, ALU.add, ALU.mult))
                    step(nc.vector.tensor_tensor(cutoff[:, :], cutoff[:, :], below[:, :], ALU.mult))
                    dve.wait_ge(s_iota, 3)
                    for n in range(2):
                        sort_places(nc, dve, step, srt, keys[:, n, :], block_no, group_no, sums, place[n], block_of[n],
                                    first_of[n], s_counted[n], s_count[n], s_hit[n], s_run[n], s_pos[n], s_end[n], passed_dve)

        with stage(nc, "count") as (sem, c2):
            keyf = sb("keyf", [P, 2, T], F32, c2)
            cell = sb("cell", [P, T], I32, c2)
            cell_t = sb("cell_t", [P, T], I32, c2)
            rows = sb("rows", [P, 2, 2, G * P], I32, c2)
            eq_dst = sb("eq_dst", [P, G, G * P], F32, c2)
            found = sb("found", [P, 2, G], F32, c2)
            late = sb("late", [P, 2, G], I32, c2)
            where = sb("where", [P, 2, G], I32, c2)
            spare = sb("spare", [P, G], I32, c2)
            s_prep, s_spare = sem("s_prep"), sem("s_spare")
            s_rows = [sem("s_rows0"), sem("s_rows1")]
            s_rowfree = sem("s_rowfree")
            s_eqd, s_eqs, s_late, s_cellcp, s_where, s_added = (
                sem("s_eqd"), sem("s_eqs"), sem("s_late"), sem("s_cellcp"), sem("s_where"), sem("s_added"))
            s_slot = sem("s_slot")
            pack2 = RecordsOfLayer2(nc, sb, c2, 'a', sem, keys, r_row, weight, place[1], sorted2)
            with nc.Block() as block:
                @block.scalar
                def _(act):
                    for b in range(2):
                        pack2.pack(act, 0, b, b, True)
                    with act.Fori(1, NG // 2) as i:
                        for b in range(2):
                            pack2.pack(act, i, i * 2 + b, b, False)

                @block.sync
                def _(sp):
                    def load(g, b):
                        wait_alone(sp, s_rowfree, g + 1, passed_sp)
                        src = h["key_rows"][bass.ds(g, 1), :].rearrange("o (k c) -> o k c", k=2)
                        sp.dma_start(rows[:, b, :, :], src.to_broadcast([P, 2, G * P])).then_inc(s_rows[b], 16)
                    with sp.Fori(0, NG // 2) as i:
                        for b in range(2):
                            load(i * 2 + b, b)

                @block.vector
                def _(dve):
                    dve.sem_inc(s_rowfree, 2)
                    n = 0
                    src, dst = keys[:, 0, 0:T], keys[:, 1, 0:T]
                    nc.vector.tensor_copy(keyf[:, :, :], keys[:, :, 0:T]).then_inc(s_prep, 1)
                    blocks = (P - 1) * P * 0 + 0x1F80
                    nc.vector.tensor_scalar(cell[:, :], dst, blocks, 13, ALU.bitwise_and,
                                            ALU.logical_shift_left).then_inc(s_prep, 1)
                    nc.vector.tensor_scalar(cell_t[:, :], src, P - 1, 13, ALU.bitwise_and,
                                            ALU.logical_shift_left).then_inc(s_prep, 1)
                    dve.wait_ge(s_prep, 3)
                    nc.vector.tensor_tensor(cell[:, :], cell[:, :], cell_t[:, :], ALU.bitwise_or).then_inc(s_prep, 1)
                    dve.wait_ge(s_prep, 4)
                    nc.vector.tensor_scalar(cell_t[:, :], src, blocks, None, ALU.bitwise_and).then_inc(s_prep, 1)
                    dve.wait_ge(s_prep, 5)
                    nc.vector.tensor_tensor(cell[:, :], cell[:, :], cell_t[:, :], ALU.bitwise_or).then_inc(s_prep, 1)
                    dve.wait_ge(s_prep, 6)
                    nc.vector.tensor_scalar(cell_t[:, :], dst, P - 1, None, ALU.bitwise_and).then_inc(s_prep, 1)
                    dve.wait_ge(s_prep, 7)
                    nc.vector.tensor_tensor(cell[:, :], cell[:, :], cell_t[:, :], ALU.bitwise_or).then_inc(s_prep, 1)
                    dve.wait_ge(s_prep, 8)
                    dve.wait_ge(s_spare, 1)
                    dve.sem_inc(s_slot, 2)

                    def group(i, g, b):
                        dve.wait_ge(s_rows[b], 16 * (i + 1))
                        for j in range(G):
                            nc.vector.scalar_tensor_tensor(
                                eq_dst[:, j, :], rows[:, b, 1, :], keyf[:, 1, bass.ds(g * G + j, 1)],
                                before[:, j, :], ALU.is_equal, ALU.mult).then_inc(s_eqd, 1)
                        dve.wait_ge(s_slot, g + 1)
                        nc.vector.tensor_copy(where[:, b, :], cell[:, bass.ds(g * G, G)]).then_inc(s_cellcp, 1)
                        for j in range(G):
                            dve.wait_ge(s_eqd, g * G + j + 1)
                            eq = nc.vector.scalar_tensor_tensor(
                                eq_dst[:, j, :], rows[:, b, 0, :], keyf[:, 0, bass.ds(g * G + j, 1)],
                                eq_dst[:, j, :], ALU.is_equal, ALU.mult, accum_out=found[:, b, j:j + 1])
                            eq.then_inc(s_eqs, 1)
                        dve.wait_ge(s_eqs, (g + 1) * G)
                        nc.vector.tensor_scalar(late[:, b, :], found[:, b, :], BEFORE, None,
                                                ALU.is_ge).then_inc(s_late, 1)
                        dve.wait_ge(s_cellcp, g + 1)
                        dve.wait_ge(s_late, g + 1)
                        dve.sem_inc(s_rowfree, 1)
                        nc.vector.copy_predicated(where[:, b, :], late[:, b, :], spare[:, :]).then_inc(s_where, 1)

                    with dve.Fori(0, NG // 2) as i:
                        for b in range(2):
                            group(i, i * 2 + b, b)

                @block.gpsimd
                def _(pool):
                    pool.iota(spare[:, :], pattern=[[P, G]], base=NB * STRIP, channel_multiplier=1).then_inc(s_spare, 1)

                    def group(g, b):
                        wait_alone(pool, s_where, g + 1, passed_pool)
                        for j in range(G):
                            pool.indirect_dma_start(
                                out=counts,
                                out_offset=bass.IndirectOffsetOnAxis(ap=where[:, b, j:j + 1].bitcast(U32), axis=0),
                                in_=found[:, b, j:j + 1], in_offset=None,
                                compute_op=ALU.add).then_inc(s_added, 16)
                        pack2.put(pool, g, b, passed_pool)
                        pool.wait_ge(s_added, 16 * G * (g + 1))
                        pool.sem_inc(s_slot, 1)

                    with pool.Fori(0, NG // 2) as i:
                        for b in range(2):
                            group(i * 2 + b, b)
                    pack2.finish(pool)

        with stage(nc, "cast") as (sem, c3):
            U = 4
            wide = sb("wide", [P, U, NP], F32, c3)
            narrow = sb("narrow", [P, U, NP], FP8, c3)
            part = sb("part", [P, U, NB], F32, c3)
            over = sb("over", [P, NB], F32, c3)
            over1 = sb("over1", [P, 1], F32, c3)
            limit = sb("limit", [P, 1], F32, c3)
            ones1 = sb("ones1", [P, 1], F32, c3)
            over_p = c3.enter_context(nc.psum_tensor("over_p", [P, 512], F32))
            s_limit, s_over, s_over1, s_overp, s_many = (
                sem("s_limit"), sem("s_over"), sem("s_over1"), sem("s_overp"), sem("s_many"))
            s_in = [sem(f"s_in{u}") for u in range(U)]
            s_saved = [sem(f"s_saved{u}") for u in range(U)]
            s_cast, s_sum, s_deg = sem("s_cast"), sem("s_sum"), sem("s_deg")
            with nc.Block() as block:
                @block.sync
                def _(sp):
                    def load(j, u, first):
                        if not first:
                            wait_alone(sp, s_cast, j - U + 1, passed_sp)
                            wait_alone(sp, s_over, j - U + 1, passed_sp)
                            wait_alone(sp, s_sum, j - U + 1, passed_sp)
                        sp.dma_start(wide[:, u, :], strip32(j)).then_inc(s_in[u], 16)
                    for u in range(U):
                        load(u, u, True)
                    with sp.Fori(1, NB // U) as i:
                        for u in range(U):
                            load(i * U + u, u, False)
                    load(NB - 1, 0, False)

                @block.scalar
                def _(act):
                    def cast(i, j, u, first):
                        act.wait_ge(s_in[u], 16 * (i + 1))
                        if not first:
                            wait_alone(act, s_saved[u], 16 * i, passed_act)
                        nc.scalar.activation(narrow[:, u, :], wide[:, u, :], ACT.Copy, saturate=False).then_inc(s_cast, 1)
                        act.wait_ge(s_sum, j + 1)
                        nc.scalar.activation(wide[:, u, :], wide[:, u, :], ACT.Relu, bias=limit[:, :],
                                             accum_out=over[:, bass.ds(j, 1)]).then_inc(s_over, 1)
                        wait_alone(act, s_cast, j + 1, passed_act)
                        act.dma_start(strips8[bass.ds(j, 1), :, :].rearrange("o p c -> p (o c)"),
                                      narrow[:, u, :].bitcast(U8)).then_inc(s_saved[u], 16)
                    act.wait_ge(s_limit, 1)
                    for u in range(U):
                        cast(0, u, u, True)
                    with act.Fori(1, NB // U) as i:
                        for u in range(U):
                            cast(i, i * U + u, u, False)
                    cast(NB // U, NB - 1, 0, False)
                    act.wait_ge(s_saved[0], 16 * (NB // U + 1))
                    for u in range(1, U):
                        act.wait_ge(s_saved[u], 16 * (NB // U))

                @block.tensor
                def _(pe):
                    pe.wait_ge(s_over1, 1)
                    nc.tensor.matmul(over_p[0:1, 0:1], over1[:, :], ones1[:, :], start=True, stop=True).then_inc(s_overp, 1)

                @block.vector
                def _(dve):
                    nc.vector.memset(ones1[:, :], 1.0)
                    nc.vector.memset(limit[:, :], -MANY).then_inc(s_limit, 1)
                    nc.vector.memset(outdeg[:, :], 0.0).then_inc(s_deg, 1)

                    def degrees(i, j, u):
                        dve.wait_ge(s_in[u], 16 * (i + 1))
                        nc.vector.tensor_reduce(part[:, u, :], wide[:, u, :].rearrange("p (b c) -> p b c", c=P),
                                                AX.X, ALU.add).then_inc(s_sum, 1)
                        dve.wait_ge(s_sum, j + 1)
                        dve.wait_ge(s_deg, j + 1)
                        nc.vector.tensor_tensor(outdeg[:, :], outdeg[:, :], part[:, u, :], ALU.add).then_inc(s_deg, 1)
                    with dve.Fori(0, NB // U) as i:
                        for u in range(U):
                            degrees(i, i * U + u, u)
                    degrees(NB // U, NB - 1, 0)
                    dve.wait_ge(s_over, NB)
                    nc.vector.tensor_reduce(over1[:, :], over[:, :], AX.X, ALU.add).then_inc(s_over1, 1)
                    dve.wait_ge(s_overp, 1)
                    nc.vector.tensor_scalar(many[:, :], over_p[0:1, 0:1], 0.0, None, ALU.is_gt).then_inc(s_many, 1)

        layer0(nc, h, sb, strips8, strip32, many, cheb, x_sb, outdeg, eye, passed, keys, r_row, weight, cutoff, place,
               sorted1, sorted2)
        tables_of_layer1(nc, h, sb, z_table, u_table, x_sb, e_parts)
        with ExitStack() as c78:
            agg = sb("agg1", [P, NB, MW], F32, c78)
            layer1_edges(nc, h, sb, sorted1, u_table, e_parts, block_of[0], first_of[0], eye, agg, passed)
            end_of_layer1(nc, h, sb, agg, x_sb)
        table_of_layer2(nc, h, sb, r_table, x_sb, eye, passed_pe)
        with ExitStack() as c9:
            agg = sb("agg2", [P, NB, D], F32, c9)
            layer2_edges(nc, h, sb, sorted2, r_table, block_of[1], first_of[1], agg, passed)
            end_of_layer2(nc, h, sb, agg, x_sb)
        layer3(nc, h, sb, strips8, strip32, many, x_sb, outdeg, eye, passed)
        with stage(nc, "store") as (sem, c9):
            s_o = sem("s_o")
            with nc.Block() as block:
                @block.sync
                def _(sp):
                    sp.dma_start(out, x_sb[:, :, :]).then_inc(s_o, 16)
                    sp.wait_ge(s_o, 16)


def in_order(eng, done):
    count = [0]

    def step(instruction):
        count[0] += 1
        instruction.then_inc(done, 1)
        eng.wait_ge(done, count[0])
    return step


def wide_ap(col):
    return col.unsqueeze(2).to_broadcast([P, NB, D])


def row_ap(row):
    return row.unsqueeze(1).to_broadcast([P, NB, D])


def normalize(nc, step, sqrt_of, x, sq, col, eps_col):
    mean, var = col[:, 0, :], col[:, 1, :]
    step(nc.vector.tensor_reduce(mean, x, AX.X, ALU.add))
    step(nc.vector.tensor_scalar(mean, mean, 1.0 / D, None, ALU.mult))
    step(nc.vector.tensor_tensor(x, x, wide_ap(mean), ALU.subtract))
    step(nc.vector.tensor_tensor(sq, x, x, ALU.mult))
    step(nc.vector.tensor_reduce(var, sq, AX.X, ALU.add))
    step(nc.vector.tensor_scalar(var, var, 1.0 / D, 1e-5, ALU.mult, ALU.add))
    sqrt_of(var)
    step(nc.vector.reciprocal(var, var))
    step(nc.vector.tensor_tensor(x, x, wide_ap(var), ALU.mult))


def layer0(nc, h, sb, strips8, strip32, many, cheb, x_sb, outdeg, eye, passed, keys, r_row, weight, cutoff, place,
           sorted1, sorted2):
    passed_sp, passed_act, passed_dve, passed_pe, passed_pool = passed
    U = 7
    W3 = 3 * D
    with stage(nc, "cheb") as (sem, c4):
        dis = sb("dis", [P, NB], F32, c4)
        dis_m1 = sb("dis_m1", [P, NB], F32, c4)
        dis_m2 = sb("dis_m2", [P, NB], F32, c4)
        has = sb("has", [P, NB], F32, c4)
        term = sb("term", [P, 2, NB, D], F32, c4)
        parts = sb("parts", [P, 2, NB, W3], BF16, c4)
        cbuf = sb("cbuf", [P, U, NP], FP8, c4)
        y = sb("y", [P, U, D], F32, c4)
        scaled = sb("scaled", [P, 2, NB, D], F32, c4)
        none = sb("none", [P, W3 - D], BF16, c4)
        r = sb("r", [P, U, D], F32, c4)
        acc = [c4.enter_context(nc.psum_tensor(f"acc{u}", [P, 512], F32)) for u in range(U)]
        s_c = [sem(f"s_c{u}") for u in range(U)]
        s_wide, s_none = sem("s_wide"), sem("s_none")
        wide = cbuf[:, :, :].rearrange("p u c -> p (u c)").bitcast(F32)[:, 0:NP]
        s_strip, s_accfree, s_parts, s_term = sem("s_strip"), sem("s_accfree"), sem("s_parts"), sem("s_term")
        s_kept = [sem("s_kept0"), sem("s_kept1")]
        s_prep4, s_root, s_root_in = sem("s_prep4"), sem("s_root"), sem("s_root_in")
        s_y, s_v, s_hi, s_r, s_mid = sem("s_y"), sem("s_v"), sem("s_hi"), sem("s_r"), sem("s_mid")
        pack2 = RecordsOfLayer2(nc, sb, c4, 'b', sem, keys, r_row, weight, place[1], sorted2)
        record = sb("record1", [P, 4, G, R1], F32, c4)
        row = sb("row1", [P, 4, G], I32, c4)
        s_packed = sem("s_packed1")
        s_put = [sem(f"s_put1_{b}") for b in range(4)]
        s_attr = [sem(f"s_attr1_{b}") for b in range(4)]
        with nc.Block() as block:
            @block.sync
            def _(sp):
                def load_wide(n0, j, first):
                    if not first:
                        wait_alone(sp, s_strip, n0 + j, passed_sp)
                    sp.dma_start(wide, strip32(j)).then_inc(s_wide, 16)

                def load(n0, rr, u, first):
                    if not first:
                        wait_alone(sp, s_strip, n0 + rr * U + u - U + 1, passed_sp)
                    sp.dma_start(cbuf[:, u, :].bitcast(U8), strips8[bass.ds(rr * U + u, 1), :, :].rearrange("o p c -> p (o c)")
                                 ).then_inc(s_c[u], 16)
                def keep(k, slot):
                    wait_alone(sp, s_term, NB * (k + 1), passed_sp)
                    sp.dma_start(cheb[:, :, bass.ds(k, 1), :].rearrange("p b k f -> p b (k f)"),
                                 term[:, slot, :, :]).then_inc(s_kept[slot], 16)

                def rest_of_pass(n0):
                    with sp.Fori(1, NB // U) as rr:
                        for u in range(U):
                            load(n0, rr, u, False)

                with sp.If(sp.value_load(many[0:1, 0:1], min_val=0, max_val=1) == 0):
                    for u in range(U):
                        load(0, 0, u, True)
                    rest_of_pass(0)
                    keep(0, 0)
                    with sp.Fori(0, (K - 2) // 2) as m:
                        for odd in range(2):
                            n0 = (m * 2 + 1 + odd) * NB
                            for u in range(U):
                                load(n0, 0, u, False)
                            keep(m * 2 + 1 + odd, 1 - odd)
                            rest_of_pass(n0)
                with sp.Else():
                    load_wide(0, 0, True)
                    with sp.Fori(1, NB) as j:
                        load_wide(0, j, False)
                    keep(0, 0)
                    with sp.Fori(0, (K - 2) // 2) as m:
                        for odd in range(2):
                            n0 = (m * 2 + 1 + odd) * NB
                            load_wide(n0, 0, False)
                            keep(m * 2 + 1 + odd, 1 - odd)
                            with sp.Fori(1, NB) as j:
                                load_wide(n0, j, False)
                keep(K - 1, 1)
                sp.wait_ge(s_kept[0], 16 * (K // 2))
                sp.wait_ge(s_kept[1], 16 * (K // 2))

            @block.tensor
            def _(pe):
                def strip(slot, n_div, n, u):
                    pe.wait_ge(s_c[u], 16 * (n_div + 1))
                    wait_alone(pe, s_accfree, n + 1, passed_pe)
                    for s in range(NB):
                        mm = nc.tensor.matmul(acc[u][:, 0:W3], cbuf[:, u, s * P:(s + 1) * P],
                                              parts[:, slot, s, :], start=(s == 0), stop=(s == NB - 1))
                    mm.then_inc(s_strip, 1)

                def wide_strip(slot, n, u):
                    wait_alone(pe, s_wide, 16 * (n + 1), passed_pe)
                    wait_alone(pe, s_accfree, n + 1, passed_pe)
                    nc.tensor.matmul(acc[u][:, D:W3], parts[:, slot, 0, 0:P], none[:, :], start=True, stop=True)
                    for s in range(NB):
                        mm = nc.tensor.matmul(acc[u][:, 0:D], wide[:, s * P:(s + 1) * P], scaled[:, slot, s, :],
                                              start=(s == 0), stop=(s == NB - 1))
                    mm.then_inc(s_strip, 1)

                def one_pass(k, slot, exact):
                    wait_alone(pe, s_parts, NB * k, passed_pe)
                    with pe.Fori(0, NB // U) as rr:
                        for u in range(U):
                            n = (k - 1) * NB + rr * U + u
                            if exact:
                                strip(slot, (k - 1) * (NB // U) + rr, n, u)
                            else:
                                wide_strip(slot, n, u)

                def passes(exact):
                    one_pass(1, 0, exact)
                    with pe.Fori(0, (K - 2) // 2) as m:
                        one_pass(m * 2 + 2, 1, exact)
                        one_pass(m * 2 + 3, 0, exact)
                pe.wait_ge(s_none, 1)
                with pe.If(pe.value_load(many[0:1, 0:1], min_val=0, max_val=1) == 0):
                    passes(True)
                with pe.Else():
                    passes(False)

            @block.scalar
            def _(act):
                act.wait_ge(s_root_in, 1)
                nc.scalar.activation(dis[:, :], dis[:, :], ACT.Sqrt).then_inc(s_root, 1)
                for b in range(2):
                    pack2.pack(act, 0, b, b, True, T // 2)
                with act.Fori(1, NG // 2) as i:
                    for b in range(2):
                        pack2.pack(act, i, i * 2 + b, b, False, T // 2)

                def pack1(i, s, b, first):
                    if not first:
                        act.wait_ge(s_put[b], 16 * G * i)
                    cols = bass.ds(s * G, G)
                    for f, of in enumerate((cutoff[:, cols], keys[:, 1, cols], keys[:, 0, cols])):
                        nc.scalar.activation(record[:, b, :, R + f:R + f + 1].rearrange("p t o -> p (t o)"), of, ACT.Copy)
                    nc.scalar.activation(row[:, b, :], place[0][:, cols], ACT.Copy).then_inc(s_packed, 1)
                    act.dma_start(record[:, b, :, 0:R], h["attr"][:, cols, :]).then_inc(s_attr[b], 16)
                for b in range(4):
                    pack1(0, b, b, True)
                with act.Fori(1, NG // 4) as i:
                    for b in range(4):
                        pack1(i, i * 4 + b, b, False)

            @block.gpsimd
            def _(pool):
                with pool.Fori(0, NG // 2) as i:
                    for b in range(2):
                        pack2.put(pool, i * 2 + b, b, passed_pool)
                with pool.Fori(0, NG // 4) as i:
                    for b in range(4):
                        wait_alone(pool, s_packed, i * 4 + b + 1, passed_pool)
                        wait_alone(pool, s_attr[b], 16 * (i + 1), passed_pool)
                        for j in range(G):
                            pool.indirect_dma_start(
                                out=sorted1,
                                out_offset=bass.IndirectOffsetOnAxis(ap=row[:, b, j:j + 1].bitcast(U32), axis=0),
                                in_=record[:, b, j, :], in_offset=None).then_inc(s_put[b], 16)
                pack2.finish(pool)
                for b in range(4):
                    pool.wait_ge(s_put[b], 16 * G * (NG // 4))

            @block.vector
            def _(dve):
                step = in_order(dve, s_prep4)
                step(nc.vector.tensor_scalar(dis[:, :], outdeg[:, :], 1e-12, None, ALU.max))
                dve.sem_inc(s_root_in, 1)
                step(nc.vector.tensor_scalar(has[:, :], outdeg[:, :], 0.0, None, ALU.is_gt))
                dve.wait_ge(s_root, 1)
                step(nc.vector.reciprocal(dis[:, :], dis[:, :]))
                step(nc.vector.tensor_tensor(dis[:, :], dis[:, :], has[:, :], ALU.mult))
                step(nc.vector.tensor_scalar(dis_m1[:, :], dis[:, :], -1.0, None, ALU.mult))
                step(nc.vector.tensor_scalar(dis_m2[:, :], dis[:, :], -2.0, None, ALU.mult))
                step(nc.vector.tensor_copy(term[:, 0, :, :], x_sb[:, :, :]))
                step(nc.vector.memset(term[:, 1, :, :], 0.0))
                nc.vector.memset(none[:, :], 0.0).then_inc(s_none, 1)
                dve.sem_inc(s_accfree, U)

                def split(slot, b, u, n):
                    blk = lambda t: t[:, slot, bass.ds(b, 1), :].rearrange("p o f -> p (o f)")
                    hi, mid, lo = (parts[:, slot, bass.ds(b, 1), i * D:(i + 1) * D].rearrange("p o f -> p (o f)")
                                   for i in range(3))
                    dve.wait_ge(s_term, n + 1)
                    v = blk(scaled)
                    nc.vector.tensor_scalar(v, blk(term), dis[:, bass.ds(b, 1)], None, ALU.mult).then_inc(s_v, 1)
                    dve.wait_ge(s_v, n + 1)
                    nc.vector.tensor_copy(hi, v).then_inc(s_hi, 1)
                    dve.wait_ge(s_hi, n + 1)
                    nc.vector.tensor_tensor(r[:, u, :], v, hi, ALU.subtract).then_inc(s_r, 1)
                    dve.wait_ge(s_r, n + 1)
                    nc.vector.tensor_copy(mid, r[:, u, :]).then_inc(s_mid, 1)
                    dve.wait_ge(s_mid, n + 1)
                    nc.vector.tensor_tensor(lo, r[:, u, :], mid, ALU.subtract).then_inc(s_parts, 1)

                def block_of_term(k, rr, u, slot, scale):
                    b = rr * U + u
                    n = (k - 1) * NB + b
                    dve.wait_ge(s_strip, n + 1)
                    nc.vector.tensor_reduce(y[:, u, :], acc[u][:, 0:W3].rearrange("p (s f) -> p f s", f=D),
                                            AX.X, ALU.add).then_inc(s_y, 1)
                    dve.wait_ge(s_y, n + 1)
                    dve.sem_inc(s_accfree, 1)
                    t = term[:, slot, bass.ds(b, 1), :].rearrange("p o f -> p (o f)")
                    nc.vector.scalar_tensor_tensor(t, y[:, u, :], scale[:, bass.ds(b, 1)], t,
                                                   ALU.mult, ALU.subtract).then_inc(s_term, 1)
                    split(slot, b, u, n + NB)

                dve.sem_inc(s_term, NB)
                with dve.Fori(0, NB // U) as rr:
                    for u in range(U):
                        split(0, rr * U + u, u, rr * U + u)
                with dve.Fori(0, NB // U) as rr:
                    for u in range(U):
                        block_of_term(1, rr, u, 1, dis_m1)
                with dve.Fori(0, (K - 2) // 2) as m:
                    for odd in range(2):
                        wait_alone(dve, s_kept[odd], (m + 1) * 16, passed_dve)
                        with dve.Fori(0, NB // U) as rr:
                            for u in range(U):
                                block_of_term(m * 2 + 2 + odd, rr, u, odd, dis_m2)

    U = 4
    Q = K // 2
    with stage(nc, "out0") as (sem, c5):
        tin = sb("tin", [P, U, K, D], F32, c5)
        tT = sb("tT", [2 * D, 2, Q, P], F32, c5)
        w0 = sb("w0", [2 * D, Q, D], F32, c5)
        b0 = sb("b0", [P, D], F32, c5)
        o_sb = sb("o_sb", [P, NB, D], F32, c5)
        sq = sb("sq", [P, NB, D], F32, c5)
        col = sb("col", [P, 2, NB], F32, c5)
        turned = [[c5.enter_context(nc.psum_tensor(f"turned{a}{b}", [P, 512], F32)) for b in range(2)] for a in range(2)]
        acc = [c5.enter_context(nc.psum_tensor(f"acc5_{u}", [P, 512], F32)) for u in range(2)]
        s_t = [sem(f"s_t{u}") for u in range(U)]
        s_w0 = sem("s_w0")
        s_turn, s_copyA, s_copyB, s_out0, s_ofree, s_tfree = (
            sem("s_turn"), sem("s_copyA"), sem("s_copyB"), sem("s_out0"), sem("s_ofree"), sem("s_tfree"))
        s_ln0, s_sq0, s_sqi0 = sem("s_ln0"), sem("s_sq0"), sem("s_sqi0")

        def over_blocks(eng, body):
            with eng.Fori(0, NB // U) as i:
                for u in range(U):
                    body(i, i * U + u, u)
            body(NB // U, NB - 1, 0)

        with nc.Block() as block:
            @block.sync
            def _(sp):
                sp.dma_start(w0[:, :, :], h["w0"]).then_inc(s_w0, 16)
                sp.dma_start(b0[:, :], h["b0"]).then_inc(s_w0, 16)
                sp.sem_inc(s_tfree, U)

                def load(i, b, u):
                    wait_alone(sp, s_tfree, b + 1, passed_sp)
                    sp.dma_start(tin[:, u, :, :], cheb[:, bass.ds(b, 1), :, :].rearrange("p o k f -> p (o k) f")
                                 ).then_inc(s_t[u], 16)
                over_blocks(sp, load)

            @block.tensor
            def _(pe):
                pe.wait_ge(s_w0, 32)

                def body(i, b, u):
                    o = u % 2
                    pe.wait_ge(s_t[u], 16 * (i + 1))
                    for a in range(2):
                        for q in range(Q // 2):
                            tr = nc.tensor.transpose(turned[o][a][0:2 * D, q * P:(q + 1) * P],
                                                     tin[:, u, 2 * (a * Q // 2 + q):2 * (a * Q // 2 + q) + 2, :]
                                                     .rearrange("p k f -> p (k f)"), eye[:, :])
                        tr.then_inc(s_turn, 1)
                    pe.wait_ge(s_copyA, b + 1)
                    pe.wait_ge(s_copyB, b + 1)
                    pe.sem_inc(s_tfree, 1)
                    pe.wait_ge(s_ofree, b + 1)
                    for q in range(Q):
                        mm = nc.tensor.matmul(acc[o][:, 0:D], tT[:, o, q, :], w0[:, q, :], start=(q == 0), stop=(q == Q - 1))
                    mm.then_inc(s_out0, 1)
                over_blocks(pe, body)

            @block.scalar
            def _(act):
                def body(i, b, u):
                    act.wait_ge(s_turn, b * 2 + 1)
                    act.wait_ge(s_out0, b + 1)
                    nc.scalar.activation(tT[:, u % 2, 0:Q // 2, :].rearrange("p q c -> p (q c)"),
                                         turned[u % 2][0][0:2 * D, :], ACT.Copy).then_inc(s_copyA, 1)
                act.sem_inc(s_out0, 2)
                over_blocks(act, body)
                act.wait_ge(s_sqi0, 1)
                nc.scalar.activation(col[:, 1, :], col[:, 1, :], ACT.Sqrt).then_inc(s_sq0, 1)

            @block.vector
            def _(dve):
                dve.sem_inc(s_ofree, 2)

                def body(i, b, u):
                    dve.wait_ge(s_turn, b * 2 + 2)
                    dve.wait_ge(s_out0, b + 1)
                    nc.vector.tensor_copy(tT[:, u % 2, Q // 2:Q, :].rearrange("p q c -> p (q c)"),
                                          turned[u % 2][1][0:2 * D, :]).then_inc(s_copyB, 1)
                    dve.wait_ge(s_out0, b + 3)
                    nc.vector.tensor_tensor(o_sb[:, bass.ds(b, 1), :].rearrange("p o f -> p (o f)"),
                                            acc[u % 2][:, 0:D], b0[:, :], ALU.add).then_inc(s_ofree, 1)
                dve.wait_ge(s_w0, 32)
                over_blocks(dve, body)
                step = in_order(dve, s_ln0)
                dve.wait_ge(s_ofree, NB + 2)
                step(nc.vector.scalar_tensor_tensor(x_sb[:, :, :], o_sb[:, :, :], 0.0, x_sb[:, :, :], ALU.max, ALU.add))

                def root(var):
                    dve.sem_inc(s_sqi0, 1)
                    dve.wait_ge(s_sq0, 1)
                normalize(nc, step, root, x_sb[:, :, :], sq[:, :, :], col, None)


def tables_of_layer1(nc, h, sb, z_table, u_table, x_sb, e_parts):
    with stage(nc, "tables") as (sem, c6):
        emb = sb("emb", [Z, 2 * EM], F32, c6)
        embT = sb("embT", [EM, Z], F32, c6)
        adapt = sb("adapt", [EM, EM], F32, c6)
        kind = sb("kind", [P, NB], I32, c6)
        mult = sb("mult", [P, NB], F32, c6)
        of_node = sb("of_node", [P, NB, 2 * EM], F32, c6)
        u_rows = sb("u_rows", [P, NB, UW], F32, c6)
        adapted = c6.enter_context(nc.psum_tensor("adapted", [P, 512], F32))
        s_small, s_adapted, s_emb, s_ztab, s_node, s_rows6, s_tab6, s_kind = (
            sem("s_small"), sem("s_adapted"), sem("s_emb"), sem("s_ztab"), sem("s_node"), sem("s_rows6"),
            sem("s_tab6"), sem("s_kind"))
        s_chain6 = sem("s_chain6")
        with nc.Block() as block:
            @block.sync
            def _(sp):
                sp.dma_start(emb[:, 0:EM], h["emb"]).then_inc(s_small, 16)
                sp.dma_start(embT[:, :], h["embT"]).then_inc(s_small, 16)
                sp.dma_start(adapt[:, :], h["adaptT"]).then_inc(s_small, 16)
                sp.dma_start(kind[:, :], h["kind"]).then_inc(s_kind, 16)
                sp.dma_start(mult[:, :], h["mult"]).then_inc(s_kind, 16)
                sp.wait_ge(s_emb, 1)
                sp.wait_ge(s_small, 48)
                sp.dma_start(z_table, emb[:, :]).then_inc(s_ztab, 16)
                sp.wait_ge(s_node, 16 * NB)
                sp.wait_ge(s_rows6, 3)
                sp.dma_start(u_table.rearrange("(b p) f -> p b f", p=P), u_rows[:, :, :]).then_inc(s_tab6, 16)
                sp.wait_ge(s_tab6, 16)

            @block.tensor
            def _(pe):
                pe.wait_ge(s_small, 48)
                nc.tensor.matmul(adapted[0:Z, 0:EM], embT[:, :], adapt[:, :], start=True, stop=True).then_inc(s_adapted, 1)

            @block.gpsimd
            def _(pool):
                pool.wait_ge(s_ztab, 16)
                pool.wait_ge(s_kind, 32)
                for b in range(NB):
                    pool.indirect_dma_start(out=of_node[:, b, :], out_offset=None, in_=z_table,
                                            in_offset=bass.IndirectOffsetOnAxis(ap=kind[:, b:b + 1].bitcast(U32), axis=0)
                                            ).then_inc(s_node, 16)

            @block.vector
            def _(dve):
                dve.wait_ge(s_adapted, 1)
                nc.vector.tensor_copy(emb[:, EM:2 * EM], adapted[0:Z, 0:EM]).then_inc(s_emb, 1)
                dve.wait_ge(s_kind, 32)
                nc.vector.tensor_tensor(u_rows[:, :, 0:D], x_sb[:, :, :], wide_ap(mult[:, :]), ALU.mult).then_inc(s_rows6, 1)
                nc.vector.tensor_copy(u_rows[:, :, D:D + 1].rearrange("p b o -> p (b o)"), mult[:, :]).then_inc(s_rows6, 1)
                dve.wait_ge(s_node, 16 * NB)
                nc.vector.tensor_copy(u_rows[:, :, D + 1:UW], of_node[:, :, EM:2 * EM]).then_inc(s_rows6, 1)
                step = in_order(dve, s_chain6)
                rest = of_node[:, :, 0:EM]
                for n in range(3):
                    part = e_parts[:, :, n * EM:(n + 1) * EM]
                    step(nc.vector.tensor_copy(part, rest))
                    if n < 2:
                        step(nc.vector.tensor_tensor(rest, rest, part, ALU.subtract))


def gather_rows(pool, table, ring, got, g, slot, ring_slot, s_got):
    for j in range(G):
        pool.indirect_dma_start(
            out=got[:, slot, j, :], out_offset=None, in_=table,
            in_offset=bass.IndirectOffsetOnAxis(ap=ring[:, ring_slot, j:j + 1].bitcast(U32), axis=0)
        ).then_inc(s_got[slot], 16)


def layer1_edges(nc, h, sb, sorted1, table, e_parts, block_of, first_of, eye, agg, passed):
    passed_sp, passed_act, passed_dve, passed_pe, passed_pool = passed
    U = 4
    with stage(nc, "edges1") as (sem, c7):
        rec = sb("rec", [P, U, G, R1], F32, c7)
        onehot = sb("onehot", [P, U, G, P], F32, c7)
        ring = sb("ring", [P, U, G], I32, c7)
        rel = sb("rel", [P, U, G], F32, c7)
        lanes = sb("lanes", [P, P], F32, c7)
        got = sb("got", [P, U, G, UW], F32, c7)
        msg = sb("msg", [P, 2, G, MW], F32, c7)
        prod = sb("prod", [P, G, 3 * EM], F32, c7)
        logit = sb("logit", [P, G], F32, c7)
        gate = sb("gate", [P, G, D], F32, c7)
        attrT = sb("attrT", [TWO, G // 2 * P], F32, c7)
        onehotT = sb("onehotT", [P, G * P], BF16, c7)
        hid = sb("hid", [2 * D + 1, G // 2 * P], F32, c7)
        w1 = sb("w1_7", [TWO, 2 * D], F32, c7)
        w2 = sb("w2_7", [2 * D + 1, 2 * D], F32, c7)
        b1 = sb("b1_7", [2 * D, 1], F32, c7)

        def bank(name):
            return c7.enter_context(nc.psum_tensor(name, [P, 512], F32))
        attr_p, hid_p, onehot_p, sum_p = bank("attr_p"), bank("hid_p"), bank("onehot_p"), bank("sum_p")
        e_p = [bank("e_p0"), bank("e_p1")]
        gate_p = [bank("gate_p0"), bank("gate_p1")]
        s_rec = [sem(f"s_rec{u}") for u in range(U)]
        s_got = [sem(f"s_got{u}") for u in range(U)]
        s_ring = sem("s_ring")
        s_used = sem("s_used")
        s_attrT = sem("s_attrT")
        s_onehotT = sem("s_onehotT")
        s_hidden = sem("s_hidden")
        s_silu = sem("s_silu")
        s_gatep = sem("s_gatep")
        s_e = sem("s_e")
        s_prod = sem("s_prod")
        s_gadd = sem("s_gadd")
        s_sum = sem("s_sum")
        s_acc = sem("s_acc")
        s_turn, s_turned, s_onehot, s_rel, s_logit, s_gcw, s_mult = (
            sem("s_turn"), sem("s_turned"), sem("s_onehot"), sem("s_rel"), sem("s_logit"), sem("s_gcw"), sem("s_mult"))
        s_const, s_ones, s_lanes, s_agg0 = sem("s_const7"), sem("s_ones7"), sem("s_lanes7"), sem("s_agg0")

        def loop(eng, body):
            with eng.Fori(0, NGS // U) as i:
                for u in range(U):
                    body(i, i * U + u, u)

        def ahead(i, u, n):
            return i + (u + n) // U, (u + n) % U

        with nc.Block() as block:
            @block.sync
            def _(sp):
                sp.dma_start(w1[:, :], h["l1_w1"]).then_inc(s_const, 16)
                sp.dma_start(w2[:, :], h["l1_w2"]).then_inc(s_const, 16)
                sp.dma_start(b1[:, :], h["l1_b1"]).then_inc(s_const, 16)

                def load(g, u):
                    sp.dma_start(rec[:, u, :, :].rearrange("p j f -> p (j f)"),
                                 sorted1[bass.ds(g * SLOTS, SLOTS), :].rearrange("(p j) f -> p (j f)", p=P)
                                 ).then_inc(s_rec[u], 16)
                for u in range(U):
                    load(u, u)

                def body(i, g, u):
                    wait_alone(sp, s_used, g + U + 1, passed_sp)
                    load(g + U, u)
                loop(sp, body)
                for u in range(U):
                    sp.wait_ge(s_rec[u], 16 * (NGS // U + 1))

            @block.gpsimd
            def _(pool):
                pool.iota(lanes[:, :], pattern=[[1, P]], base=0, channel_multiplier=0,
                          allow_small_or_imprecise_dtypes=True).then_inc(s_lanes, 1)

                def body(i, g, u):
                    wait_alone(pool, s_ring, g + 1, passed_pool)
                    wait_alone(pool, s_used, g + 1, passed_pool)
                    gather_rows(pool, table, ring, got, g, u, u, s_got)
                loop(pool, body)

            @block.tensor
            def _(pe):
                pe.wait_ge(s_const, 48)

                def turn(i, g, u):
                    wait_alone(pe, s_rec[u], 16 * (i + 1), passed_pe)
                    wait_alone(pe, s_attrT, g + 1, passed_pe)
                    for q in range(2):
                        tr = nc.tensor.transpose(
                            attr_p[0:TWO, q * P:(q + 1) * P],
                            rec[:, u, 2 * q:2 * q + 2, :].rearrange("p t f -> p (t f)")[:, 0:TWO], eye[:, :])
                    tr.then_inc(s_turn, 1)
                    pe.wait_ge(s_onehot, g + 1)
                    pe.wait_ge(s_onehotT, g + 1)
                    for j in range(G):
                        tr = nc.tensor.transpose(onehot_p[:, j * P:(j + 1) * P], onehot[:, u, j, :], eye[:, :])
                    tr.then_inc(s_turned, 1)

                def hidden(g):
                    pe.wait_ge(s_attrT, g + 2)
                    pe.wait_ge(s_silu, g + 1)
                    nc.tensor.matmul(hid_p[0:2 * D, 0:2 * P], w1[:, :], attrT[:, :], start=True, stop=True
                                     ).then_inc(s_hidden, 1)

                def fetch(g, u):
                    blk = pe.value_load(block_of[0:1, bass.ds(g, 1)], min_val=0, max_val=NB - 1)
                    pe.wait_ge(s_onehotT, g + 2)
                    pe.wait_ge(s_prod, g + 1)
                    for j in range(G):
                        mm = nc.tensor.matmul(e_p[u % 2][:, j * 3 * EM:(j + 1) * 3 * EM], onehotT[:, j * P:(j + 1) * P],
                                              e_parts[:, bass.ds(blk, 1), :].rearrange("p o f -> p (o f)"),
                                              start=True, stop=True)
                    mm.then_inc(s_e, 1)

                def gates(g, u):
                    pe.wait_ge(s_silu, g + 2)
                    pe.wait_ge(s_gadd, g + 1)
                    for q in range(2):
                        mm = nc.tensor.matmul(gate_p[u % 2][:, q * 2 * D:(q + 1) * 2 * D], hid[:, q * P:(q + 1) * P],
                                              w2[:, :], start=True, stop=True)
                    mm.then_inc(s_gatep, 1)

                for g in range(2):
                    turn(0, g, g)
                    hidden(g)
                    fetch(g, g)
                    gates(g, g)

                def body(i, g, u):
                    pe.wait_ge(s_used, g + U + 1)
                    pe.wait_ge(s_acc, g + 1)
                    for j in range(G):
                        mm = nc.tensor.matmul(sum_p[:, 0:MW], onehot[:, u, j, :], msg[:, u % 2, j, :],
                                              start=(j == 0), stop=(j == G - 1))
                    mm.then_inc(s_sum, 1)
                    i2, u2 = ahead(i, u, 2)
                    turn(i2, g + 2, u2)
                    hidden(g + 2)
                    fetch(g + 2, u2)
                    gates(g + 2, u2)
                loop(pe, body)

            @block.scalar
            def _(act):
                act.wait_ge(s_const, 48)
                act.sem_inc(s_attrT, 1)
                act.sem_inc(s_onehotT, 1)
                act.sem_inc(s_silu, 1)

                def body(g):
                    act.wait_ge(s_turn, g + 1)
                    act.wait_ge(s_hidden, g + 1)
                    nc.scalar.activation(attrT[:, :], attr_p[0:TWO, 0:2 * P], ACT.Copy).then_inc(s_attrT, 1)
                    act.wait_ge(s_turned, g + 1)
                    act.wait_ge(s_e, g + 1)
                    nc.scalar.activation(onehotT[:, :], onehot_p[:, :], ACT.Copy).then_inc(s_onehotT, 1)
                    act.wait_ge(s_hidden, g + 2)
                    act.wait_ge(s_gatep, g + 1)
                    nc.scalar.activation(hid[0:2 * D, :], hid_p[0:2 * D, 0:2 * P], ACT.Silu, bias=b1[:, :]
                                         ).then_inc(s_silu, 1)
                act.wait_ge(s_ones, 1)
                for g in range(2):
                    body(g)
                loop(act, lambda i, g, u: body(g + 2))

            @block.vector
            def _(dve):
                for s, n in ((s_used, U), (s_hidden, 1), (s_gatep, 1), (s_e, 1), (s_prod, 2), (s_gadd, 2),
                             (s_sum, U), (s_acc, 1)):
                    dve.sem_inc(s, n)
                nc.vector.memset(agg[:, :, :], 0.0).then_inc(s_agg0, 1)
                nc.vector.memset(hid[2 * D:2 * D + 1, :], 1.0).then_inc(s_ones, 1)
                dve.wait_ge(s_lanes, 1)
                dve.wait_ge(s_agg0, 1)

                def prepare(i, g, u):
                    dve.wait_ge(s_rec[u], 16 * (i + 1))
                    nc.vector.tensor_copy(ring[:, u, :], rec[:, u, :, R + 1:R + 2].rearrange("p j o -> p (j o)")
                                          ).then_inc(s_ring, 1)
                    dve.wait_ge(s_sum, g + 1)
                    nc.vector.tensor_scalar(rel[:, u, :], rec[:, u, :, R + 2:R1].rearrange("p j o -> p (j o)"),
                                            first_of[:, bass.ds(g, 1)], None, ALU.subtract).then_inc(s_rel, 1)
                    dve.wait_ge(s_rel, g + 1)
                    for j in range(G):
                        one = nc.vector.tensor_scalar(onehot[:, u, j, :], lanes[:, :], rel[:, u, j:j + 1], None, ALU.is_equal)
                    one.then_inc(s_onehot, 1)

                def messages(i, g, u):
                    b = u % 2
                    dve.wait_ge(s_got[u], 16 * G * (i + 1))
                    dve.wait_ge(s_e, g + 2)
                    nc.vector.tensor_tensor(
                        prod[:, :, :].rearrange("p j (n k) -> p j n k", n=3),
                        e_p[b][:, 0:G * 3 * EM].rearrange("p (j n k) -> p j n k", j=G, n=3),
                        got[:, u, :, D + 1:UW].unsqueeze(2).to_broadcast([P, G, 3, EM]), ALU.mult).then_inc(s_prod, 1)
                    dve.wait_ge(s_sum, g + 3)
                    nc.vector.tensor_copy(msg[:, b, :, D:MW], got[:, u, :, D:MW]).then_inc(s_mult, 1)
                    dve.wait_ge(s_prod, g + 3)
                    nc.vector.tensor_reduce(logit[:, :], prod[:, :, :], AX.X, ALU.add).then_inc(s_logit, 1)
                    dve.wait_ge(s_logit, g + 1)
                    dve.wait_ge(s_gatep, g + 2)
                    nc.vector.tensor_tensor(gate[:, :, :], gate_p[b][:, 0:G * D].rearrange("p (j f) -> p j f", j=G),
                                            logit[:, :].unsqueeze(2).to_broadcast([P, G, D]), ALU.add).then_inc(s_gadd, 1)
                    dve.wait_ge(s_gadd, g + 3)
                    nc.vector.tensor_tensor(gate[:, :, :], gate[:, :, :], rec[:, u, :, R:R + 1].to_broadcast([P, G, D]),
                                            ALU.mult).then_inc(s_gcw, 1)
                    dve.wait_ge(s_gcw, g + 1)
                    dve.wait_ge(s_mult, g + 1)
                    nc.vector.tensor_tensor(msg[:, b, :, 0:D], gate[:, :, :], got[:, u, :, 0:D], ALU.mult
                                            ).then_inc(s_used, 1)

                for g in range(2):
                    prepare(0, g, g)

                def body(i, g, u):
                    messages(i, g, u)
                    i2, u2 = ahead(i, u, 2)
                    prepare(i2, g + 2, u2)
                    blk = dve.value_load(block_of[0:1, bass.ds(g, 1)], min_val=0, max_val=NB - 1)
                    at = agg[:, bass.ds(blk, 1), :].rearrange("p o f -> p (o f)")
                    dve.wait_ge(s_sum, g + U + 1)
                    nc.vector.tensor_tensor(at, at, sum_p[:, 0:MW], ALU.add).then_inc(s_acc, 1)
                    dve.wait_ge(s_acc, g + 2)
                loop(dve, body)


def layer2_edges(nc, h, sb, sorted2, table, block_of, first_of, agg, passed):
    passed_sp, passed_act, passed_dve, passed_pe, passed_pool = passed
    U = 4
    with stage(nc, "edges2") as (sem, c9):
        rec = sb("rec9", [P, U, G, R2], F32, c9)
        onehot = sb("onehot9", [P, U, G, P], F32, c9)
        ring = sb("ring9", [P, U, G], I32, c9)
        rel = sb("rel9", [P, U, G], F32, c9)
        lanes = sb("lanes9", [P, P], F32, c9)
        got = sb("got9", [P, U, G, D], F32, c9)
        sum_p = [c9.enter_context(nc.psum_tensor(f"sum9_{n}", [P, 512], F32)) for n in range(2)]
        s_rec = [sem(f"s_rec9_{u}") for u in range(U)]
        s_got = [sem(f"s_got9_{u}") for u in range(U)]
        s_ring, s_rel, s_onehot = sem("s_ring9"), sem("s_rel9"), sem("s_onehot9")
        s_sum = sem("s_sum9")
        s_acc = sem("s_acc9")
        s_lanes, s_agg0 = sem("s_lanes9"), sem("s_agg0_9")

        def loop(eng, body):
            with eng.Fori(0, NGS // U) as i:
                for u in range(U):
                    body(i, i * U + u, u)

        with nc.Block() as block:
            @block.sync
            def _(sp):
                def load(g, u):
                    sp.dma_start(rec[:, u, :, :].rearrange("p j f -> p (j f)"),
                                 sorted2[bass.ds(g * SLOTS, SLOTS), :].rearrange("(p j) f -> p (j f)", p=P)
                                 ).then_inc(s_rec[u], 16)
                for u in range(U):
                    load(u, u)

                def body(i, g, u):
                    wait_alone(sp, s_onehot, g + 1, passed_sp)
                    load(g + U, u)
                loop(sp, body)
                for u in range(U):
                    sp.wait_ge(s_rec[u], 16 * (NGS // U + 1))

            @block.gpsimd
            def _(pool):
                pool.iota(lanes[:, :], pattern=[[1, P]], base=0, channel_multiplier=0,
                          allow_small_or_imprecise_dtypes=True).then_inc(s_lanes, 1)

                def body(i, g, u):
                    wait_alone(pool, s_ring, g + 1, passed_pool)
                    wait_alone(pool, s_sum, g + 1, passed_pool)
                    gather_rows(pool, table, ring, got, g, u, u, s_got)
                loop(pool, body)

            @block.tensor
            def _(pe):
                def body(i, g, u):
                    pe.wait_ge(s_onehot, g + 1)
                    pe.wait_ge(s_got[u], 16 * G * (i + 1))
                    pe.wait_ge(s_acc, g + 1)
                    for j in range(G):
                        mm = nc.tensor.matmul(sum_p[u % 2][:, 0:D], onehot[:, u, j, :], got[:, u, j, :],
                                              start=(j == 0), stop=(j == G - 1))
                    mm.then_inc(s_sum, 1)
                loop(pe, body)

            @block.vector
            def _(dve):
                dve.sem_inc(s_sum, U)
                dve.sem_inc(s_acc, 2)
                nc.vector.memset(agg[:, :, :], 0.0).then_inc(s_agg0, 1)
                dve.wait_ge(s_lanes, 1)
                dve.wait_ge(s_agg0, 1)

                def prepare(i, g, u):
                    dve.wait_ge(s_rec[u], 16 * (i + 1))
                    dve.wait_ge(s_sum, g + 1)
                    nc.vector.tensor_copy(ring[:, u, :], rec[:, u, :, 0:1].rearrange("p j o -> p (j o)")).then_inc(s_ring, 1)
                    nc.vector.tensor_scalar(rel[:, u, :], rec[:, u, :, 2:3].rearrange("p j o -> p (j o)"),
                                            first_of[:, bass.ds(g, 1)], None, ALU.subtract).then_inc(s_rel, 1)
                    dve.wait_ge(s_rel, g + 1)
                    for j in range(G):
                        one = nc.vector.tensor_scalar(onehot[:, u, j, :], lanes[:, :], rel[:, u, j:j + 1],
                                                      rec[:, u, j, 1:2], ALU.is_equal, ALU.mult)
                    one.then_inc(s_onehot, 1)

                for g in range(3):
                    prepare(0, g, g)

                def body(i, g, u):
                    prepare(i + (u + 3) // U, g + 3, (u + 3) % U)
                    blk = dve.value_load(block_of[0:1, bass.ds(g, 1)], min_val=0, max_val=NB - 1)
                    at = agg[:, bass.ds(blk, 1), :].rearrange("p o f -> p (o f)")
                    dve.wait_ge(s_sum, g + U + 1)
                    nc.vector.tensor_tensor(at, at, sum_p[u % 2][:, 0:D], ALU.add).then_inc(s_acc, 1)
                    dve.wait_ge(s_acc, g + 3)
                loop(dve, body)


def end_of_layer1(nc, h, sb, agg, x_sb):
    with stage(nc, "end1") as (sem, c8):
        gamma = sb("gamma", [P, D], F32, c8)
        beta = sb("beta", [P, D], F32, c8)
        y = sb("y8", [P, NB, D], F32, c8)
        sq = sb("sq8", [P, NB, D], F32, c8)
        tot = sb("tot8", [P, NB], F32, c8)
        col = sb("col8", [P, 2, NB], F32, c8)
        s_in8, s_chain8, s_rt8, s_rti8 = sem("s_in8"), sem("s_chain8"), sem("s_rt8"), sem("s_rti8")
        with nc.Block() as block:
            @block.sync
            def _(sp):
                sp.dma_start(gamma[:, :], h["gamma"]).then_inc(s_in8, 16)
                sp.dma_start(beta[:, :], h["beta"]).then_inc(s_in8, 16)

            @block.scalar
            def _(act):
                for n in range(2):
                    act.wait_ge(s_rti8, n + 1)
                    nc.scalar.activation(col[:, 1, :], col[:, 1, :], ACT.Sqrt).then_inc(s_rt8, 1)

            @block.vector
            def _(dve):
                step = in_order(dve, s_chain8)
                dve.wait_ge(s_in8, 32)
                roots = [0]

                def root(var):
                    roots[0] += 1
                    dve.sem_inc(s_rti8, 1)
                    dve.wait_ge(s_rt8, roots[0])
                step(nc.vector.tensor_scalar(tot[:, :], agg[:, :, D:MW].rearrange("p b o -> p (b o)"), 1e-8, None, ALU.max))
                step(nc.vector.reciprocal(tot[:, :], tot[:, :]))
                step(nc.vector.tensor_tensor(y[:, :, :], agg[:, :, 0:D], wide_ap(tot[:, :]), ALU.mult))
                step(nc.vector.tensor_tensor(y[:, :, :], y[:, :, :], x_sb[:, :, :], ALU.add))
                normalize(nc, step, root, y[:, :, :], sq[:, :, :], col, None)
                step(nc.vector.tensor_tensor(y[:, :, :], y[:, :, :], row_ap(gamma[:, :]), ALU.mult))
                step(nc.vector.tensor_tensor(y[:, :, :], y[:, :, :], row_ap(beta[:, :]), ALU.add))
                step(nc.vector.tensor_tensor(x_sb[:, :, :], y[:, :, :], x_sb[:, :, :], ALU.add))
                normalize(nc, step, root, x_sb[:, :, :], sq[:, :, :], col, None)


def table_of_layer2(nc, h, sb, r_table, x_sb, eye, passed_pe):
    Q = NR // 2
    C = 4
    with stage(nc, "rtable") as (sem, c9):
        xc = sb("xc", [P, C, D], F32, c9)
        xT = sb("xT9", [D, C * P], F32, c9)
        hT = sb("hT9", [2 * D, Q, C * P], F32, c9)
        rows = sb("rows9", [P, C, NR * D], F32, c9)
        w1 = sb("w1_9", [D, Q, 2 * D], F32, c9)
        w2 = sb("w2_9", [2 * D, Q, 2 * D], F32, c9)
        b1 = sb("b1_9", [2 * D, 1], F32, c9)
        turned = c9.enter_context(nc.psum_tensor("turned9", [P, 512], F32))
        hp = [c9.enter_context(nc.psum_tensor(f"hp9_{q}", [P, 512], F32)) for q in range(2)]
        rp = [c9.enter_context(nc.psum_tensor(f"rp9_{c}", [P, 512], F32)) for c in range(C)]
        s_c9, s_xc, s_turn9, s_xT, s_hp, s_hT, s_rp, s_rows9, s_stored = (
            sem("s_c9"), sem("s_xc"), sem("s_turn9"), sem("s_xT"), sem("s_hp"), sem("s_hT"), sem("s_rp"),
            sem("s_rows9"), sem("s_stored9"))

        def chunks(eng, body):
            with eng.Fori(0, NB // C) as i:
                body(i, i * C, C)
            body(NB // C, NB - 1, 1)

        with nc.Block() as block:
            @block.sync
            def _(sp):
                sp.dma_start(w1[:, :, :], h["l2_w1"]).then_inc(s_c9, 16)
                sp.dma_start(w2[:, :, :], h["l2_w2"]).then_inc(s_c9, 16)
                sp.dma_start(b1[:, :], h["l2_b1"]).then_inc(s_c9, 16)

                def body(i, b0, n):
                    sp.wait_ge(s_rows9, i + 1)
                    sp.sem_inc(s_c9, 1)
                    dst = r_table.rearrange("(b p r) f -> p b (r f)", p=P, r=NR)[:, bass.ds(b0, n), :]
                    sp.dma_start(dst, rows[:, 0:n, :]).then_inc(s_stored, 16)
                chunks(sp, body)
                sp.wait_ge(s_stored, 16 * (NB // C + 2))

            @block.tensor
            def _(pe):
                pe.wait_ge(s_c9, 48)

                def body(i, b0, n):
                    wait_alone(pe, s_xc, i + 1, passed_pe)
                    for c in range(n):
                        tr = nc.tensor.transpose(turned[0:D, c * P:(c + 1) * P], xc[:, c, :], eye[:, :])
                    tr.then_inc(s_turn9, 1)
                    pe.wait_ge(s_xT, i + 1)
                    for q in range(Q):
                        pe.wait_ge(s_hT, i * Q + q + 1)
                        nc.tensor.matmul(hp[q % 2][0:2 * D, 0:n * P], w1[:, q, :], xT[:, 0:n * P],
                                         start=True, stop=True).then_inc(s_hp, 1)
                    pe.wait_ge(s_hT, (i + 1) * Q + 2)
                    for c in range(n):
                        for q in range(Q):
                            mm = nc.tensor.matmul(rp[c][:, q * 2 * D:(q + 1) * 2 * D], hT[:, q, c * P:(c + 1) * P],
                                                  w2[:, q, :], start=True, stop=True)
                    mm.then_inc(s_rp, 1)
                chunks(pe, body)

            @block.scalar
            def _(act):
                act.sem_inc(s_hT, 2)
                act.wait_ge(s_c9, 48)

                def body(i, b0, n):
                    for q in range(Q):
                        act.wait_ge(s_hp, i * Q + q + 1)
                        nc.scalar.activation(hT[:, q, 0:n * P], hp[q % 2][0:2 * D, 0:n * P], ACT.Relu,
                                             bias=b1[:, :]).then_inc(s_hT, 1)
                chunks(act, body)

            @block.vector
            def _(dve):
                dve.sem_inc(s_stored, 16)

                def body(i, b0, n):
                    nc.vector.tensor_copy(xc[:, 0:n, :], x_sb[:, bass.ds(b0, n), :]).then_inc(s_xc, 1)
                    dve.wait_ge(s_turn9, i + 1)
                    nc.vector.tensor_copy(xT[:, 0:n * P], turned[0:D, 0:n * P]).then_inc(s_xT, 1)
                    dve.wait_ge(s_rp, i + 1)
                    dve.wait_ge(s_stored, 16 * (i + 1))
                    for c in range(n):
                        cpy = nc.vector.tensor_copy(rows[:, c, :], rp[c][:, 0:NR * D])
                    cpy.then_inc(s_rows9, 1)
                chunks(dve, body)


def end_of_layer2(nc, h, sb, agg, x_sb):
    with stage(nc, "end2") as (sem, c8):
        bias = sb("bias10", [P, D], F32, c8)
        sq = sb("sq10", [P, NB, D], F32, c8)
        col = sb("col10", [P, 2, NB], F32, c8)
        s_in10, s_chain10, s_rt10, s_rti10 = sem("s_in10"), sem("s_chain10"), sem("s_rt10"), sem("s_rti10")
        with nc.Block() as block:
            @block.sync
            def _(sp):
                sp.dma_start(bias[:, :], h["l2_b2"]).then_inc(s_in10, 16)

            @block.scalar
            def _(act):
                act.wait_ge(s_rti10, 1)
                nc.scalar.activation(col[:, 1, :], col[:, 1, :], ACT.Sqrt).then_inc(s_rt10, 1)

            @block.vector
            def _(dve):
                step = in_order(dve, s_chain10)
                dve.wait_ge(s_in10, 16)

                def root(var):
                    dve.sem_inc(s_rti10, 1)
                    dve.wait_ge(s_rt10, 1)
                a = agg[:, :, :]
                step(nc.vector.tensor_tensor(a, a, row_ap(bias[:, :]), ALU.add))
                step(nc.vector.scalar_tensor_tensor(x_sb[:, :, :], a, 0.0, x_sb[:, :, :], ALU.max, ALU.add))
                normalize(nc, step, root, x_sb[:, :, :], sq[:, :, :], col, None)


def layer3(nc, h, sb, strips8, strip32, many, x_sb, outdeg, eye, passed):
    U = 7
    W3 = 3 * D
    passed_sp, passed_act, passed_dve, passed_pe, passed_pool = passed
    with stage(nc, "layer3") as (sem, c11):
        ci = sb("ci", [P, NB], F32, c11)
        v = sb("v11", [P, NB, D], F32, c11)
        r = sb("r11", [P, NB, D], F32, c11)
        parts = sb("parts11", [P, NB, W3 + 1], BF16, c11)
        none = sb("none11", [P, W3 - D], BF16, c11)
        ones1 = sb("ones11", [P, 1], F32, c11)
        s_wide = sem("s_wide")
        cbuf = sb("cbuf11", [P, U, NP], FP8, c11)
        wide = cbuf[:, :, :].rearrange("p u c -> p (u c)").bitcast(F32)[:, 0:NP]
        agg = sb("agg11", [P, NB, D], F32, c11)
        deg = sb("deg11", [P, NB], F32, c11)
        cj = sb("cj11", [P, NB], F32, c11)
        acc = [c11.enter_context(nc.psum_tensor(f"acc11_{u}", [P, 512], F32)) for u in range(U)]
        s_c = [sem(f"s_c11_{u}") for u in range(U)]
        s_strip, s_accfree, s_chain, s_parts, s_sum, s_deg = (
            sem("s_strip11"), sem("s_accfree11"), sem("s_chain11"), sem("s_parts11"), sem("s_sum11"), sem("s_deg11"))
        s_rt, s_rti = sem("s_rt11"), sem("s_rti11")
        with nc.Block() as block:
            @block.sync
            def _(sp):
                def load(rr, u, first):
                    if not first:
                        wait_alone(sp, s_strip, rr * U + u - U + 1, passed_sp)
                    sp.dma_start(cbuf[:, u, :].bitcast(U8), strips8[bass.ds(rr * U + u, 1), :, :].rearrange("o p c -> p (o c)")
                                 ).then_inc(s_c[u], 16)
                with sp.If(sp.value_load(many[0:1, 0:1], min_val=0, max_val=1) == 0):
                    for u in range(U):
                        load(0, u, True)
                    with sp.Fori(1, NB // U) as rr:
                        for u in range(U):
                            load(rr, u, False)
                with sp.Else():
                    sp.dma_start(wide, strip32(0)).then_inc(s_wide, 16)
                    with sp.Fori(1, NB) as j:
                        wait_alone(sp, s_strip, j, passed_sp)
                        sp.dma_start(wide, strip32(j)).then_inc(s_wide, 16)

            @block.tensor
            def _(pe):
                def strip(rr, u):
                    wait_alone(pe, s_c[u], 16 * (rr + 1), passed_pe)
                    wait_alone(pe, s_accfree, rr * U + u + 1, passed_pe)
                    for s in range(NB):
                        mm = nc.tensor.matmul(acc[u][:, 0:W3 + 1], cbuf[:, u, s * P:(s + 1) * P], parts[:, s, :],
                                              start=(s == 0), stop=(s == NB - 1))
                    mm.then_inc(s_strip, 1)

                def wide_strip(rr, u):
                    wait_alone(pe, s_wide, 16 * (rr * U + u + 1), passed_pe)
                    wait_alone(pe, s_accfree, rr * U + u + 1, passed_pe)
                    nc.tensor.matmul(acc[u][:, D:W3], parts[:, 0, 0:P], none[:, :], start=True, stop=True)
                    for s in range(NB):
                        nc.tensor.matmul(acc[u][:, W3:W3 + 1], wide[:, s * P:(s + 1) * P], ones1[:, :],
                                         start=(s == 0), stop=(s == NB - 1))
                    for s in range(NB):
                        mm = nc.tensor.matmul(acc[u][:, 0:D], wide[:, s * P:(s + 1) * P], v[:, s, :],
                                              start=(s == 0), stop=(s == NB - 1))
                    mm.then_inc(s_strip, 1)
                pe.wait_ge(s_parts, 1)
                with pe.If(pe.value_load(many[0:1, 0:1], min_val=0, max_val=1) == 0):
                    with pe.Fori(0, NB // U) as rr:
                        for u in range(U):
                            strip(rr, u)
                with pe.Else():
                    with pe.Fori(0, NB // U) as rr:
                        for u in range(U):
                            wide_strip(rr, u)

            @block.scalar
            def _(act):
                act.wait_ge(s_rti, 1)
                nc.scalar.activation(ci[:, :], ci[:, :], ACT.Sqrt).then_inc(s_rt, 1)
                act.wait_ge(s_rti, 2)
                nc.scalar.activation(cj[:, :], cj[:, :], ACT.Sqrt).then_inc(s_rt, 1)

            @block.vector
            def _(dve):
                step = in_order(dve, s_chain)
                step(nc.vector.tensor_scalar(ci[:, :], outdeg[:, :], 1.0, None, ALU.max))
                dve.sem_inc(s_rti, 1)
                dve.wait_ge(s_rt, 1)
                step(nc.vector.reciprocal(ci[:, :], ci[:, :]))
                step(nc.vector.tensor_tensor(v[:, :, :], x_sb[:, :, :], wide_ap(ci[:, :]), ALU.mult))
                step(nc.vector.tensor_copy(parts[:, :, 0:D], v[:, :, :]))
                step(nc.vector.tensor_tensor(r[:, :, :], v[:, :, :], parts[:, :, 0:D], ALU.subtract))
                step(nc.vector.tensor_copy(parts[:, :, D:2 * D], r[:, :, :]))
                step(nc.vector.tensor_tensor(parts[:, :, 2 * D:W3], r[:, :, :], parts[:, :, D:2 * D], ALU.subtract))
                step(nc.vector.memset(parts[:, :, W3:W3 + 1], 1.0))
                step(nc.vector.memset(none[:, :], 0.0))
                step(nc.vector.memset(ones1[:, :], 1.0))
                dve.sem_inc(s_parts, 1)
                dve.sem_inc(s_accfree, U)
                with dve.Fori(0, NB // U) as rr:
                    for u in range(U):
                        n = rr * U + u
                        dve.wait_ge(s_strip, n + 1)
                        nc.vector.tensor_reduce(agg[:, bass.ds(n, 1), :].rearrange("p o f -> p (o f)"),
                                                acc[u][:, 0:W3].rearrange("p (s f) -> p f s", f=D),
                                                AX.X, ALU.add).then_inc(s_sum, 1)
                        nc.vector.tensor_copy(deg[:, bass.ds(n, 1)], acc[u][:, W3:W3 + 1]).then_inc(s_deg, 1)
                        dve.wait_ge(s_sum, n + 1)
                        dve.wait_ge(s_deg, n + 1)
                        dve.sem_inc(s_accfree, 1)
                step(nc.vector.tensor_scalar(cj[:, :], deg[:, :], 1.0, None, ALU.max))
                dve.sem_inc(s_rti, 1)
                dve.wait_ge(s_rt, 2)
                step(nc.vector.reciprocal(cj[:, :], cj[:, :]))
                step(nc.vector.tensor_tensor(agg[:, :, :], agg[:, :, :], wide_ap(cj[:, :]), ALU.mult))
                step(nc.vector.tensor_scalar(deg[:, :], deg[:, :], 0.0, None, ALU.is_gt))
                step(nc.vector.tensor_scalar(cj[:, :], deg[:, :], -1.0, 1.0, ALU.mult, ALU.add))
                step(nc.vector.tensor_tensor(agg[:, :, :], agg[:, :, :], wide_ap(deg[:, :]), ALU.mult))
                step(nc.vector.tensor_tensor(v[:, :, :], x_sb[:, :, :], wide_ap(cj[:, :]), ALU.mult))
                step(nc.vector.tensor_tensor(agg[:, :, :], agg[:, :, :], v[:, :, :], ALU.add))

        hc = sb("hc", [P, 2, D], F32, c11)
        hT = sb("hT11", [D, 2, P], F32, c11)
        wt = sb("wt11", [D, D], F32, c11)
        b3 = sb("b3", [P, D], F32, c11)
        col = sb("col11", [P, 2, NB], F32, c11)
        s_w, s_hc, s_tn, s_hT, s_mm, s_o = (
            sem("s_w11"), sem("s_hc11"), sem("s_tn11"), sem("s_hT11"), sem("s_mm11"), sem("s_o11"))
        s_chainb, s_rtb, s_rtib = sem("s_chain11b"), sem("s_rt11b"), sem("s_rti11b")

        def blocks(eng, body):
            with eng.Fori(0, NB // 2) as i:
                for u in range(2):
                    body(i * 2 + u, u)
            body(NB - 1, 0)
        with nc.Block() as block:
            @block.sync
            def _(sp):
                sp.dma_start(wt[:, :], h["l3_w"]).then_inc(s_w, 16)
                sp.dma_start(b3[:, :], h["l3_b"]).then_inc(s_w, 16)

            @block.tensor
            def _(pe):
                pe.wait_ge(s_w, 32)

                def body(b, u):
                    wait_alone(pe, s_hc, b + 1, passed_pe)
                    nc.tensor.transpose(acc[u][0:D, 0:P], hc[:, u, :], eye[:, :]).then_inc(s_tn, 1)
                    pe.wait_ge(s_hT, b + 1)
                    nc.tensor.matmul(acc[2 + u][:, 0:D], hT[:, u, :], wt[:, :], start=True, stop=True).then_inc(s_mm, 1)
                blocks(pe, body)

            @block.scalar
            def _(act):
                def body(b, u):
                    act.wait_ge(s_tn, b + 1)
                    nc.scalar.activation(hT[:, u, :], acc[u][0:D, 0:P], ACT.Copy).then_inc(s_hT, 1)
                blocks(act, body)
                act.wait_ge(s_rtib, 1)
                nc.scalar.activation(col[:, 1, :], col[:, 1, :], ACT.Sqrt).then_inc(s_rtb, 1)

            @block.vector
            def _(dve):
                dve.wait_ge(s_w, 32)

                def body(b, u):
                    nc.vector.tensor_copy(hc[:, u, :], agg[:, bass.ds(b, 1), :].rearrange("p o f -> p (o f)")).then_inc(s_hc, 1)
                    dve.wait_ge(s_mm, b + 1)
                    nc.vector.tensor_tensor(v[:, bass.ds(b, 1), :].rearrange("p o f -> p (o f)"), acc[2 + u][:, 0:D],
                                            b3[:, :], ALU.add).then_inc(s_o, 1)
                blocks(dve, body)
                dve.wait_ge(s_o, NB)
                step = in_order(dve, s_chainb)
                step(nc.vector.scalar_tensor_tensor(x_sb[:, :, :], v[:, :, :], 0.0, x_sb[:, :, :], ALU.max, ALU.add))

                def root(var):
                    dve.sem_inc(s_rtib, 1)
                    dve.wait_ge(s_rtb, 1)
                normalize(nc, step, root, x_sb[:, :, :], r[:, :, :], col, None)


class RecordsOfLayer2:
    HALF = T // 4

    def __init__(self, nc, sb, memory, name, sem, keys, r_row, weight, place, sorted2):
        self.nc, self.keys, self.r_row, self.weight, self.place, self.out = nc, keys, r_row, weight, place, sorted2
        self.record = sb("record2" + name, [P, 2, 2, R2], F32, memory)
        self.row = sb("row2" + name, [P, 2, 2], I32, memory)
        self.s_packed = sem("s_packed2" + name)
        self.s_put = [sem(f"s_put2{name}{b}") for b in range(2)]

    def pack(self, act, i, s, b, first, start=0):
        nc = self.nc
        if not first:
            act.wait_ge(self.s_put[b], 32 * i)
        cols = bass.ds(start + s * 2, 2)
        for f, of in enumerate((self.r_row[:, cols], self.weight[:, cols], self.keys[:, 1, cols])):
            nc.scalar.activation(self.record[:, b, :, f:f + 1].rearrange("p t o -> p (t o)"), of, ACT.Copy)
        nc.scalar.activation(self.row[:, b, :], self.place[:, cols], ACT.Copy).then_inc(self.s_packed, 1)

    def put(self, pool, s, b, passed_pool):
        wait_alone(pool, self.s_packed, s + 1, passed_pool)
        for t in range(2):
            pool.indirect_dma_start(
                out=self.out, out_offset=bass.IndirectOffsetOnAxis(ap=self.row[:, b, t:t + 1].bitcast(U32), axis=0),
                in_=self.record[:, b, t, :], in_offset=None).then_inc(self.s_put[b], 16)

    def finish(self, pool):
        for b in range(2):
            pool.wait_ge(self.s_put[b], 32 * (self.HALF // 2))


def kernel(**inputs):
    import numpy as np
    import concourse.bacc as bacc
    from concourse.bass_utils import run_bass_kernel_spmd

    a = {k: np.asarray(v) for k, v in inputs.items()}

    def pad(v, rows, fill=0):
        w = np.full((rows,) + v.shape[1:], fill, v.dtype)
        w[:len(v)] = v
        return w

    def by_node(v, w):
        return pad(v.reshape(N, w), NP).reshape(NB, P, w).transpose(1, 0, 2)

    def by_edge(v, fill=0):
        return pad(v.reshape(E), P * T, fill).reshape(P, T)

    def every(v):
        return np.broadcast_to(v.reshape(1, -1), (P, v.size))

    def two2(m, o):
        w = np.zeros((2, m.shape[0], 2, m.shape[1]), m.dtype)
        w[0, :, 0], w[1, :, 1] = m, o
        return w.reshape(2 * m.shape[0], 2 * m.shape[1])

    def two(m):
        return two2(m, m)

    i, w = np.arange(P * T - E, dtype=np.int32), NP - N
    src = np.concatenate([a["src"], N + i % w]).reshape(P, T)
    dst = np.concatenate([a["dst"], N + i // w % w]).reshape(P, T)
    keys = np.stack([src, dst], 1)
    arrays = {
        "x": by_node(a["x"], D),
        "key_cols": keys,
        "key_rows": keys.reshape(P, 2, NG, G).transpose(2, 1, 3, 0).reshape(NG, 2 * G * P),
        "w0": a["L0_gnn_weights"].reshape(K // 2, 2 * D, D).transpose(1, 0, 2),
        "b0": every(a["L0_gnn_bias"]),
        "emb": a["L1_gnn_emb"],
        "embT": a["L1_gnn_emb"].T,
        "adaptT": a["L1_gnn_adaptW"].T,
        "kind": by_node(a["node_type_119"], 1)[:, :, 0],
        "mult": by_node(a["node_vec"], 1)[:, :, 0],
        "distance": by_edge(a["edge_weight"]),
        "weight": by_edge(a["edge_weight1"]),
        "relation": by_edge(a["edge_type_8"]),
        "attr": pad(a["edge_attr_40"], P * T).reshape(P, T, R),
        "l1_w1": two(pad(a["L1_gnn_W1"].T, R1))[:TWO],
        "l1_b1": np.tile(a["L1_gnn_b1"], 2).reshape(-1, 1),
        "l1_w2": np.concatenate([two(a["L1_gnn_W2"].T), np.tile(a["L1_gnn_b2"], 2).reshape(1, -1)]),
        "gamma": every(a["L1_gnn_gamma"]),
        "beta": every(a["L1_gnn_beta"]),
        "l2_w1": a["L2_gnn_weight1"].reshape(NR // 2, 2, D, D).transpose(2, 0, 1, 3).reshape(D, NR // 2, 2 * D),
        "l2_b1": np.tile(a["L2_gnn_bias1"], 2).reshape(-1, 1),
        "l2_w2": np.stack([two2(a["L2_gnn_weight2"][2 * q], a["L2_gnn_weight2"][2 * q + 1]) for q in range(NR // 2)], 1),
        "l2_b2": every(a["L2_gnn_bias2"]),
        "l3_w": a["L3_gnn_W"].T,
        "l3_b": every(a["L3_gnn_b"]),
    }
    nc = bacc.Bacc("TRN2", target_bir_lowering=False, num_devices=1)
    arrays = {f"in_{k}": np.ascontiguousarray(v) for k, v in arrays.items()}
    h = {k[3:]: nc.dram_tensor(k, v.shape, mybir.dt.from_np(v.dtype), kind="ExternalInput").ap()
         for k, v in arrays.items()}
    out = nc.dram_tensor("out", (P, NB, D), F32, kind="ExternalOutput").ap()
    gnn_kernel(nc, h, out)
    r = run_bass_kernel_spmd(nc, [arrays], core_ids=[0])
    return r.results[0]["out"].transpose(1, 0, 2).reshape(NP, D)[:N]
```

```python
import concourse.bass as bass
from concourse import mybir
from concourse.alu_op_type import AluOpType as ALU
from contextlib import ExitStack, contextmanager

F32 = mybir.dt.float32
BF16 = mybir.dt.bfloat16
FP8 = mybir.dt.float8e4
I32 = mybir.dt.int32
U8 = mybir.dt.uint8
U32 = mybir.dt.uint32
ACT = mybir.ActivationFunctionType
AX = mybir.AxisListType

P = 128
N = 6250
D = 48
NB = -(-N // P)
NP = NB * P
E = 206250
G = 4
NG = 404
GC = 8
ON_ACT = 3
NC = 202
T = G * NG
K = 16
R = 40
Z, EM = 119, 32
NR = 8
ROW = 64 * P
STRIP = P * ROW
SLOTS = G * P
NGS = 452
FILL = 24
AHEAD = 4
R1 = R + 3
TWO = R1 + R
IN_COUNT, IN_CAST, IN_CHEB, IN_OUT0 = 2 * NC, 10 * (NB - 1), 540, 4 * (NB - 1)
AT_COUNT, AT_CAST, AT_CHEB, AT_OUT0 = 2, 10, 5, 4
assert IN_COUNT + IN_CAST + IN_CHEB + IN_OUT0 == T
R2 = 3
BLANK = -1.0
UW = D + 1 + EM
MW = D + 1
BEFORE = 1024.0
MANY = 16.0
assert NGS >= (P * T + NB * (SLOTS - 1)) // SLOTS and NGS % 4 == 0
assert NG % 4 == 0 and GC * NC == T and NC % 2 == 0
PI = 3.141592653589793


@contextmanager
def stage(nc, label):
    held = []

    def sem(name):
        held.append(nc.alloc_semaphore(name=f"{label}_{name}"))
        return held[-1]
    with ExitStack() as memory:
        yield sem, memory
    nc.clear_and_free_semaphores(held)
    nc.all_engine_barrier()


def wait_alone(eng, semaphore, value, passed):
    eng.wait_ge(semaphore, value)
    eng.sem_inc(passed, 1)


class CountingSort:

    def __init__(self, nc, sb, memory, name, sem, key, shared, place, block_of, first_of):
        self.nc, self.key, self.place, self.block_of, self.first_of = nc, key, place, block_of, first_of
        (self.block_no, self.minus_block, self.group_no, self.sums, self.lower, self.ones, self.one, self.shifted,
         self.hit, self.square, self.run, self.pos) = shared

        def own(n, shape, dt):
            return sb(f"srt{name}_{n}", shape, dt, memory)
        self.block = own("block", [P, T], BF16)
        self.per_block, self.total, self.groups = (own(n, [P, NB], F32) for n in ("per_block", "total", "groups"))
        self.groups_i = own("groups_i", [P, NB], I32)
        self.end, self.base = own("end", [P, NB], F32), own("base", [P, NB], F32)
        self.blk = own("blk", [P, NGS + AHEAD], F32)
        self.s_counted, self.s_sums, self.s_square, self.s_hit, self.s_run, self.s_pos, self.s_end, self.s_ready = (
            sem(f"{n}{name}") for n in ("s_counted", "s_sums", "s_square", "s_hit", "s_run", "s_pos", "s_end", "s_ready"))

    def start(self, dve, step):
        nc = self.nc
        step(nc.vector.tensor_scalar(self.shifted[:, :], self.key, 7, None, ALU.logical_shift_right))
        step(nc.vector.tensor_copy(self.block[:, :], self.shifted[:, :]))
        dve.sem_inc(self.s_counted, 1)
        dve.sem_inc(self.s_ready, 1)

    def count_on_dve(self, dve, b):
        dve.wait_ge(self.s_counted, b + 1)
        self.nc.vector.tensor_scalar(self.pos[:, :], self.block[:, :], self.block_no[:, bass.ds(b, 1)], None,
                                     ALU.is_equal, ALU.add, accum_out=self.per_block[:, bass.ds(b, 1)]
                                     ).then_inc(self.s_counted, 1)

    def squares(self, act, b, slot, free):
        act.wait_ge(free, b)
        self.nc.scalar.activation(self.square[:, slot, :], self.block[:, :], ACT.Square,
                                  bias=self.minus_block[:, bass.ds(b, 1)]).then_inc(self.s_square, 1)

    def marks_on_act(self, act, squared, take, free):
        nc = self.nc
        nc.scalar.activation(self.square[:, 0, :], self.block[:, :], ACT.Square,
                             bias=self.minus_block[:, 0:1]).then_inc(self.s_square, 1)
        with act.Fori(0, NB // 2) as i:
            for u in range(2):
                b = i * 2 + u
                self.squares(act, b + 1, 1 - u, free)
                act.wait_ge(self.s_square, squared + b + 1)
                take(b, u)
        act.wait_ge(self.s_square, squared + NB)
        take(NB - 1, 0)

    def count_on_act(self, act):
        def take(b, slot):
            self.nc.scalar.activation(self.square[:, slot, :], self.square[:, slot, :], ACT.Relu, scale=-1.0,
                                      bias=self.one[:, :], accum_out=self.per_block[:, bass.ds(b, 1)]
                                      ).then_inc(self.s_counted, 1)
        self.marks_on_act(act, 0, take, self.s_counted)

    def sum_up(self, pe):
        pe.wait_ge(self.s_counted, NB + 1)
        self.nc.tensor.matmul(self.sums[:, 0:NB], self.lower[:, :], self.per_block[:, :], start=True, stop=True
                              ).then_inc(self.s_sums, 1)
        self.nc.tensor.matmul(self.sums[:, 64:64 + NB], self.ones[:, :], self.per_block[:, :], start=True, stop=True
                              ).then_inc(self.s_sums, 1)

    def bases(self, dve, step):
        nc = self.nc
        total, groups_i, groups, end, base = (t[:, :] for t in (self.total, self.groups_i, self.groups, self.end, self.base))
        dve.wait_ge(self.s_sums, 2)
        step(nc.vector.tensor_copy(total, self.sums[:, 64:64 + NB]))
        step(nc.vector.tensor_scalar(groups_i, total, float(SLOTS - 1), None, ALU.add))
        step(nc.vector.tensor_scalar(groups_i, groups_i, 9, None, ALU.logical_shift_right))
        step(nc.vector.tensor_copy(groups, groups_i))
        step(nc.vector.memset(total, 1.0))
        step(nc.vector.tensor_tensor_scan(end, total, groups, 0.0, ALU.mult, ALU.add))
        step(nc.vector.tensor_tensor(base, end, groups, ALU.subtract))
        step(nc.vector.tensor_scalar(base, base, float(SLOTS), -1.0, ALU.mult, ALU.add))
        step(nc.vector.tensor_tensor(base, base, self.sums[:, 0:NB], ALU.add))
        step(nc.vector.memset(self.blk[:, :], 0.0))
        step(nc.vector.memset(self.run[:, :], 1.0))
        dve.sem_inc(self.s_end, 1)
        dve.sem_inc(self.s_pos, 2)

    def group_blocks(self, dve, b):
        dve.wait_ge(self.s_end, b + 1)
        self.nc.vector.scalar_tensor_tensor(self.blk[:, :], self.group_no[:, :], self.end[:, bass.ds(b, 1)],
                                            self.blk[:, :], ALU.is_ge, ALU.add).then_inc(self.s_end, 1)

    def mark_on_act(self, act, squared):
        def take(b, slot):
            act.wait_ge(self.s_pos, b + 1)
            self.nc.scalar.activation(self.hit[:, slot, :], self.square[:, slot, :], ACT.Relu, scale=-1.0,
                                      bias=self.one[:, :]).then_inc(self.s_hit, 1)
        self.marks_on_act(act, squared, take, self.s_hit)

    def number(self, dve, b, slot):
        dve.wait_ge(self.s_hit, b + 2)
        dve.wait_ge(self.s_pos, b + 2)
        self.nc.vector.tensor_tensor_scan(self.run[:, :], self.hit[:, slot, :], self.hit[:, slot, :],
                                          self.base[:, bass.ds(b, 1)], ALU.add, ALU.bypass).then_inc(self.s_run, 1)

    def pick(self, dve, b, slot, passed):
        wait_alone(dve, self.s_run, b + 1, passed)
        self.nc.vector.copy_predicated(self.pos[:, :], self.hit[:, slot, :], self.run[:, :]).then_inc(self.s_pos, 1)

    def finish(self, dve, step):
        nc = self.nc
        dve.wait_ge(self.s_end, NB + 1)
        step(nc.vector.tensor_scalar(self.blk[:, :], self.blk[:, :], float(NB - 1), None, ALU.min))
        step(nc.vector.tensor_copy(self.block_of[:, :], self.blk[:, :]))
        step(nc.vector.tensor_scalar(self.first_of[:, :], self.blk[:, :], float(P), None, ALU.mult))
        dve.wait_ge(self.s_pos, NB + 2)
        step(nc.vector.tensor_copy(self.place[:, :], self.pos[:, :]))


def gnn_kernel(nc, h, out):
    dram = lambda name, shape, dt: nc.dram_tensor(name, shape, dt).ap()
    counts = dram("counts", ((NB + 1) * STRIP, 1), F32)
    strips8 = dram("strips8", (NB, P, NB * P), U8)
    cheb = dram("cheb", (P, NB, K, D), F32)
    z_table = dram("z_table", (Z, 2 * EM), F32)
    u_table = dram("u_table", (NP, UW), F32)
    r_table = dram("r_table", (NP * NR, D), F32)
    sorted1 = dram("sorted1", ((NGS + AHEAD) * SLOTS, R1), F32)
    sorted2 = dram("sorted2", ((NGS + AHEAD) * SLOTS, R2), F32)

    def strip32(j):
        return counts[bass.ds(j * STRIP, STRIP), :].rearrange("(p c) o -> p (c o)", p=P)[:, 0:NP]

    ctx = ExitStack()
    with ctx:
        def keep_sem(name):
            return ctx.enter_context(nc.semaphore(name))

        def sb(name, shape, dt, c=ctx):
            return c.enter_context(nc.sbuf_tensor(name, shape, dt))

        passed_sp, passed_act, passed_dve, passed_pe, passed_pool = passed = [
            keep_sem(f"passed_{e}") for e in ("sp", "act", "dve", "pe", "pool")]

        keys = sb("keys", [P, 2, T], I32)
        r_row = sb("r_row", [P, T], F32)
        weight = sb("weight", [P, T], F32)
        cutoff = sb("cutoff", [P, T], F32)
        place = [sb(f"place{n}", [P, T], I32) for n in (1, 2)]
        block_of = [sb(f"block_of{n}", [P, NGS + AHEAD], I32) for n in (1, 2)]
        first_of = [sb(f"first_of{n}", [P, NGS + AHEAD], F32) for n in (1, 2)]
        e_parts = sb("e_parts", [P, NB, 3 * EM], BF16)
        x_sb = sb("x_sb", [P, NB, D], F32)
        outdeg = sb("outdeg", [P, NB], F32)
        many = sb("many", [1, 1], I32)
        before = sb("before", [P, GC * P], F32)
        eye = sb("eye", [P, P], F32)

        edges2 = keys, r_row, weight, place[1], sorted2
        with stage(nc, "clear") as (sem, c1):
            zeros = sb("zeros", [P, NP], F32, c1)
            fill2 = sb("fill2", [P, (NGS + AHEAD) * G, R2], F32, c1)
            half_pi = sb("half_pi", [P, 1], F32, c1)
            below = sb("below", [P, T], F32, c1)
            s_keys, s_xin, s_edge = sem("s_keys"), sem("s_xin"), sem("s_edge")
            s_zero, s_fill, s_clear, s_ones, s_eye0 = (
                sem("s_zero"), sem("s_fill"), sem("s_clear"), sem("s_ones"), sem("s_eye0"))
            s_masks, s_cos_in, s_cos, s_chain1 = sem("s_masks"), sem("s_cos_in"), sem("s_cos"), sem("s_chain1")
            lower = sb("lower", [P, P], F32, c1)
            ones = sb("ones", [P, P], F32, c1)
            block_no = sb("block_no", [P, NB], F32, c1)
            minus_block = sb("minus_block", [P, NB], F32, c1)
            group_no = sb("group_no", [P, NGS + AHEAD], F32, c1)
            sums = c1.enter_context(nc.psum_tensor("sums", [P, 512], F32))
            one = sb("one", [P, 1], F32, c1)
            shared = (block_no, minus_block, group_no, sums, lower, ones, one,
                      sb("srt_shifted", [P, T], I32, c1), sb("srt_hit", [P, 2, T], mybir.dt.int16, c1),
                      sb("srt_square", [P, 2, T], BF16, c1), sb("srt_run", [P, T], F32, c1), sb("srt_pos", [P, T], F32, c1))
            by_src, by_dst = (CountingSort(nc, sb, c1, str(n + 1), sem, keys[:, n, :], shared, place[n], block_of[n],
                                           first_of[n]) for n in range(2))

            def blocks_in_pairs(eng, body):
                with eng.Fori(0, NB // 2) as i:
                    for u in range(2):
                        body(i * 2 + u, u)
                body(NB - 1, 0)
            s_iota = sem("s_iota")
            with nc.Block() as block:
                @block.sync
                def _(sp):
                    sp.dma_start(keys[:, :, :], h["key_cols"]).then_inc(s_keys, 16)
                    sp.dma_start(x_sb[:, :, :], h["x"]).then_inc(s_xin, 16)
                    sp.dma_start(cutoff[:, :], h["distance"]).then_inc(s_edge, 16)
                    sp.dma_start(weight[:, :], h["weight"]).then_inc(s_edge, 16)
                    sp.dma_start(place[0][:, :], h["relation"]).then_inc(s_edge, 16)
                    sp.wait_ge(s_zero, 1)
                    with sp.Fori(0, NB) as j:
                        sp.dma_start(strip32(j), zeros[:, :]).then_inc(s_clear, 16)
                    sp.dma_start(counts[NB * STRIP:NB * STRIP + GC * P, :].rearrange("(p c) o -> p (c o)", p=P),
                                 zeros[:, 0:GC]).then_inc(s_clear, 16)
                    sp.wait_ge(s_fill, 2)
                    sp.dma_start(sorted2.rearrange("(p r) f -> p (r f)", p=P),
                                 fill2[:, :, :].rearrange("p r f -> p (r f)")).then_inc(s_clear, 16)
                    sp.wait_ge(s_keys, 16)
                    sp.wait_ge(s_xin, 16)
                    sp.wait_ge(s_clear, 16 * (NB + 1 + 1))

                @block.gpsimd
                def _(pool):
                    pool.memset(before[:, :], 1.0).then_inc(s_ones, 1)
                    pool.memset(ones[:, :], 1.0).then_inc(s_ones, 1)
                    pool.memset(eye[:, :], 0.0).then_inc(s_eye0, 1)
                    pool.iota(block_no[:, :], pattern=[[1, NB]], base=0, channel_multiplier=0,
                              allow_small_or_imprecise_dtypes=True).then_inc(s_iota, 1)
                    pool.iota(group_no[:, :], pattern=[[1, NGS + AHEAD]], base=0, channel_multiplier=0,
                              allow_small_or_imprecise_dtypes=True).then_inc(s_iota, 1)
                    pool.wait_ge(s_ones, 2)
                    pool.affine_select(out=lower[:, :], in_=ones[:, :], compare_op=ALU.is_gt, fill=0.0, base=0,
                                       pattern=[[1, P]], channel_multiplier=-1).then_inc(s_iota, 1)
                    pool.affine_select(out=before[:, :], in_=before[:, :], compare_op=ALU.is_ge, fill=BEFORE, base=0,
                                       pattern=[[1, GC * P]], channel_multiplier=-1).then_inc(s_masks, 1)
                    pool.wait_ge(s_eye0, 1)
                    pool.affine_select(out=eye[:, :], in_=eye[:, :], compare_op=ALU.not_equal, fill=1.0,
                                       base=0, pattern=[[-1, P]], channel_multiplier=1).then_inc(s_masks, 1)

                @block.scalar
                def _(act):
                    act.wait_ge(s_cos_in, 1)
                    nc.scalar.activation(cutoff[:, :], cutoff[:, :], ACT.Sin, bias=half_pi[:, :],
                                         scale=-PI / 6.0).then_inc(s_cos, 1)
                    act.wait_ge(by_src.s_ready, 1)
                    by_src.count_on_act(act)
                    act.wait_ge(by_src.s_counted, NB + 1)
                    act.wait_ge(by_dst.s_ready, 1)
                    act.sem_inc(by_dst.s_hit, 1)
                    by_dst.mark_on_act(act, 0)
                    act.wait_ge(by_dst.s_hit, NB + 1)
                    act.wait_ge(by_dst.s_pos, NB + 2)
                    act.sem_inc(by_src.s_hit, 1)
                    by_src.mark_on_act(act, NB)

                @block.tensor
                def _(pe):
                    pe.wait_ge(s_iota, 3)
                    by_dst.sum_up(pe)
                    pe.wait_ge(by_src.s_ready, 2)
                    by_src.sum_up(pe)

                @block.vector
                def _(dve):
                    nc.vector.memset(zeros[:, :], 0.0).then_inc(s_zero, 1)
                    nc.vector.memset(fill2[:, :, :], 0.0).then_inc(s_fill, 1)
                    dve.wait_ge(s_fill, 1)
                    nc.vector.memset(fill2[:, :, R2 - 1:R2], BLANK).then_inc(s_fill, 1)
                    step = in_order(dve, s_chain1)
                    dve.wait_ge(s_edge, 48)
                    dve.wait_ge(s_keys, 16)
                    step(nc.vector.memset(half_pi[:, :], PI / 2.0))
                    step(nc.vector.tensor_scalar(below[:, :], cutoff[:, :], 6.0, None, ALU.is_lt))
                    step(nc.vector.tensor_scalar(cutoff[:, :], cutoff[:, :], 6.0, None, ALU.min))
                    dve.sem_inc(s_cos_in, 1)
                    step(nc.vector.scalar_tensor_tensor(r_row[:, :], keys[:, 0, :], float(NR), place[0][:, :],
                                                        ALU.mult, ALU.add))
                    dve.wait_ge(s_cos, 1)
                    step(nc.vector.tensor_scalar(cutoff[:, :], cutoff[:, :], 1.0, 0.5, ALU.add, ALU.mult))
                    step(nc.vector.tensor_tensor(cutoff[:, :], cutoff[:, :], below[:, :], ALU.mult))
                    dve.wait_ge(s_iota, 3)
                    step(nc.vector.memset(one[:, :], 1.0))
                    step(nc.vector.tensor_scalar(minus_block[:, :], block_no[:, :], -1.0, None, ALU.mult))
                    by_src.start(dve, step)
                    by_dst.start(dve, step)
                    with dve.Fori(0, NB) as b:
                        by_dst.count_on_dve(dve, b)
                    by_dst.bases(dve, step)
                    dve.sem_inc(by_src.s_ready, 1)

                    def places(srt):
                        def body(b, u):
                            srt.number(dve, b, u)
                            srt.group_blocks(dve, b)
                            srt.pick(dve, b, u, passed_dve)
                        blocks_in_pairs(dve, body)
                        srt.finish(dve, step)
                    places(by_dst)
                    by_src.bases(dve, step)
                    places(by_src)

        with stage(nc, "count") as (sem, c2):
            fill1 = sb("fill1", [P, FILL, R1], F32, c2)
            keyf = sb("keyf", [P, 2, T], F32, c2)
            cell = sb("cell", [P, T], I32, c2)
            cell_t = sb("cell_t", [P, T], I32, c2)
            rows = sb("rows", [P, 2, 2, GC * P], I32, c2)
            equal = [[sb(f"equal{v}_{j}", [P, (GC - j) * P], BF16, c2) for j in range(GC)] for v in range(2)]
            found = sb("found", [P, 2, GC], F32, c2)
            summed = sb("summed", [P, 2, GC], F32, c2)
            amount = sb("amount", [P, 2, GC], F32, c2)
            late = sb("late", [P, 2, GC], I32, c2)
            where = sb("where", [P, 2, GC], I32, c2)
            spare = sb("spare", [P, GC], I32, c2)
            apart = sb("apart", [P, ON_ACT, GC * P], BF16, c2)
            minus_dst = sb("minus_dst", [P, T], F32, c2)
            one_f = sb("one_f", [P, 1], F32, c2)
            s_eqa, s_apart = sem("s_eqa"), sem("s_apart")
            one_col = sb("one_col", [P, 1], BF16, c2)
            no_col = sb("no_col", [P, 1], BF16, c2)
            earlier = [c2.enter_context(nc.psum_tensor(f"earlier{v}", [P, 512], F32)) for v in range(2)]
            s_prep, s_spare, s_blank, s_fill = sem("s_prep"), sem("s_spare"), sem("s_blank"), sem("s_fill")
            s_rows = [sem("s_rows0"), sem("s_rows1")]
            s_eqd, s_eqs = sem("s_eqd"), sem("s_eqs")
            s_earlier = sem("s_earlier")
            s_summed = sem("s_summed")
            s_late, s_cellcp, s_amount, s_where = sem("s_late"), sem("s_cellcp"), sem("s_amount"), sem("s_where")
            s_added = sem("s_added")
            s_slot = sem("s_slot")
            pack2 = RecordsOfLayer2(nc, sb, c2, "a", sem, edges2, AT_COUNT, 0, IN_COUNT)

            def loop(eng, body, start=0):
                with eng.Fori(start, NC // 2) as i:
                    for v in range(2):
                        body(i, i * 2 + v, v)
            with nc.Block() as block:
                @block.scalar
                def _(act):
                    fills = (NGS + AHEAD) * G // FILL
                    act.wait_ge(s_fill, 2)
                    act.sem_inc(s_eqa, ON_ACT)
                    act.wait_ge(s_prep, 5)

                    def blank(j):
                        act.dma_start(sorted1.rearrange("(p r) f -> p (r f)", p=P)[:, bass.ds(j * (FILL * R1), FILL * R1)],
                                      fill1[:, :, :].rearrange("p r f -> p (r f)")).then_inc(s_blank, 16)

                    def compare_dst(i, g, v):
                        wait_alone(act, s_rows[v], 16 * (i + 1), passed_act)
                        wait_alone(act, s_earlier, g + 1, passed_act)
                        act.wait_ge(s_eqa, (g + 1) * ON_ACT)
                        for j in range(ON_ACT):
                            nc.scalar.activation(apart[:, j, 0:(GC - 1 - j) * P], rows[:, v, 1, (j + 1) * P:], ACT.Square,
                                                 bias=minus_dst[:, bass.ds(g * GC + j, 1)]).then_inc(s_apart, 1)
                        for j in range(ON_ACT):
                            act.wait_ge(s_apart, g * ON_ACT + j + 1)
                            nc.scalar.activation(equal[v][j][:, P:], apart[:, j, 0:(GC - 1 - j) * P], ACT.Relu, scale=-1.0,
                                                 bias=one_f[:, :]).then_inc(s_eqa, 1)
                    for v in range(2):
                        compare_dst(0, v, v)
                        pack2.pack(act, 0, v, v, True)
                    blank(0)
                    with act.Fori(1, fills) as i:
                        for v in range(2):
                            compare_dst(i, i * 2 + v, v)
                            pack2.pack(act, i, i * 2 + v, v, False)
                        blank(i)

                    def rest(i, g, v):
                        compare_dst(i, g, v)
                        pack2.pack(act, i, g, v, False)
                    loop(act, rest, fills)
                    act.wait_ge(s_blank, 16 * fills)

                @block.sync
                def _(sp):
                    def load(i, g, v):
                        if g is not v:
                            wait_alone(sp, s_eqs, (g - 1) * GC, passed_sp)
                        src = h["key_rows"][bass.ds(g, 1), :].rearrange("o (k c) -> o k c", k=2)
                        sp.dma_start(rows[:, v, :, :], src.to_broadcast([P, 2, GC * P])).then_inc(s_rows[v], 16)
                    for v in range(2):
                        load(0, v, v)
                    loop(sp, load, 1)

                @block.tensor
                def _(pe):
                    pe.wait_ge(s_prep, 3)

                    def sum_earlier(i, g, v):
                        pe.wait_ge(s_summed, g + 1)
                        pe.wait_ge(s_eqs, (g + 1) * GC)
                        nc.tensor.matmul(earlier[v][:, 0:1], equal[v][0][:, 0:P], no_col[:, :], start=True, stop=True)
                        for k in range(1, GC):
                            for j in range(k):
                                mm = nc.tensor.matmul(earlier[v][:, k:k + 1], equal[v][j][:, (k - j) * P:(k - j + 1) * P],
                                                      one_col[:, :], start=(j == 0), stop=(j == k - 1))
                        mm.then_inc(s_earlier, 1)
                    loop(pe, sum_earlier)

                @block.vector
                def _(dve):
                    for s in (s_earlier, s_summed, s_slot):
                        dve.sem_inc(s, 2)
                    src, dst = keys[:, 0, 0:T], keys[:, 1, 0:T]
                    step = in_order(dve, s_prep)
                    step(nc.vector.memset(one_col[:, :], 1.0))
                    step(nc.vector.memset(no_col[:, :], 0.0))
                    step(nc.vector.tensor_copy(keyf[:, :, :], keys[:, :, 0:T]))
                    step(nc.vector.tensor_scalar(minus_dst[:, :], keyf[:, 1, :], -1.0, None, ALU.mult))
                    step(nc.vector.memset(one_f[:, :], 1.0))
                    nc.vector.memset(fill1[:, :, 0:R1 - 1], 0.0).then_inc(s_fill, 1)
                    nc.vector.memset(fill1[:, :, R1 - 1:R1], BLANK).then_inc(s_fill, 1)
                    blocks = 0x1F80
                    c, t = cell[:, :], cell_t[:, :]
                    step(nc.vector.tensor_scalar(c, dst, blocks, 13, ALU.bitwise_and, ALU.logical_shift_left))
                    step(nc.vector.tensor_scalar(t, src, P - 1, 13, ALU.bitwise_and, ALU.logical_shift_left))
                    step(nc.vector.tensor_tensor(c, c, t, ALU.bitwise_or))
                    step(nc.vector.tensor_scalar(t, src, blocks, None, ALU.bitwise_and))
                    step(nc.vector.tensor_tensor(c, c, t, ALU.bitwise_or))
                    step(nc.vector.tensor_scalar(t, dst, P - 1, None, ALU.bitwise_and))
                    step(nc.vector.tensor_tensor(c, c, t, ALU.bitwise_or))
                    dve.wait_ge(s_spare, 1)

                    def compare_dst(i, g, v):
                        dve.wait_ge(s_rows[v], 16 * (i + 1))
                        dve.wait_ge(s_earlier, g + 1)
                        for j in range(GC):
                            w = P if j < ON_ACT else (GC - j) * P
                            nc.vector.scalar_tensor_tensor(
                                equal[v][j][:, 0:w], rows[:, v, 1, j * P:j * P + w], keyf[:, 1, bass.ds(g * GC + j, 1)],
                                before[:, 0:w], ALU.is_equal, ALU.mult).then_inc(s_eqd, 1)

                    def compare_src(g, v):
                        dve.wait_ge(s_summed, g + 1)
                        for j in range(GC):
                            dve.wait_ge(s_eqd, g * GC + j + 1)
                            if j < ON_ACT:
                                dve.wait_ge(s_eqa, (g + 1) * ON_ACT + j + 1)
                            nc.vector.scalar_tensor_tensor(
                                equal[v][j][:, :], rows[:, v, 0, j * P:], keyf[:, 0, bass.ds(g * GC + j, 1)],
                                equal[v][j][:, :], ALU.is_equal, ALU.mult, accum_out=found[:, v, j:j + 1]
                                ).then_inc(s_eqs, 1)

                    def name_cells(g, v):
                        dve.wait_ge(s_slot, g + 1)
                        nc.vector.tensor_copy(where[:, v, :], cell[:, bass.ds(g * GC, GC)]).then_inc(s_cellcp, 1)
                        dve.wait_ge(s_eqs, (g + 1) * GC)
                        nc.vector.tensor_copy(amount[:, v, :], found[:, v, :]).then_inc(s_amount, 1)
                        dve.wait_ge(s_earlier, g + 3)
                        nc.vector.scalar_tensor_tensor(summed[:, v, :], earlier[v][:, 0:GC], BEFORE, found[:, v, :],
                                                       ALU.mult, ALU.add).then_inc(s_summed, 1)
                        dve.wait_ge(s_summed, g + 3)
                        nc.vector.tensor_scalar(late[:, v, :], summed[:, v, :], BEFORE, None,
                                                ALU.is_ge).then_inc(s_late, 1)
                        wait_alone(dve, s_cellcp, g + 1, passed_dve)
                        wait_alone(dve, s_amount, g + 1, passed_dve)
                        wait_alone(dve, s_late, g + 1, passed_dve)
                        nc.vector.copy_predicated(where[:, v, :], late[:, v, :], spare[:, :]).then_inc(s_where, 1)

                    def body(i, g, v):
                        compare_dst(i, g, v)
                        name_cells(g - 1, 1 - v)
                        compare_src(g, v)
                    compare_dst(0, 0, 0)
                    compare_src(0, 0)
                    body(0, 1, 1)
                    loop(dve, body, 1)
                    name_cells(NC - 1, 1)

                @block.gpsimd
                def _(pool):
                    pool.iota(spare[:, :], pattern=[[P, GC]], base=NB * STRIP, channel_multiplier=1).then_inc(s_spare, 1)

                    def add(i, g, v):
                        wait_alone(pool, s_where, g + 1, passed_pool)
                        for j in range(GC):
                            pool.indirect_dma_start(
                                out=counts,
                                out_offset=bass.IndirectOffsetOnAxis(ap=where[:, v, j:j + 1].bitcast(U32), axis=0),
                                in_=amount[:, v, j:j + 1], in_offset=None,
                                compute_op=ALU.add).then_inc(s_added, 16)
                        pack2.put(pool, g, v, passed_pool)
                        pool.wait_ge(s_added, 16 * GC * (g + 1))
                        pool.sem_inc(s_slot, 1)
                    loop(pool, add)
                    pack2.finish(pool)

        with stage(nc, "cast") as (sem, c3):
            U = 4
            wide = sb("wide", [P, U, NP], F32, c3)
            narrow = sb("narrow", [P, U, NP], FP8, c3)
            part = sb("part", [P, U, NB], F32, c3)
            over = sb("over", [P, NB], F32, c3)
            over1 = sb("over1", [P, 1], F32, c3)
            limit = sb("limit", [P, 1], F32, c3)
            ones1 = sb("ones1", [P, 1], F32, c3)
            pack2 = RecordsOfLayer2(nc, sb, c3, "b", sem, edges2, AT_CAST, IN_COUNT, IN_CAST)
            over_p = c3.enter_context(nc.psum_tensor("over_p", [P, 512], F32))
            s_limit, s_over, s_over1, s_overp, s_many = (
                sem("s_limit"), sem("s_over"), sem("s_over1"), sem("s_overp"), sem("s_many"))
            s_in = [sem(f"s_in{u}") for u in range(U)]
            s_saved = [sem(f"s_saved{u}") for u in range(U)]
            s_cast, s_sum, s_deg = sem("s_cast"), sem("s_sum"), sem("s_deg")
            with nc.Block() as block:
                @block.sync
                def _(sp):
                    def load(j, u, first):
                        if not first:
                            wait_alone(sp, s_cast, j - U + 1, passed_sp)
                            wait_alone(sp, s_over, j - U + 1, passed_sp)
                            wait_alone(sp, s_sum, j - U + 1, passed_sp)
                        sp.dma_start(wide[:, u, :], strip32(j)).then_inc(s_in[u], 16)
                    for u in range(U):
                        load(u, u, True)
                    with sp.Fori(1, NB // U) as i:
                        for u in range(U):
                            load(i * U + u, u, False)
                    load(NB - 1, 0, False)

                @block.scalar
                def _(act):
                    def cast(i, j, u, first):
                        act.wait_ge(s_in[u], 16 * (i + 1))
                        if not first:
                            wait_alone(act, s_saved[u], 16 * i, passed_act)
                        nc.scalar.activation(narrow[:, u, :], wide[:, u, :], ACT.Copy, saturate=False).then_inc(s_cast, 1)
                        act.wait_ge(s_sum, j + 1)
                        nc.scalar.activation(wide[:, u, :], wide[:, u, :], ACT.Relu, bias=limit[:, :],
                                             accum_out=over[:, bass.ds(j, 1)]).then_inc(s_over, 1)
                        wait_alone(act, s_cast, j + 1, passed_act)
                        act.dma_start(strips8[bass.ds(j, 1), :, :].rearrange("o p c -> p (o c)"),
                                      narrow[:, u, :].bitcast(U8)).then_inc(s_saved[u], 16)
                    act.wait_ge(s_limit, 1)
                    for u in range(U):
                        cast(0, u, u, True)
                        pack2.pack(act, u // 2, u, u % 2, u < 2)
                    with act.Fori(1, NB // U) as i:
                        for u in range(U):
                            cast(i, i * U + u, u, False)
                            pack2.pack(act, i * 2 + u // 2, i * U + u, u % 2, False)
                    cast(NB // U, NB - 1, 0, False)
                    act.wait_ge(s_saved[0], 16 * (NB // U + 1))
                    for u in range(1, U):
                        act.wait_ge(s_saved[u], 16 * (NB // U))

                @block.gpsimd
                def _(pool):
                    pack2.put_all(pool, passed_pool)
                    pack2.finish(pool)

                @block.tensor
                def _(pe):
                    pe.wait_ge(s_over1, 1)
                    nc.tensor.matmul(over_p[0:1, 0:1], over1[:, :], ones1[:, :], start=True, stop=True).then_inc(s_overp, 1)

                @block.vector
                def _(dve):
                    nc.vector.memset(ones1[:, :], 1.0)
                    nc.vector.memset(limit[:, :], -MANY).then_inc(s_limit, 1)
                    nc.vector.memset(outdeg[:, :], 0.0).then_inc(s_deg, 1)

                    def degrees(i, j, u):
                        dve.wait_ge(s_in[u], 16 * (i + 1))
                        nc.vector.tensor_reduce(part[:, u, :], wide[:, u, :].rearrange("p (b c) -> p b c", c=P),
                                                AX.X, ALU.add).then_inc(s_sum, 1)
                        dve.wait_ge(s_sum, j + 1)
                        dve.wait_ge(s_deg, j + 1)
                        nc.vector.tensor_tensor(outdeg[:, :], outdeg[:, :], part[:, u, :], ALU.add).then_inc(s_deg, 1)
                    with dve.Fori(0, NB // U) as i:
                        for u in range(U):
                            degrees(i, i * U + u, u)
                    degrees(NB // U, NB - 1, 0)
                    dve.wait_ge(s_over, NB)
                    nc.vector.tensor_reduce(over1[:, :], over[:, :], AX.X, ALU.add).then_inc(s_over1, 1)
                    dve.wait_ge(s_overp, 1)
                    nc.vector.tensor_scalar(many[:, :], over_p[0:1, 0:1], 0.0, None, ALU.is_gt).then_inc(s_many, 1)

        layer0(nc, h, sb, strips8, strip32, many, cheb, x_sb, outdeg, eye, passed, keys, cutoff, place,
               edges2, sorted1, z_table, u_table, e_parts)
        with ExitStack() as c78:
            agg = sb("agg1", [P, NB, MW], F32, c78)
            layer1_edges(nc, h, sb, sorted1, u_table, e_parts, block_of[0], first_of[0], eye, agg, passed)
            end_of_layer1(nc, h, sb, agg, x_sb)
        table_of_layer2(nc, h, sb, r_table, x_sb, eye, passed_pe, passed_sp)
        with ExitStack() as c9:
            agg = sb("agg2", [P, NB, D], F32, c9)
            layer2_edges(nc, h, sb, sorted2, r_table, block_of[1], first_of[1], agg, passed)
            end_of_layer2(nc, h, sb, agg, x_sb)
        layer3(nc, h, sb, strips8, strip32, many, x_sb, outdeg, eye, passed)
        with stage(nc, "store") as (sem, c9):
            s_o = sem("s_o")
            with nc.Block() as block:
                @block.sync
                def _(sp):
                    sp.dma_start(out, x_sb[:, :, :]).then_inc(s_o, 16)
                    sp.wait_ge(s_o, 16)


def in_order(eng, done):
    count = [0]

    def step(instruction):
        count[0] += 1
        instruction.then_inc(done, 1)
        eng.wait_ge(done, count[0])
    return step


def wide_ap(col):
    return col.unsqueeze(2).to_broadcast([P, NB, D])


def row_ap(row):
    return row.unsqueeze(1).to_broadcast([P, NB, D])


def normalize(nc, step, sqrt_of, x, sq, col, eps_col):
    mean, var = col[:, 0, :], col[:, 1, :]
    step(nc.vector.tensor_reduce(mean, x, AX.X, ALU.add))
    step(nc.vector.tensor_scalar(mean, mean, 1.0 / D, None, ALU.mult))
    step(nc.vector.tensor_tensor(x, x, wide_ap(mean), ALU.subtract))
    step(nc.vector.tensor_tensor(sq, x, x, ALU.mult))
    step(nc.vector.tensor_reduce(var, sq, AX.X, ALU.add))
    step(nc.vector.tensor_scalar(var, var, 1.0 / D, 1e-5, ALU.mult, ALU.add))
    sqrt_of(var)
    step(nc.vector.reciprocal(var, var))
    step(nc.vector.tensor_tensor(x, x, wide_ap(var), ALU.mult))


def layer0(nc, h, sb, strips8, strip32, many, cheb, x_sb, outdeg, eye, passed, keys, cutoff, place,
           edges2, sorted1, z_table, u_table, e_parts):
    passed_sp, passed_act, passed_dve, passed_pe, passed_pool = passed
    U = 7
    W3 = 3 * D
    with stage(nc, "cheb") as (sem, c4):
        dis = sb("dis", [P, NB], F32, c4)
        dis_m1 = sb("dis_m1", [P, NB], F32, c4)
        dis_m2 = sb("dis_m2", [P, NB], F32, c4)
        has = sb("has", [P, NB], F32, c4)
        term = sb("term", [P, 2, NB, D], F32, c4)
        parts = sb("parts", [P, 2, NB, W3], BF16, c4)
        cbuf = sb("cbuf", [P, U, NP], FP8, c4)
        y = sb("y", [P, U, D], F32, c4)
        scaled = sb("scaled", [P, 2, NB, D], F32, c4)
        none = sb("none", [P, W3 - D], BF16, c4)
        r = sb("r", [P, U, D], F32, c4)
        acc = [c4.enter_context(nc.psum_tensor(f"acc{u}", [P, 512], F32)) for u in range(U)]
        s_c = [sem(f"s_c{u}") for u in range(U)]
        s_wide, s_none = sem("s_wide"), sem("s_none")
        wide = cbuf[:, :, :].rearrange("p u c -> p (u c)").bitcast(F32)[:, 0:NP]
        s_strip, s_accfree, s_parts, s_term = sem("s_strip"), sem("s_accfree"), sem("s_parts"), sem("s_term")
        s_kept = [sem("s_kept0"), sem("s_kept1")]
        s_prep4, s_root, s_root_in = sem("s_prep4"), sem("s_root"), sem("s_root_in")
        s_y, s_v, s_hi, s_r, s_mid = sem("s_y"), sem("s_v"), sem("s_hi"), sem("s_r"), sem("s_mid")
        pack2 = RecordsOfLayer2(nc, sb, c4, "c", sem, edges2, AT_CHEB, IN_COUNT + IN_CAST, IN_CHEB)
        record = sb("record1", [P, 4, G, R1], F32, c4)
        row = sb("row1", [P, 4, G], I32, c4)
        s_packed = sem("s_packed1")
        s_put = [sem(f"s_put1_{b}") for b in range(4)]
        s_attr = [sem(f"s_attr1_{b}") for b in range(4)]
        with nc.Block() as block:
            @block.sync
            def _(sp):
                def load_wide(n0, j, first):
                    if not first:
                        wait_alone(sp, s_strip, n0 + j, passed_sp)
                    sp.dma_start(wide, strip32(j)).then_inc(s_wide, 16)

                def load(n0, rr, u, first):
                    if not first:
                        wait_alone(sp, s_strip, n0 + rr * U + u - U + 1, passed_sp)
                    sp.dma_start(cbuf[:, u, :].bitcast(U8), strips8[bass.ds(rr * U + u, 1), :, :].rearrange("o p c -> p (o c)")
                                 ).then_inc(s_c[u], 16)
                def keep(k, slot):
                    wait_alone(sp, s_term, NB * (k + 1), passed_sp)
                    sp.dma_start(cheb[:, :, bass.ds(k, 1), :].rearrange("p b k f -> p b (k f)"),
                                 term[:, slot, :, :]).then_inc(s_kept[slot], 16)

                def rest_of_pass(n0):
                    with sp.Fori(1, NB // U) as rr:
                        for u in range(U):
                            load(n0, rr, u, False)

                with sp.If(sp.value_load(many[0:1, 0:1], min_val=0, max_val=1) == 0):
                    for u in range(U):
                        load(0, 0, u, True)
                    rest_of_pass(0)
                    keep(0, 0)
                    with sp.Fori(0, (K - 2) // 2) as m:
                        for odd in range(2):
                            n0 = (m * 2 + 1 + odd) * NB
                            for u in range(U):
                                load(n0, 0, u, False)
                            keep(m * 2 + 1 + odd, 1 - odd)
                            rest_of_pass(n0)
                with sp.Else():
                    load_wide(0, 0, True)
                    with sp.Fori(1, NB) as j:
                        load_wide(0, j, False)
                    keep(0, 0)
                    with sp.Fori(0, (K - 2) // 2) as m:
                        for odd in range(2):
                            n0 = (m * 2 + 1 + odd) * NB
                            load_wide(n0, 0, False)
                            keep(m * 2 + 1 + odd, 1 - odd)
                            with sp.Fori(1, NB) as j:
                                load_wide(n0, j, False)
                keep(K - 1, 1)
                sp.wait_ge(s_kept[0], 16 * (K // 2))
                sp.wait_ge(s_kept[1], 16 * (K // 2))

            @block.tensor
            def _(pe):
                def strip(slot, n_div, n, u):
                    pe.wait_ge(s_c[u], 16 * (n_div + 1))
                    wait_alone(pe, s_accfree, n + 1, passed_pe)
                    for s in range(NB):
                        mm = nc.tensor.matmul(acc[u][:, 0:W3], cbuf[:, u, s * P:(s + 1) * P],
                                              parts[:, slot, s, :], start=(s == 0), stop=(s == NB - 1))
                    mm.then_inc(s_strip, 1)

                def wide_strip(slot, n, u):
                    wait_alone(pe, s_wide, 16 * (n + 1), passed_pe)
                    wait_alone(pe, s_accfree, n + 1, passed_pe)
                    nc.tensor.matmul(acc[u][:, D:W3], parts[:, slot, 0, 0:P], none[:, :], start=True, stop=True)
                    for s in range(NB):
                        mm = nc.tensor.matmul(acc[u][:, 0:D], wide[:, s * P:(s + 1) * P], scaled[:, slot, s, :],
                                              start=(s == 0), stop=(s == NB - 1))
                    mm.then_inc(s_strip, 1)

                def one_pass(k, slot, exact):
                    wait_alone(pe, s_parts, NB * k, passed_pe)
                    with pe.Fori(0, NB // U) as rr:
                        for u in range(U):
                            n = (k - 1) * NB + rr * U + u
                            if exact:
                                strip(slot, (k - 1) * (NB // U) + rr, n, u)
                            else:
                                wide_strip(slot, n, u)

                def passes(exact):
                    one_pass(1, 0, exact)
                    with pe.Fori(0, (K - 2) // 2) as m:
                        one_pass(m * 2 + 2, 1, exact)
                        one_pass(m * 2 + 3, 0, exact)
                pe.wait_ge(s_none, 1)
                with pe.If(pe.value_load(many[0:1, 0:1], min_val=0, max_val=1) == 0):
                    passes(True)
                with pe.Else():
                    passes(False)

            @block.scalar
            def _(act):
                act.wait_ge(s_root_in, 1)
                nc.scalar.activation(dis[:, :], dis[:, :], ACT.Sqrt).then_inc(s_root, 1)
                pack2.pack_all(act)

                def pack1(i, s, b, first):
                    if not first:
                        act.wait_ge(s_put[b], 16 * G * i)
                    cols = bass.ds(s * G, G)
                    for f, of in enumerate((cutoff[:, cols], keys[:, 1, cols], keys[:, 0, cols])):
                        nc.scalar.activation(record[:, b, :, R + f:R + f + 1].rearrange("p t o -> p (t o)"), of, ACT.Copy)
                    nc.scalar.activation(row[:, b, :], place[0][:, cols], ACT.Copy).then_inc(s_packed, 1)
                    act.dma_start(record[:, b, :, 0:R], h["attr"][:, cols, :]).then_inc(s_attr[b], 16)
                for b in range(4):
                    pack1(0, b, b, True)
                with act.Fori(1, NG // 4) as i:
                    for b in range(4):
                        pack1(i, i * 4 + b, b, False)

            @block.gpsimd
            def _(pool):
                pack2.put_all(pool, passed_pool)
                with pool.Fori(0, NG // 4) as i:
                    for b in range(4):
                        wait_alone(pool, s_packed, i * 4 + b + 1, passed_pool)
                        wait_alone(pool, s_attr[b], 16 * (i + 1), passed_pool)
                        for j in range(G):
                            pool.indirect_dma_start(
                                out=sorted1,
                                out_offset=bass.IndirectOffsetOnAxis(ap=row[:, b, j:j + 1].bitcast(U32), axis=0),
                                in_=record[:, b, j, :], in_offset=None).then_inc(s_put[b], 16)
                pack2.finish(pool)
                for b in range(4):
                    pool.wait_ge(s_put[b], 16 * G * (NG // 4))

            @block.vector
            def _(dve):
                step = in_order(dve, s_prep4)
                step(nc.vector.tensor_scalar(dis[:, :], outdeg[:, :], 1e-12, None, ALU.max))
                dve.sem_inc(s_root_in, 1)
                step(nc.vector.tensor_scalar(has[:, :], outdeg[:, :], 0.0, None, ALU.is_gt))
                dve.wait_ge(s_root, 1)
                step(nc.vector.reciprocal(dis[:, :], dis[:, :]))
                step(nc.vector.tensor_tensor(dis[:, :], dis[:, :], has[:, :], ALU.mult))
                step(nc.vector.tensor_scalar(dis_m1[:, :], dis[:, :], -1.0, None, ALU.mult))
                step(nc.vector.tensor_scalar(dis_m2[:, :], dis[:, :], -2.0, None, ALU.mult))
                step(nc.vector.tensor_copy(term[:, 0, :, :], x_sb[:, :, :]))
                step(nc.vector.memset(term[:, 1, :, :], 0.0))
                nc.vector.memset(none[:, :], 0.0).then_inc(s_none, 1)
                dve.sem_inc(s_accfree, U)

                def split(slot, b, u, n):
                    blk = lambda t: t[:, slot, bass.ds(b, 1), :].rearrange("p o f -> p (o f)")
                    hi, mid, lo = (parts[:, slot, bass.ds(b, 1), i * D:(i + 1) * D].rearrange("p o f -> p (o f)")
                                   for i in range(3))
                    dve.wait_ge(s_term, n + 1)
                    v = blk(scaled)
                    nc.vector.tensor_scalar(v, blk(term), dis[:, bass.ds(b, 1)], None, ALU.mult).then_inc(s_v, 1)
                    dve.wait_ge(s_v, n + 1)
                    nc.vector.tensor_copy(hi, v).then_inc(s_hi, 1)
                    dve.wait_ge(s_hi, n + 1)
                    nc.vector.tensor_tensor(r[:, u, :], v, hi, ALU.subtract).then_inc(s_r, 1)
                    dve.wait_ge(s_r, n + 1)
                    nc.vector.tensor_copy(mid, r[:, u, :]).then_inc(s_mid, 1)
                    dve.wait_ge(s_mid, n + 1)
                    nc.vector.tensor_tensor(lo, r[:, u, :], mid, ALU.subtract).then_inc(s_parts, 1)

                def block_of_term(k, rr, u, slot, scale):
                    b = rr * U + u
                    n = (k - 1) * NB + b
                    dve.wait_ge(s_strip, n + 1)
                    nc.vector.tensor_reduce(y[:, u, :], acc[u][:, 0:W3].rearrange("p (s f) -> p f s", f=D),
                                            AX.X, ALU.add).then_inc(s_y, 1)
                    dve.wait_ge(s_y, n + 1)
                    dve.sem_inc(s_accfree, 1)
                    t = term[:, slot, bass.ds(b, 1), :].rearrange("p o f -> p (o f)")
                    nc.vector.scalar_tensor_tensor(t, y[:, u, :], scale[:, bass.ds(b, 1)], t,
                                                   ALU.mult, ALU.subtract).then_inc(s_term, 1)
                    split(slot, b, u, n + NB)

                dve.sem_inc(s_term, NB)
                with dve.Fori(0, NB // U) as rr:
                    for u in range(U):
                        split(0, rr * U + u, u, rr * U + u)
                with dve.Fori(0, NB // U) as rr:
                    for u in range(U):
                        block_of_term(1, rr, u, 1, dis_m1)
                with dve.Fori(0, (K - 2) // 2) as m:
                    for odd in range(2):
                        wait_alone(dve, s_kept[odd], (m + 1) * 16, passed_dve)
                        with dve.Fori(0, NB // U) as rr:
                            for u in range(U):
                                block_of_term(m * 2 + 2 + odd, rr, u, odd, dis_m2)

    U = 4
    Q = K // 2
    with stage(nc, "out0") as (sem, c5):
        tin = sb("tin", [P, U, K, D], F32, c5)
        tT = sb("tT", [2 * D, 2, Q, P], F32, c5)
        w0 = sb("w0", [2 * D, Q, D], F32, c5)
        b0 = sb("b0", [P, D], F32, c5)
        o_sb = sb("o_sb", [P, NB, D], F32, c5)
        sq = sb("sq", [P, NB, D], F32, c5)
        col = sb("col", [P, 2, NB], F32, c5)
        turned = [[c5.enter_context(nc.psum_tensor(f"turned{a}{b}", [P, 512], F32)) for b in range(2)] for a in range(2)]
        acc = [c5.enter_context(nc.psum_tensor(f"acc5_{u}", [P, 512], F32)) for u in range(2)]
        s_t = [sem(f"s_t{u}") for u in range(U)]
        s_w0 = sem("s_w0")
        s_turn, s_copyA, s_copyB, s_out0, s_ofree, s_tfree = (
            sem("s_turn"), sem("s_copyA"), sem("s_copyB"), sem("s_out0"), sem("s_ofree"), sem("s_tfree"))
        s_ln0, s_sq0, s_sqi0 = sem("s_ln0"), sem("s_sq0"), sem("s_sqi0")
        pack2 = RecordsOfLayer2(nc, sb, c5, "d", sem, edges2, AT_OUT0, T - IN_OUT0, IN_OUT0)
        emb = sb("emb", [Z, 2 * EM], F32, c5)
        embT = sb("embT", [EM, Z], F32, c5)
        adapt = sb("adapt", [EM, EM], F32, c5)
        kind = sb("kind", [P, NB], I32, c5)
        mult = sb("mult", [P, NB], F32, c5)
        of_node = sb("of_node", [P, NB, 2 * EM], F32, c5)
        u_rows = sb("u_rows", [P, NB, UW], F32, c5)
        adapted = c5.enter_context(nc.psum_tensor("adapted", [P, 512], F32))
        s_small, s_adapted, s_emb, s_ztab, s_node, s_rows6, s_tab6, s_kind = (
            sem("s_small"), sem("s_adapted"), sem("s_emb"), sem("s_ztab"), sem("s_node"), sem("s_rows6"),
            sem("s_tab6"), sem("s_kind"))

        def over_blocks(eng, body):
            with eng.Fori(0, NB // U) as i:
                for u in range(U):
                    body(i, i * U + u, u)
            body(NB // U, NB - 1, 0)

        with nc.Block() as block:
            @block.sync
            def _(sp):
                sp.dma_start(w0[:, :, :], h["w0"]).then_inc(s_w0, 16)
                sp.dma_start(b0[:, :], h["b0"]).then_inc(s_w0, 16)
                sp.sem_inc(s_tfree, U)
                sp.dma_start(emb[:, 0:EM], h["emb"]).then_inc(s_small, 16)
                sp.dma_start(embT[:, :], h["embT"]).then_inc(s_small, 16)
                sp.dma_start(adapt[:, :], h["adaptT"]).then_inc(s_small, 16)
                sp.dma_start(kind[:, :], h["kind"]).then_inc(s_kind, 16)
                sp.dma_start(mult[:, :], h["mult"]).then_inc(s_kind, 16)

                def load(i, b, u):
                    wait_alone(sp, s_tfree, b + 1, passed_sp)
                    sp.dma_start(tin[:, u, :, :], cheb[:, bass.ds(b, 1), :, :].rearrange("p o k f -> p (o k) f")
                                 ).then_inc(s_t[u], 16)
                over_blocks(sp, load)
                sp.wait_ge(s_rows6, 3)
                sp.dma_start(u_table.rearrange("(b p) f -> p b f", p=P), u_rows[:, :, :]).then_inc(s_tab6, 16)
                sp.wait_ge(s_tab6, 16)

            @block.gpsimd
            def _(pool):
                pack2.put_all(pool, passed_pool)
                pool.wait_ge(s_ztab, 16)
                pool.wait_ge(s_kind, 32)
                for b in range(NB):
                    pool.indirect_dma_start(out=of_node[:, b, :], out_offset=None, in_=z_table,
                                            in_offset=bass.IndirectOffsetOnAxis(ap=kind[:, b:b + 1].bitcast(U32), axis=0)
                                            ).then_inc(s_node, 16)
                pack2.finish(pool)

            @block.tensor
            def _(pe):
                pe.wait_ge(s_small, 48)
                nc.tensor.matmul(adapted[0:Z, 0:EM], embT[:, :], adapt[:, :], start=True, stop=True).then_inc(s_adapted, 1)
                pe.wait_ge(s_w0, 32)

                def body(i, b, u):
                    o = u % 2
                    pe.wait_ge(s_t[u], 16 * (i + 1))
                    for a in range(2):
                        for q in range(Q // 2):
                            tr = nc.tensor.transpose(turned[o][a][0:2 * D, q * P:(q + 1) * P],
                                                     tin[:, u, 2 * (a * Q // 2 + q):2 * (a * Q // 2 + q) + 2, :]
                                                     .rearrange("p k f -> p (k f)"), eye[:, :])
                        tr.then_inc(s_turn, 1)
                    pe.wait_ge(s_copyA, b + 1)
                    pe.wait_ge(s_copyB, b + 1)
                    pe.sem_inc(s_tfree, 1)
                    pe.wait_ge(s_ofree, b + 1)
                    for q in range(Q):
                        mm = nc.tensor.matmul(acc[o][:, 0:D], tT[:, o, q, :], w0[:, q, :], start=(q == 0), stop=(q == Q - 1))
                    mm.then_inc(s_out0, 1)
                over_blocks(pe, body)

            @block.scalar
            def _(act):
                def body(i, b, u):
                    act.wait_ge(s_turn, b * 2 + 1)
                    act.wait_ge(s_out0, b + 1)
                    nc.scalar.activation(tT[:, u % 2, 0:Q // 2, :].rearrange("p q c -> p (q c)"),
                                         turned[u % 2][0][0:2 * D, :], ACT.Copy).then_inc(s_copyA, 1)
                act.sem_inc(s_out0, 2)
                act.wait_ge(s_emb, 1)
                act.wait_ge(s_small, 48)
                act.dma_start(z_table, emb[:, :]).then_inc(s_ztab, 16)
                for u in range(U):
                    body(0, u, u)
                    pack2.pack(act, u // 2, u, u % 2, u < 2)
                with act.Fori(1, NB // U) as i:
                    for u in range(U):
                        body(i, i * U + u, u)
                        pack2.pack(act, i * 2 + u // 2, i * U + u, u % 2, False)
                body(NB // U, NB - 1, 0)
                act.wait_ge(s_sqi0, 1)
                nc.scalar.activation(col[:, 1, :], col[:, 1, :], ACT.Sqrt).then_inc(s_sq0, 1)

            @block.vector
            def _(dve):
                dve.sem_inc(s_ofree, 2)

                def body(i, b, u):
                    dve.wait_ge(s_turn, b * 2 + 2)
                    dve.wait_ge(s_out0, b + 1)
                    nc.vector.tensor_copy(tT[:, u % 2, Q // 2:Q, :].rearrange("p q c -> p (q c)"),
                                          turned[u % 2][1][0:2 * D, :]).then_inc(s_copyB, 1)
                    dve.wait_ge(s_out0, b + 3)
                    nc.vector.tensor_tensor(o_sb[:, bass.ds(b, 1), :].rearrange("p o f -> p (o f)"),
                                            acc[u % 2][:, 0:D], b0[:, :], ALU.add).then_inc(s_ofree, 1)
                dve.wait_ge(s_adapted, 1)
                nc.vector.tensor_copy(emb[:, EM:2 * EM], adapted[0:Z, 0:EM]).then_inc(s_emb, 1)
                dve.wait_ge(s_w0, 32)
                over_blocks(dve, body)
                step = in_order(dve, s_ln0)
                dve.wait_ge(s_ofree, NB + 2)
                step(nc.vector.scalar_tensor_tensor(x_sb[:, :, :], o_sb[:, :, :], 0.0, x_sb[:, :, :], ALU.max, ALU.add))

                def root(var):
                    dve.sem_inc(s_sqi0, 1)
                    dve.wait_ge(s_sq0, 1)
                normalize(nc, step, root, x_sb[:, :, :], sq[:, :, :], col, None)
                dve.wait_ge(s_kind, 32)
                nc.vector.tensor_tensor(u_rows[:, :, 0:D], x_sb[:, :, :], wide_ap(mult[:, :]), ALU.mult).then_inc(s_rows6, 1)
                nc.vector.tensor_copy(u_rows[:, :, D:D + 1].rearrange("p b o -> p (b o)"), mult[:, :]).then_inc(s_rows6, 1)
                dve.wait_ge(s_node, 16 * NB)
                nc.vector.tensor_copy(u_rows[:, :, D + 1:UW], of_node[:, :, EM:2 * EM]).then_inc(s_rows6, 1)
                rest = of_node[:, :, 0:EM]
                for n in range(3):
                    part = e_parts[:, :, n * EM:(n + 1) * EM]
                    step(nc.vector.tensor_copy(part, rest))
                    if n < 2:
                        step(nc.vector.tensor_tensor(rest, rest, part, ALU.subtract))


def gather_rows(pool, table, ring, got, g, slot, ring_slot, s_got):
    for j in range(G):
        pool.indirect_dma_start(
            out=got[:, slot, j, :], out_offset=None, in_=table,
            in_offset=bass.IndirectOffsetOnAxis(ap=ring[:, ring_slot, j:j + 1].bitcast(U32), axis=0)
        ).then_inc(s_got[slot], 16)


def layer1_edges(nc, h, sb, sorted1, table, e_parts, block_of, first_of, eye, agg, passed):
    passed_sp, passed_act, passed_dve, passed_pe, passed_pool = passed
    U = 4
    with stage(nc, "edges1") as (sem, c7):
        rec = sb("rec", [P, U, G, R1], F32, c7)
        onehot = sb("onehot", [P, U, G, P], F32, c7)
        ring = sb("ring", [P, U, G], I32, c7)
        rel = sb("rel", [P, U, G], F32, c7)
        cutoff = sb("cutoff_of_group", [P, U, G], F32, c7)
        lanes = sb("lanes", [P, P], F32, c7)
        got = sb("got", [P, U, G, UW], F32, c7)
        msg = sb("msg", [P, 2, G, MW], F32, c7)
        prod = sb("prod", [P, 2, G, 3 * EM], F32, c7)
        logit = sb("logit", [P, 2, G], F32, c7)
        gate = sb("gate", [P, 2, G, D], F32, c7)
        cut = sb("cut", [P, 2, G, D], F32, c7)
        attrT = sb("attrT", [TWO, 2, G // 2 * P], F32, c7)
        onehotT = sb("onehotT", [P, 2, G * P], BF16, c7)
        hid = sb("hid", [2 * D + 1, 2, G // 2 * P], F32, c7)
        w1 = sb("w1_7", [TWO, 2 * D], F32, c7)
        w2 = sb("w2_7", [2 * D + 1, 2 * D], F32, c7)
        b1 = sb("b1_7", [2 * D, 1], F32, c7)

        def bank(name):
            return c7.enter_context(nc.psum_tensor(name, [P, 512], F32))
        attr_p, hid_p, onehot_p, sum_p = bank("attr_p"), bank("hid_p"), bank("onehot_p"), bank("sum_p")
        e_p = [bank("e_p0"), bank("e_p1")]
        gate_p = [bank("gate_p0"), bank("gate_p1")]
        s_rec = [sem(f"s_rec{u}") for u in range(U)]
        s_got = [sem(f"s_got{u}") for u in range(U)]
        s_ring = sem("s_ring")
        s_cutoff = sem("s_cutoff")
        s_rel = sem("s_rel")
        s_onehot = sem("s_onehot")
        s_used = sem("s_used")
        s_turn = sem("s_turn")
        s_turned = sem("s_turned")
        s_attrT = sem("s_attrT")
        s_onehotT = sem("s_onehotT")
        s_hidden = sem("s_hidden")
        s_silu = sem("s_silu")
        s_gatep = sem("s_gatep")
        s_e = sem("s_e")
        s_prod = sem("s_prod")
        s_gadd = sem("s_gadd")
        s_sum = sem("s_sum")
        s_acc = sem("s_acc")
        s_logit, s_cut, s_mult = sem("s_logit"), sem("s_cut"), sem("s_mult")
        s_const, s_ones, s_lanes, s_agg0 = sem("s_const7"), sem("s_ones7"), sem("s_lanes7"), sem("s_agg0")

        def loop(eng, body, start=0):
            with eng.Fori(start, NGS // U) as i:
                for u in range(U):
                    body(i, i * U + u, u)

        def ahead(i, u, n):
            return i + (u + n) // U, (u + n) % U

        with nc.Block() as block:
            @block.sync
            def _(sp):
                sp.dma_start(w1[:, :], h["l1_w1"]).then_inc(s_const, 16)
                sp.dma_start(w2[:, :], h["l1_w2"]).then_inc(s_const, 16)
                sp.dma_start(b1[:, :], h["l1_b1"]).then_inc(s_const, 16)

                def load(g, u):
                    sp.dma_start(rec[:, u, :, :].rearrange("p j f -> p (j f)"),
                                 sorted1[bass.ds(g * SLOTS, SLOTS), :].rearrange("(p j) f -> p (j f)", p=P)
                                 ).then_inc(s_rec[u], 16)
                for u in range(U):
                    load(u, u)

                def body(i, g, u):
                    for s in (s_turn, s_ring, s_cutoff, s_rel):
                        wait_alone(sp, s, g + 1, passed_sp)
                    load(g + U, u)
                loop(sp, body)
                for u in range(U):
                    sp.wait_ge(s_rec[u], 16 * (NGS // U + 1))

            @block.gpsimd
            def _(pool):
                pool.iota(lanes[:, :], pattern=[[1, P]], base=0, channel_multiplier=0,
                          allow_small_or_imprecise_dtypes=True).then_inc(s_lanes, 1)

                def body(i, g, u):
                    wait_alone(pool, s_ring, g + 1, passed_pool)
                    wait_alone(pool, s_used, g + 1, passed_pool)
                    gather_rows(pool, table, ring, got, g, u, u, s_got)
                loop(pool, body)

            @block.tensor
            def _(pe):
                pe.wait_ge(s_const, 48)

                def turn_attributes(i, g, u):
                    wait_alone(pe, s_rec[u], 16 * (i + 1), passed_pe)
                    wait_alone(pe, s_attrT, g + 1, passed_pe)
                    for q in range(2):
                        tr = nc.tensor.transpose(
                            attr_p[0:TWO, q * P:(q + 1) * P],
                            rec[:, u, 2 * q:2 * q + 2, :].rearrange("p t f -> p (t f)")[:, 0:TWO], eye[:, :])
                    tr.then_inc(s_turn, 1)

                def turn_ones(g, u):
                    pe.wait_ge(s_onehot, g + 1)
                    pe.wait_ge(s_onehotT, g + 1)
                    for j in range(G):
                        tr = nc.tensor.transpose(onehot_p[:, j * P:(j + 1) * P], onehot[:, u, j, :], eye[:, :])
                    tr.then_inc(s_turned, 1)

                def hidden(g, u):
                    pe.wait_ge(s_attrT, g + 2)
                    pe.wait_ge(s_silu, g + 1)
                    nc.tensor.matmul(hid_p[0:2 * D, 0:2 * P], w1[:, :], attrT[:, u % 2, :], start=True, stop=True
                                     ).then_inc(s_hidden, 1)

                def fetch(g, u):
                    blk = pe.value_load(block_of[0:1, bass.ds(g, 1)], min_val=0, max_val=NB - 1)
                    pe.wait_ge(s_onehotT, g + 2)
                    pe.wait_ge(s_prod, g + 1)
                    for j in range(G):
                        mm = nc.tensor.matmul(e_p[u % 2][:, j * 3 * EM:(j + 1) * 3 * EM],
                                              onehotT[:, u % 2, j * P:(j + 1) * P],
                                              e_parts[:, bass.ds(blk, 1), :].rearrange("p o f -> p (o f)"),
                                              start=True, stop=True)
                    mm.then_inc(s_e, 1)

                def gates(g, u):
                    pe.wait_ge(s_silu, g + 2)
                    pe.wait_ge(s_gadd, g + 1)
                    for q in range(2):
                        mm = nc.tensor.matmul(gate_p[u % 2][:, q * 2 * D:(q + 1) * 2 * D],
                                              hid[:, u % 2, q * P:(q + 1) * P], w2[:, :], start=True, stop=True)
                    mm.then_inc(s_gatep, 1)

                for g in range(3):
                    turn_attributes(0, g, g)
                    if g > 0:
                        hidden(g - 1, g - 1)
                        fetch(g - 1, g - 1)
                    if g > 1:
                        gates(g - 2, g - 2)
                    turn_ones(g, g)

                def body(i, g, u):
                    i3, u3 = ahead(i, u, 3)
                    turn_attributes(i3, g + 3, u3)
                    hidden(g + 2, (u + 2) % U)
                    fetch(g + 2, (u + 2) % U)
                    gates(g + 1, (u + 1) % U)
                    turn_ones(g + 3, u3)
                    pe.wait_ge(s_used, g + U + 1)
                    pe.wait_ge(s_acc, g + 1)
                    for j in range(G):
                        mm = nc.tensor.matmul(sum_p[:, 0:MW], onehot[:, u, j, :], msg[:, u % 2, j, :],
                                              start=(j == 0), stop=(j == G - 1))
                    mm.then_inc(s_sum, 1)
                loop(pe, body)

            @block.scalar
            def _(act):
                act.wait_ge(s_const, 48)
                for s in (s_attrT, s_onehotT, s_silu):
                    act.sem_inc(s, 1)

                def copy_attributes(g, u):
                    act.wait_ge(s_turn, g + 1)
                    act.wait_ge(s_hidden, g + 1)
                    nc.scalar.activation(attrT[:, u % 2, :], attr_p[0:TWO, 0:2 * P], ACT.Copy).then_inc(s_attrT, 1)

                def silu(g, u):
                    act.wait_ge(s_hidden, g + 3)
                    act.wait_ge(s_gatep, g + 1)
                    nc.scalar.activation(hid[0:2 * D, u % 2, :], hid_p[0:2 * D, 0:2 * P], ACT.Silu, bias=b1[:, :]
                                         ).then_inc(s_silu, 1)

                def copy_ones(g, u):
                    act.wait_ge(s_turned, g + 1)
                    act.wait_ge(s_e, g + 1)
                    nc.scalar.activation(onehotT[:, u % 2, :], onehot_p[:, :], ACT.Copy).then_inc(s_onehotT, 1)
                act.wait_ge(s_ones, 1)
                for g in range(3):
                    copy_attributes(g, g)
                    if g > 0:
                        silu(g - 1, g - 1)
                    copy_ones(g, g)

                def body(i, g, u):
                    copy_attributes(g + 3, (u + 3) % U)
                    silu(g + 2, (u + 2) % U)
                    copy_ones(g + 3, (u + 3) % U)
                loop(act, body)

            @block.vector
            def _(dve):
                for s, n in ((s_used, U), (s_hidden, 2), (s_gatep, 2), (s_e, 2), (s_prod, 2), (s_gadd, 2),
                             (s_sum, U), (s_acc, 1)):
                    dve.sem_inc(s, n)
                nc.vector.memset(agg[:, :, :], 0.0).then_inc(s_agg0, 1)
                nc.vector.memset(hid[2 * D:2 * D + 1, :, :], 1.0).then_inc(s_ones, 1)
                dve.wait_ge(s_lanes, 1)
                dve.wait_ge(s_agg0, 1)

                def field(u, f):
                    return rec[:, u, :, f:f + 1].rearrange("p j o -> p (j o)")

                def prepare(i, g, u):
                    dve.wait_ge(s_rec[u], 16 * (i + 1))
                    nc.vector.tensor_copy(ring[:, u, :], field(u, R + 1)).then_inc(s_ring, 1)
                    nc.vector.tensor_copy(cutoff[:, u, :], field(u, R)).then_inc(s_cutoff, 1)
                    nc.vector.tensor_scalar(rel[:, u, :], field(u, R + 2), first_of[:, bass.ds(g, 1)], None,
                                            ALU.subtract).then_inc(s_rel, 1)

                def ones_of(g, u):
                    dve.wait_ge(s_sum, g + 1)
                    dve.wait_ge(s_rel, g + 1)
                    for j in range(G):
                        one = nc.vector.tensor_scalar(onehot[:, u, j, :], lanes[:, :], rel[:, u, j:j + 1], None, ALU.is_equal)
                    one.then_inc(s_onehot, 1)

                def products(i, g, u):
                    b = u % 2
                    dve.wait_ge(s_got[u], 16 * G * (i + 1))
                    dve.wait_ge(s_e, g + 3)
                    nc.vector.tensor_tensor(
                        prod[:, b, :, :].rearrange("p j (n k) -> p j n k", n=3),
                        e_p[b][:, 0:G * 3 * EM].rearrange("p (j n k) -> p j n k", j=G, n=3),
                        got[:, u, :, D + 1:UW].unsqueeze(2).to_broadcast([P, G, 3, EM]), ALU.mult).then_inc(s_prod, 1)
                    dve.wait_ge(s_cutoff, g + 1)
                    nc.vector.tensor_tensor(cut[:, b, :, :], got[:, u, :, 0:D],
                                            cutoff[:, u, :].unsqueeze(2).to_broadcast([P, G, D]), ALU.mult).then_inc(s_cut, 1)
                    dve.wait_ge(s_sum, g + 3)
                    nc.vector.tensor_copy(msg[:, b, :, D:MW], got[:, u, :, D:MW]).then_inc(s_mult, 1)

                def sum_products(g, u):
                    dve.wait_ge(s_prod, g + 3)
                    nc.vector.tensor_reduce(logit[:, u % 2, :], prod[:, u % 2, :, :], AX.X, ALU.add).then_inc(s_logit, 1)

                def add_logits(g, u):
                    b = u % 2
                    dve.wait_ge(s_logit, g + 1)
                    dve.wait_ge(s_gatep, g + 3)
                    nc.vector.tensor_tensor(gate[:, b, :, :], gate_p[b][:, 0:G * D].rearrange("p (j f) -> p j f", j=G),
                                            logit[:, b, :].unsqueeze(2).to_broadcast([P, G, D]), ALU.add).then_inc(s_gadd, 1)

                def messages(g, u):
                    b = u % 2
                    dve.wait_ge(s_gadd, g + 3)
                    dve.wait_ge(s_cut, g + 1)
                    dve.wait_ge(s_mult, g + 1)
                    nc.vector.tensor_tensor(msg[:, b, :, 0:D], gate[:, b, :, :], cut[:, b, :, :], ALU.mult
                                            ).then_inc(s_used, 1)

                def add_sum(g):
                    blk = dve.value_load(block_of[0:1, bass.ds(g, 1)], min_val=0, max_val=NB - 1)
                    at = agg[:, bass.ds(blk, 1), :].rearrange("p o f -> p (o f)")
                    dve.wait_ge(s_sum, g + U + 1)
                    dve.wait_ge(s_acc, g + 1)
                    nc.vector.tensor_tensor(at, at, sum_p[:, 0:MW], ALU.add).then_inc(s_acc, 1)

                for g in range(3):
                    prepare(0, g, g)
                    ones_of(g, g)

                def body(i, g, u, first=False):
                    i3, u3 = ahead(i, u, 3)
                    products(i, g, u)
                    prepare(i3, g + 3, u3)
                    sum_products(g, u)
                    if not first:
                        add_sum(g - 1)
                    add_logits(g, u)
                    ones_of(g + 3, u3)
                    messages(g, u)
                for u in range(U):
                    body(0, u, u, u == 0)
                loop(dve, body, 1)
                add_sum(NGS - 1)


def layer2_edges(nc, h, sb, sorted2, table, block_of, first_of, agg, passed):
    passed_sp, passed_act, passed_dve, passed_pe, passed_pool = passed
    U = 4
    with stage(nc, "edges2") as (sem, c9):
        rec = sb("rec9", [P, U, G, R2], F32, c9)
        onehot = sb("onehot9", [P, U, G, P], F32, c9)
        ring = sb("ring9", [P, U, G], I32, c9)
        rel = sb("rel9", [P, U, G], F32, c9)
        lanes = sb("lanes9", [P, P], F32, c9)
        got = sb("got9", [P, U, G, D], F32, c9)
        sum_p = [c9.enter_context(nc.psum_tensor(f"sum9_{n}", [P, 512], F32)) for n in range(2)]
        s_rec = [sem(f"s_rec9_{u}") for u in range(U)]
        s_got = [sem(f"s_got9_{u}") for u in range(U)]
        s_ring, s_rel, s_onehot = sem("s_ring9"), sem("s_rel9"), sem("s_onehot9")
        s_sum = sem("s_sum9")
        s_acc = sem("s_acc9")
        s_lanes, s_agg0 = sem("s_lanes9"), sem("s_agg0_9")

        def loop(eng, body):
            with eng.Fori(0, NGS // U) as i:
                for u in range(U):
                    body(i, i * U + u, u)

        with nc.Block() as block:
            @block.sync
            def _(sp):
                def load(g, u):
                    sp.dma_start(rec[:, u, :, :].rearrange("p j f -> p (j f)"),
                                 sorted2[bass.ds(g * SLOTS, SLOTS), :].rearrange("(p j) f -> p (j f)", p=P)
                                 ).then_inc(s_rec[u], 16)
                for u in range(U):
                    load(u, u)

                def body(i, g, u):
                    wait_alone(sp, s_onehot, g + 1, passed_sp)
                    load(g + U, u)
                loop(sp, body)
                for u in range(U):
                    sp.wait_ge(s_rec[u], 16 * (NGS // U + 1))

            @block.gpsimd
            def _(pool):
                pool.iota(lanes[:, :], pattern=[[1, P]], base=0, channel_multiplier=0,
                          allow_small_or_imprecise_dtypes=True).then_inc(s_lanes, 1)

                def body(i, g, u):
                    wait_alone(pool, s_ring, g + 1, passed_pool)
                    wait_alone(pool, s_sum, g + 1, passed_pool)
                    gather_rows(pool, table, ring, got, g, u, u, s_got)
                loop(pool, body)

            @block.tensor
            def _(pe):
                def body(i, g, u):
                    pe.wait_ge(s_onehot, g + 1)
                    pe.wait_ge(s_got[u], 16 * G * (i + 1))
                    pe.wait_ge(s_acc, g + 1)
                    for j in range(G):
                        mm = nc.tensor.matmul(sum_p[u % 2][:, 0:D], onehot[:, u, j, :], got[:, u, j, :],
                                              start=(j == 0), stop=(j == G - 1))
                    mm.then_inc(s_sum, 1)
                loop(pe, body)

            @block.vector
            def _(dve):
                dve.sem_inc(s_sum, U)
                dve.sem_inc(s_acc, 2)
                nc.vector.memset(agg[:, :, :], 0.0).then_inc(s_agg0, 1)
                dve.wait_ge(s_lanes, 1)
                dve.wait_ge(s_agg0, 1)

                def prepare(i, g, u):
                    dve.wait_ge(s_rec[u], 16 * (i + 1))
                    dve.wait_ge(s_sum, g + 1)
                    nc.vector.tensor_copy(ring[:, u, :], rec[:, u, :, 0:1].rearrange("p j o -> p (j o)")).then_inc(s_ring, 1)
                    nc.vector.tensor_scalar(rel[:, u, :], rec[:, u, :, 2:3].rearrange("p j o -> p (j o)"),
                                            first_of[:, bass.ds(g, 1)], None, ALU.subtract).then_inc(s_rel, 1)
                    dve.wait_ge(s_rel, g + 1)
                    for j in range(G):
                        one = nc.vector.tensor_scalar(onehot[:, u, j, :], lanes[:, :], rel[:, u, j:j + 1],
                                                      rec[:, u, j, 1:2], ALU.is_equal, ALU.mult)
                    one.then_inc(s_onehot, 1)

                for g in range(3):
                    prepare(0, g, g)

                def body(i, g, u):
                    prepare(i + (u + 3) // U, g + 3, (u + 3) % U)
                    blk = dve.value_load(block_of[0:1, bass.ds(g, 1)], min_val=0, max_val=NB - 1)
                    at = agg[:, bass.ds(blk, 1), :].rearrange("p o f -> p (o f)")
                    dve.wait_ge(s_sum, g + U + 1)
                    nc.vector.tensor_tensor(at, at, sum_p[u % 2][:, 0:D], ALU.add).then_inc(s_acc, 1)
                    dve.wait_ge(s_acc, g + 3)
                loop(dve, body)


def end_of_layer1(nc, h, sb, agg, x_sb):
    with stage(nc, "end1") as (sem, c8):
        gamma = sb("gamma", [P, D], F32, c8)
        beta = sb("beta", [P, D], F32, c8)
        y = sb("y8", [P, NB, D], F32, c8)
        sq = sb("sq8", [P, NB, D], F32, c8)
        tot = sb("tot8", [P, NB], F32, c8)
        col = sb("col8", [P, 2, NB], F32, c8)
        s_in8, s_chain8, s_rt8, s_rti8 = sem("s_in8"), sem("s_chain8"), sem("s_rt8"), sem("s_rti8")
        with nc.Block() as block:
            @block.sync
            def _(sp):
                sp.dma_start(gamma[:, :], h["gamma"]).then_inc(s_in8, 16)
                sp.dma_start(beta[:, :], h["beta"]).then_inc(s_in8, 16)

            @block.scalar
            def _(act):
                for n in range(2):
                    act.wait_ge(s_rti8, n + 1)
                    nc.scalar.activation(col[:, 1, :], col[:, 1, :], ACT.Sqrt).then_inc(s_rt8, 1)

            @block.vector
            def _(dve):
                step = in_order(dve, s_chain8)
                dve.wait_ge(s_in8, 32)
                roots = [0]

                def root(var):
                    roots[0] += 1
                    dve.sem_inc(s_rti8, 1)
                    dve.wait_ge(s_rt8, roots[0])
                step(nc.vector.tensor_scalar(tot[:, :], agg[:, :, D:MW].rearrange("p b o -> p (b o)"), 1e-8, None, ALU.max))
                step(nc.vector.reciprocal(tot[:, :], tot[:, :]))
                step(nc.vector.tensor_tensor(y[:, :, :], agg[:, :, 0:D], wide_ap(tot[:, :]), ALU.mult))
                step(nc.vector.tensor_tensor(y[:, :, :], y[:, :, :], x_sb[:, :, :], ALU.add))
                normalize(nc, step, root, y[:, :, :], sq[:, :, :], col, None)
                step(nc.vector.tensor_tensor(y[:, :, :], y[:, :, :], row_ap(gamma[:, :]), ALU.mult))
                step(nc.vector.tensor_tensor(y[:, :, :], y[:, :, :], row_ap(beta[:, :]), ALU.add))
                step(nc.vector.tensor_tensor(x_sb[:, :, :], y[:, :, :], x_sb[:, :, :], ALU.add))
                normalize(nc, step, root, x_sb[:, :, :], sq[:, :, :], col, None)


def table_of_layer2(nc, h, sb, r_table, x_sb, eye, passed_pe, passed_sp):
    Q = NR // 2
    C = 4
    with stage(nc, "rtable") as (sem, c9):
        xc = sb("xc", [P, 2, C, D], F32, c9)
        xT = sb("xT9", [D, 2, C * P], F32, c9)
        hT = sb("hT9", [2 * D, 2, Q, C * P], F32, c9)
        rows = sb("rows9", [P, 2, C, NR * D], F32, c9)
        w1 = sb("w1_9", [D, Q, 2 * D], F32, c9)
        w2 = sb("w2_9", [2 * D, Q, 2 * D], F32, c9)
        b1 = sb("b1_9", [2 * D, 1], F32, c9)
        turned = c9.enter_context(nc.psum_tensor("turned9", [P, 512], F32))
        hp = [c9.enter_context(nc.psum_tensor(f"hp9_{q}", [P, 512], F32)) for q in range(2)]
        rp = [c9.enter_context(nc.psum_tensor(f"rp9_{c}", [P, 512], F32)) for c in range(C)]
        s_c9, s_xc, s_turn9, s_xT, s_hp, s_hT, s_rp, s_rows9 = (
            sem("s_c9"), sem("s_xc"), sem("s_turn9"), sem("s_xT"), sem("s_hp"), sem("s_hT"), sem("s_rp"),
            sem("s_rows9"))
        s_stored = [sem(f"s_stored9_{v}") for v in range(2)]
        CH = NB // C
        assert CH % 2 == 0 and NB % C == 1

        def chunks(eng, body):
            with eng.Fori(0, CH // 2) as m:
                for v in range(2):
                    body(m * 2 + v, (m * 2 + v) * C, C, v)
            body(CH, NB - 1, 1, 0)

        with nc.Block() as block:
            @block.sync
            def _(sp):
                sp.dma_start(w1[:, :, :], h["l2_w1"]).then_inc(s_c9, 16)
                sp.dma_start(w2[:, :, :], h["l2_w2"]).then_inc(s_c9, 16)
                sp.dma_start(b1[:, :], h["l2_b1"]).then_inc(s_c9, 16)

                def body(i, b0, n, v):
                    wait_alone(sp, s_rows9, i + 2, passed_sp)
                    dst = r_table.rearrange("(b p r) f -> p b (r f)", p=P, r=NR)[:, bass.ds(b0, n), :]
                    sp.dma_start(dst, rows[:, v, 0:n, :]).then_inc(s_stored[v], 16)
                chunks(sp, body)
                sp.wait_ge(s_stored[0], 16 * (CH // 2 + 2))
                sp.wait_ge(s_stored[1], 16 * (CH // 2 + 1))

            @block.tensor
            def _(pe):
                pe.wait_ge(s_c9, 48)

                def hidden(i, n, v):
                    wait_alone(pe, s_xc, i + 1, passed_pe)
                    for c in range(n):
                        tr = nc.tensor.transpose(turned[0:D, c * P:(c + 1) * P], xc[:, v, c, :], eye[:, :])
                    tr.then_inc(s_turn9, 1)
                    pe.wait_ge(s_xT, i + 1)
                    for q in range(Q):
                        pe.wait_ge(s_hT, i * Q + q + 1)
                        nc.tensor.matmul(hp[q % 2][0:2 * D, 0:n * P], w1[:, q, :], xT[:, v, 0:n * P],
                                         start=True, stop=True).then_inc(s_hp, 1)

                def rows_of(i, n, v):
                    pe.wait_ge(s_hT, (i + 1) * Q + 2)
                    pe.wait_ge(s_rows9, i + 1)
                    for c in range(n):
                        for q in range(Q):
                            mm = nc.tensor.matmul(rp[c][:, q * 2 * D:(q + 1) * 2 * D], hT[:, v, q, c * P:(c + 1) * P],
                                                  w2[:, q, :], start=True, stop=True)
                    mm.then_inc(s_rp, 1)
                hidden(0, C, 0)
                with pe.Fori(0, CH // 2 - 1) as m:
                    for v in range(2):
                        hidden(m * 2 + v + 1, C, 1 - v)
                        rows_of(m * 2 + v, C, v)
                hidden(CH - 1, C, 1)
                rows_of(CH - 2, C, 0)
                hidden(CH, 1, 0)
                rows_of(CH - 1, C, 1)
                rows_of(CH, 1, 0)

            @block.scalar
            def _(act):
                act.sem_inc(s_hT, 2)
                act.wait_ge(s_c9, 48)

                def body(i, b0, n, v):
                    for q in range(Q):
                        act.wait_ge(s_hp, i * Q + q + 1)
                        nc.scalar.activation(hT[:, v, q, 0:n * P], hp[q % 2][0:2 * D, 0:n * P], ACT.Relu,
                                             bias=b1[:, :]).then_inc(s_hT, 1)
                chunks(act, body)

            @block.vector
            def _(dve):
                for v in range(2):
                    dve.sem_inc(s_stored[v], 16)
                dve.sem_inc(s_rows9, 1)

                def give(i, n, v):
                    nc.vector.tensor_copy(xc[:, v, 0:n, :], x_sb[:, bass.ds(i * C, n), :]).then_inc(s_xc, 1)

                def take_turned(i, n, v):
                    dve.wait_ge(s_turn9, i + 1)
                    nc.vector.tensor_copy(xT[:, v, 0:n * P], turned[0:D, 0:n * P]).then_inc(s_xT, 1)

                def take_rows(i, m, n, v):
                    dve.wait_ge(s_rp, i + 1)
                    dve.wait_ge(s_stored[v], 16 * (m + 1))
                    for c in range(n):
                        cpy = nc.vector.tensor_copy(rows[:, v, c, :], rp[c][:, 0:NR * D])
                    cpy.then_inc(s_rows9, 1)

                give(0, C, 0)
                take_turned(0, C, 0)
                give(1, C, 1)
                with dve.Fori(0, CH // 2 - 1) as m:
                    for v in range(2):
                        i = m * 2 + v
                        take_turned(i + 1, C, 1 - v)
                        give(i + 2, C, v)
                        take_rows(i, m, C, v)
                take_turned(CH - 1, C, 1)
                give(CH, 1, 0)
                take_rows(CH - 2, CH // 2 - 1, C, 0)
                take_turned(CH, 1, 0)
                take_rows(CH - 1, CH // 2 - 1, C, 1)
                take_rows(CH, CH // 2, 1, 0)


def end_of_layer2(nc, h, sb, agg, x_sb):
    with stage(nc, "end2") as (sem, c8):
        bias = sb("bias10", [P, D], F32, c8)
        sq = sb("sq10", [P, NB, D], F32, c8)
        col = sb("col10", [P, 2, NB], F32, c8)
        s_in10, s_chain10, s_rt10, s_rti10 = sem("s_in10"), sem("s_chain10"), sem("s_rt10"), sem("s_rti10")
        with nc.Block() as block:
            @block.sync
            def _(sp):
                sp.dma_start(bias[:, :], h["l2_b2"]).then_inc(s_in10, 16)

            @block.scalar
            def _(act):
                act.wait_ge(s_rti10, 1)
                nc.scalar.activation(col[:, 1, :], col[:, 1, :], ACT.Sqrt).then_inc(s_rt10, 1)

            @block.vector
            def _(dve):
                step = in_order(dve, s_chain10)
                dve.wait_ge(s_in10, 16)

                def root(var):
                    dve.sem_inc(s_rti10, 1)
                    dve.wait_ge(s_rt10, 1)
                a = agg[:, :, :]
                step(nc.vector.tensor_tensor(a, a, row_ap(bias[:, :]), ALU.add))
                step(nc.vector.scalar_tensor_tensor(x_sb[:, :, :], a, 0.0, x_sb[:, :, :], ALU.max, ALU.add))
                normalize(nc, step, root, x_sb[:, :, :], sq[:, :, :], col, None)


def layer3(nc, h, sb, strips8, strip32, many, x_sb, outdeg, eye, passed):
    U = 7
    W3 = 3 * D
    passed_sp, passed_act, passed_dve, passed_pe, passed_pool = passed
    with stage(nc, "layer3") as (sem, c11):
        ci = sb("ci", [P, NB], F32, c11)
        v = sb("v11", [P, NB, D], F32, c11)
        r = sb("r11", [P, NB, D], F32, c11)
        parts = sb("parts11", [P, NB, W3 + 1], BF16, c11)
        none = sb("none11", [P, W3 - D], BF16, c11)
        ones1 = sb("ones11", [P, 1], F32, c11)
        s_wide = sem("s_wide")
        cbuf = sb("cbuf11", [P, U, NP], FP8, c11)
        wide = cbuf[:, :, :].rearrange("p u c -> p (u c)").bitcast(F32)[:, 0:NP]
        agg = sb("agg11", [P, NB, D], F32, c11)
        deg = sb("deg11", [P, NB], F32, c11)
        cj = sb("cj11", [P, NB], F32, c11)
        acc = [c11.enter_context(nc.psum_tensor(f"acc11_{u}", [P, 512], F32)) for u in range(U)]
        s_c = [sem(f"s_c11_{u}") for u in range(U)]
        s_strip, s_accfree, s_chain, s_parts, s_sum, s_deg = (
            sem("s_strip11"), sem("s_accfree11"), sem("s_chain11"), sem("s_parts11"), sem("s_sum11"), sem("s_deg11"))
        s_rt, s_rti = sem("s_rt11"), sem("s_rti11")
        with nc.Block() as block:
            @block.sync
            def _(sp):
                def load(rr, u, first):
                    if not first:
                        wait_alone(sp, s_strip, rr * U + u - U + 1, passed_sp)
                    sp.dma_start(cbuf[:, u, :].bitcast(U8), strips8[bass.ds(rr * U + u, 1), :, :].rearrange("o p c -> p (o c)")
                                 ).then_inc(s_c[u], 16)
                with sp.If(sp.value_load(many[0:1, 0:1], min_val=0, max_val=1) == 0):
                    for u in range(U):
                        load(0, u, True)
                    with sp.Fori(1, NB // U) as rr:
                        for u in range(U):
                            load(rr, u, False)
                with sp.Else():
                    sp.dma_start(wide, strip32(0)).then_inc(s_wide, 16)
                    with sp.Fori(1, NB) as j:
                        wait_alone(sp, s_strip, j, passed_sp)
                        sp.dma_start(wide, strip32(j)).then_inc(s_wide, 16)

            @block.tensor
            def _(pe):
                def strip(rr, u):
                    wait_alone(pe, s_c[u], 16 * (rr + 1), passed_pe)
                    wait_alone(pe, s_accfree, rr * U + u + 1, passed_pe)
                    for s in range(NB):
                        mm = nc.tensor.matmul(acc[u][:, 0:W3 + 1], cbuf[:, u, s * P:(s + 1) * P], parts[:, s, :],
                                              start=(s == 0), stop=(s == NB - 1))
                    mm.then_inc(s_strip, 1)

                def wide_strip(rr, u):
                    wait_alone(pe, s_wide, 16 * (rr * U + u + 1), passed_pe)
                    wait_alone(pe, s_accfree, rr * U + u + 1, passed_pe)
                    nc.tensor.matmul(acc[u][:, D:W3], parts[:, 0, 0:P], none[:, :], start=True, stop=True)
                    for s in range(NB):
                        nc.tensor.matmul(acc[u][:, W3:W3 + 1], wide[:, s * P:(s + 1) * P], ones1[:, :],
                                         start=(s == 0), stop=(s == NB - 1))
                    for s in range(NB):
                        mm = nc.tensor.matmul(acc[u][:, 0:D], wide[:, s * P:(s + 1) * P], v[:, s, :],
                                              start=(s == 0), stop=(s == NB - 1))
                    mm.then_inc(s_strip, 1)
                pe.wait_ge(s_parts, 1)
                with pe.If(pe.value_load(many[0:1, 0:1], min_val=0, max_val=1) == 0):
                    with pe.Fori(0, NB // U) as rr:
                        for u in range(U):
                            strip(rr, u)
                with pe.Else():
                    with pe.Fori(0, NB // U) as rr:
                        for u in range(U):
                            wide_strip(rr, u)

            @block.scalar
            def _(act):
                act.wait_ge(s_rti, 1)
                nc.scalar.activation(ci[:, :], ci[:, :], ACT.Sqrt).then_inc(s_rt, 1)
                act.wait_ge(s_rti, 2)
                nc.scalar.activation(cj[:, :], cj[:, :], ACT.Sqrt).then_inc(s_rt, 1)

            @block.vector
            def _(dve):
                step = in_order(dve, s_chain)
                step(nc.vector.tensor_scalar(ci[:, :], outdeg[:, :], 1.0, None, ALU.max))
                dve.sem_inc(s_rti, 1)
                dve.wait_ge(s_rt, 1)
                step(nc.vector.reciprocal(ci[:, :], ci[:, :]))
                step(nc.vector.tensor_tensor(v[:, :, :], x_sb[:, :, :], wide_ap(ci[:, :]), ALU.mult))
                step(nc.vector.tensor_copy(parts[:, :, 0:D], v[:, :, :]))
                step(nc.vector.tensor_tensor(r[:, :, :], v[:, :, :], parts[:, :, 0:D], ALU.subtract))
                step(nc.vector.tensor_copy(parts[:, :, D:2 * D], r[:, :, :]))
                step(nc.vector.tensor_tensor(parts[:, :, 2 * D:W3], r[:, :, :], parts[:, :, D:2 * D], ALU.subtract))
                step(nc.vector.memset(parts[:, :, W3:W3 + 1], 1.0))
                step(nc.vector.memset(none[:, :], 0.0))
                step(nc.vector.memset(ones1[:, :], 1.0))
                dve.sem_inc(s_parts, 1)
                dve.sem_inc(s_accfree, U)
                with dve.Fori(0, NB // U) as rr:
                    for u in range(U):
                        n = rr * U + u
                        dve.wait_ge(s_strip, n + 1)
                        nc.vector.tensor_reduce(agg[:, bass.ds(n, 1), :].rearrange("p o f -> p (o f)"),
                                                acc[u][:, 0:W3].rearrange("p (s f) -> p f s", f=D),
                                                AX.X, ALU.add).then_inc(s_sum, 1)
                        nc.vector.tensor_copy(deg[:, bass.ds(n, 1)], acc[u][:, W3:W3 + 1]).then_inc(s_deg, 1)
                        dve.wait_ge(s_sum, n + 1)
                        dve.wait_ge(s_deg, n + 1)
                        dve.sem_inc(s_accfree, 1)
                step(nc.vector.tensor_scalar(cj[:, :], deg[:, :], 1.0, None, ALU.max))
                dve.sem_inc(s_rti, 1)
                dve.wait_ge(s_rt, 2)
                step(nc.vector.reciprocal(cj[:, :], cj[:, :]))
                step(nc.vector.tensor_tensor(agg[:, :, :], agg[:, :, :], wide_ap(cj[:, :]), ALU.mult))
                step(nc.vector.tensor_scalar(deg[:, :], deg[:, :], 0.0, None, ALU.is_gt))
                step(nc.vector.tensor_scalar(cj[:, :], deg[:, :], -1.0, 1.0, ALU.mult, ALU.add))
                step(nc.vector.tensor_tensor(agg[:, :, :], agg[:, :, :], wide_ap(deg[:, :]), ALU.mult))
                step(nc.vector.tensor_tensor(v[:, :, :], x_sb[:, :, :], wide_ap(cj[:, :]), ALU.mult))
                step(nc.vector.tensor_tensor(agg[:, :, :], agg[:, :, :], v[:, :, :], ALU.add))

        hc = sb("hc", [P, 2, D], F32, c11)
        hT = sb("hT11", [D, 2, P], F32, c11)
        wt = sb("wt11", [D, D], F32, c11)
        b3 = sb("b3", [P, D], F32, c11)
        col = sb("col11", [P, 2, NB], F32, c11)
        s_w, s_hc, s_tn, s_hT, s_mm, s_o = (
            sem("s_w11"), sem("s_hc11"), sem("s_tn11"), sem("s_hT11"), sem("s_mm11"), sem("s_o11"))
        s_chainb, s_rtb, s_rtib = sem("s_chain11b"), sem("s_rt11b"), sem("s_rti11b")

        def blocks(eng, body):
            with eng.Fori(0, NB // 2) as i:
                for u in range(2):
                    body(i * 2 + u, u)
            body(NB - 1, 0)
        with nc.Block() as block:
            @block.sync
            def _(sp):
                sp.dma_start(wt[:, :], h["l3_w"]).then_inc(s_w, 16)
                sp.dma_start(b3[:, :], h["l3_b"]).then_inc(s_w, 16)

            @block.tensor
            def _(pe):
                pe.wait_ge(s_w, 32)

                def body(b, u):
                    wait_alone(pe, s_hc, b + 1, passed_pe)
                    nc.tensor.transpose(acc[u][0:D, 0:P], hc[:, u, :], eye[:, :]).then_inc(s_tn, 1)
                    pe.wait_ge(s_hT, b + 1)
                    nc.tensor.matmul(acc[2 + u][:, 0:D], hT[:, u, :], wt[:, :], start=True, stop=True).then_inc(s_mm, 1)
                blocks(pe, body)

            @block.scalar
            def _(act):
                def body(b, u):
                    act.wait_ge(s_tn, b + 1)
                    nc.scalar.activation(hT[:, u, :], acc[u][0:D, 0:P], ACT.Copy).then_inc(s_hT, 1)
                blocks(act, body)
                act.wait_ge(s_rtib, 1)
                nc.scalar.activation(col[:, 1, :], col[:, 1, :], ACT.Sqrt).then_inc(s_rtb, 1)

            @block.vector
            def _(dve):
                dve.wait_ge(s_w, 32)

                def body(b, u):
                    nc.vector.tensor_copy(hc[:, u, :], agg[:, bass.ds(b, 1), :].rearrange("p o f -> p (o f)")).then_inc(s_hc, 1)
                    dve.wait_ge(s_mm, b + 1)
                    nc.vector.tensor_tensor(v[:, bass.ds(b, 1), :].rearrange("p o f -> p (o f)"), acc[2 + u][:, 0:D],
                                            b3[:, :], ALU.add).then_inc(s_o, 1)
                blocks(dve, body)
                dve.wait_ge(s_o, NB)
                step = in_order(dve, s_chainb)
                step(nc.vector.scalar_tensor_tensor(x_sb[:, :, :], v[:, :, :], 0.0, x_sb[:, :, :], ALU.max, ALU.add))

                def root(var):
                    dve.sem_inc(s_rtib, 1)
                    dve.wait_ge(s_rtb, 1)
                normalize(nc, step, root, x_sb[:, :, :], r[:, :, :], col, None)


class RecordsOfLayer2:

    def __init__(self, nc, sb, memory, name, sem, edges, n, first_tile, tiles):
        self.nc, self.n, self.first_tile, self.steps = nc, n, first_tile, tiles // n
        assert tiles % (2 * n) == 0
        self.keys, self.r_row, self.weight, self.place, self.out = edges
        self.record = sb("record2" + name, [P, 2, n, R2], F32, memory)
        self.row = sb("row2" + name, [P, 2, n], I32, memory)
        self.s_packed = sem("s_packed2" + name)
        self.s_put = [sem(f"s_put2{name}{b}") for b in range(2)]

    def pack(self, act, i, s, b, first):
        nc = self.nc
        if not first:
            act.wait_ge(self.s_put[b], 16 * self.n * i)
        cols = bass.ds(self.first_tile + s * self.n, self.n)
        for f, of in enumerate((self.r_row[:, cols], self.weight[:, cols], self.keys[:, 1, cols])):
            nc.scalar.activation(self.record[:, b, :, f:f + 1].rearrange("p t o -> p (t o)"), of, ACT.Copy)
        nc.scalar.activation(self.row[:, b, :], self.place[:, cols], ACT.Copy).then_inc(self.s_packed, 1)

    def pack_all(self, act):
        for b in range(2):
            self.pack(act, 0, b, b, True)
        with act.Fori(1, self.steps // 2) as i:
            for b in range(2):
                self.pack(act, i, i * 2 + b, b, False)

    def put(self, pool, s, b, passed_pool):
        wait_alone(pool, self.s_packed, s + 1, passed_pool)
        for t in range(self.n):
            pool.indirect_dma_start(
                out=self.out, out_offset=bass.IndirectOffsetOnAxis(ap=self.row[:, b, t:t + 1].bitcast(U32), axis=0),
                in_=self.record[:, b, t, :], in_offset=None).then_inc(self.s_put[b], 16)

    def put_all(self, pool, passed_pool):
        with pool.Fori(0, self.steps // 2) as i:
            for b in range(2):
                self.put(pool, i * 2 + b, b, passed_pool)

    def finish(self, pool):
        for b in range(2):
            pool.wait_ge(self.s_put[b], 16 * self.n * (self.steps // 2))


def kernel(**inputs):
    import numpy as np
    import concourse.bacc as bacc
    from concourse.bass_utils import run_bass_kernel_spmd

    a = {k: np.asarray(v) for k, v in inputs.items()}

    def pad(v, rows, fill=0):
        w = np.full((rows,) + v.shape[1:], fill, v.dtype)
        w[:len(v)] = v
        return w

    def by_node(v, w):
        return pad(v.reshape(N, w), NP).reshape(NB, P, w).transpose(1, 0, 2)

    def by_edge(v, fill=0):
        return pad(v.reshape(E), P * T, fill).reshape(P, T)

    def every(v):
        return np.broadcast_to(v.reshape(1, -1), (P, v.size))

    def two2(m, o):
        w = np.zeros((2, m.shape[0], 2, m.shape[1]), m.dtype)
        w[0, :, 0], w[1, :, 1] = m, o
        return w.reshape(2 * m.shape[0], 2 * m.shape[1])

    def two(m):
        return two2(m, m)

    i, w = np.arange(P * T - E, dtype=np.int32), NP - N
    src = np.concatenate([a["src"], N + i % w]).reshape(P, T)
    dst = np.concatenate([a["dst"], N + i // w % w]).reshape(P, T)
    keys = np.stack([src, dst], 1)
    arrays = {
        "x": by_node(a["x"], D),
        "key_cols": keys,
        "key_rows": keys.reshape(P, 2, NC, GC).transpose(2, 1, 3, 0).reshape(NC, 2 * GC * P),
        "w0": a["L0_gnn_weights"].reshape(K // 2, 2 * D, D).transpose(1, 0, 2),
        "b0": every(a["L0_gnn_bias"]),
        "emb": a["L1_gnn_emb"],
        "embT": a["L1_gnn_emb"].T,
        "adaptT": a["L1_gnn_adaptW"].T,
        "kind": by_node(a["node_type_119"], 1)[:, :, 0],
        "mult": by_node(a["node_vec"], 1)[:, :, 0],
        "distance": by_edge(a["edge_weight"]),
        "weight": by_edge(a["edge_weight1"]),
        "relation": by_edge(a["edge_type_8"]),
        "attr": pad(a["edge_attr_40"], P * T).reshape(P, T, R),
        "l1_w1": two(pad(a["L1_gnn_W1"].T, R1))[:TWO],
        "l1_b1": np.tile(a["L1_gnn_b1"], 2).reshape(-1, 1),
        "l1_w2": np.concatenate([two(a["L1_gnn_W2"].T), np.tile(a["L1_gnn_b2"], 2).reshape(1, -1)]),
        "gamma": every(a["L1_gnn_gamma"]),
        "beta": every(a["L1_gnn_beta"]),
        "l2_w1": a["L2_gnn_weight1"].reshape(NR // 2, 2, D, D).transpose(2, 0, 1, 3).reshape(D, NR // 2, 2 * D),
        "l2_b1": np.tile(a["L2_gnn_bias1"], 2).reshape(-1, 1),
        "l2_w2": np.stack([two2(a["L2_gnn_weight2"][2 * q], a["L2_gnn_weight2"][2 * q + 1]) for q in range(NR // 2)], 1),
        "l2_b2": every(a["L2_gnn_bias2"]),
        "l3_w": a["L3_gnn_W"].T,
        "l3_b": every(a["L3_gnn_b"]),
    }
    nc = bacc.Bacc("TRN2", target_bir_lowering=False, num_devices=1)
    arrays = {f"in_{k}": np.ascontiguousarray(v) for k, v in arrays.items()}
    h = {k[3:]: nc.dram_tensor(k, v.shape, mybir.dt.from_np(v.dtype), kind="ExternalInput").ap()
         for k, v in arrays.items()}
    out = nc.dram_tensor("out", (P, NB, D), F32, kind="ExternalOutput").ap()
    gnn_kernel(nc, h, out)
    r = run_bass_kernel_spmd(nc, [arrays], core_ids=[0])
    return r.results[0]["out"].transpose(1, 0, 2).reshape(NP, D)[:N]
```
